# Optimizing a Trainium2 kernel written in Bass

```python
import numpy as np
import jax
import jax.numpy as jnp

def _softmax(x, axis=-1):
    return jax.nn.softmax(x, axis=axis)

def _gelu(x):
    return jax.nn.gelu(x, approximate=True)

def _silu(x):
    return jax.nn.silu(x)

def _sigmoid(x):
    return jax.nn.sigmoid(x)

def _layernorm(x, axis=-1, eps=1e-05):
    m = jnp.mean(x, axis=axis, keepdims=True)
    v = jnp.var(x, axis=axis, keepdims=True)
    return (x - m) / jnp.sqrt(v + eps)

def _scatter_add(tgt, idx, src, axis=0):
    return tgt.at[idx].add(src)

def _segment_sum(src, seg, n):
    return jax.ops.segment_sum(src, seg, n)
kernel_name = 'mk_perceiver_d2_seqx_r4_303165'

def setup_inputs(seed: int=0):
    np.random.seed(seed)
    _w = jnp.asarray

    def _rec_inputs():
        import jax
        import jax.numpy as jnp
        _rk = jax.random.key(seed)
        x = 7.22e-05 + 1 * jax.random.normal(jax.random.fold_in(_rk, 1), (32, 32, 256), jnp.float32)
        _lenS = 32 - jax.random.randint(jax.random.fold_in(_rk, 7), (32,), 0, max(1, 32 // 4) + 1, jnp.int32)
        _lenS2 = 257 - jax.random.randint(jax.random.fold_in(_rk, 8), (32,), 0, max(1, 257 // 4) + 1, jnp.int32)
        _ctx_1024P = jax.random.normal(jax.random.fold_in(_rk, 11), (32, 16, 256), jnp.float32)
        _ctx_1024c = jax.random.dirichlet(jax.random.fold_in(_rk, 511), 0.3 * jnp.ones((16,), jnp.float32), (32, 257))
        _ctx_1024t = jnp.einsum('bsk,bkd->bsd', _ctx_1024c, _ctx_1024P)
        _ctx_1024t = _ctx_1024t * jax.lax.rsqrt(jnp.mean(jnp.square(_ctx_1024t)) + 1e-12) * 0.953939
        ctx_1024 = 4.13588e-05 + 0.999923 * (_ctx_1024t + 0.3 * jax.random.normal(jax.random.fold_in(_rk, 611), (32, 257, 256), jnp.float32))
        _validS = jnp.arange(32)[None, :] < _lenS[:, None]
        _validS2 = jnp.arange(257)[None, :] < _lenS2[:, None]
        _causal = jnp.tril(jnp.ones((32, 32), dtype=bool))
        mask_1x1xSxS2_fk1 = jnp.where(jnp.broadcast_to(_validS2[0:1, None, None, :], (1, 1, 32, 257)), 1.0, 0.0).astype(jnp.float32)
        return (x, ctx_1024, mask_1x1xSxS2_fk1)
    x, ctx_1024, mask_1x1xSxS2_fk1 = _rec_inputs()

    def _L0_xattn_setup():
        import jax, jax.numpy as jnp
        import numpy as np
        B, T, C = (4, 512, 256)
        NH = 16
        HS = C // NH

        def _split_heads(x):
            Bq, Tq, Cq = x.shape
            return x.reshape(Bq, Tq, NH, Cq // NH).transpose(0, 2, 1, 3)
        key = jax.random.key(seed)
        ks = jax.random.split(key, 11)
        s = 1.0 / np.sqrt(C)
        inp = {'query': jax.random.normal(ks[0], (B, T, C), jnp.float32), 'key': jax.random.normal(ks[1], (B, T, C), jnp.float32), 'value': jax.random.normal(ks[2], (B, T, C), jnp.float32), 'mask': jnp.triu(jnp.ones((T, T), jnp.float32), k=1)[None, None, :, :], 'Wq': jax.random.normal(ks[3], (C, C), jnp.float32) * s, 'bq': jnp.zeros((C,), jnp.float32), 'Wk': jax.random.normal(ks[4], (C, C), jnp.float32) * s, 'bk': jnp.zeros((C,), jnp.float32), 'Wv': jax.random.normal(ks[5], (C, C), jnp.float32) * s, 'bv': jnp.zeros((C,), jnp.float32), 'Wo': jax.random.normal(ks[6], (C, C), jnp.float32) * s, 'bo': jnp.zeros((C,), jnp.float32)}
        return inp
    _L0_xattn_all = _L0_xattn_setup()
    _L0_xattn_in = {k: v for k, v in _L0_xattn_all.items() if k in ('Wq', 'bq', 'Wk', 'bk', 'Wv', 'bv', 'Wo', 'bo')}
    del _L0_xattn_all

    def _L0_attn_setup():
        import jax, jax.numpy as jnp
        import numpy as np
        B, T, DIM, HEADS, CF = (2, 1024, 256, 16, 4)

        def _compress(z, w, bias):
            y = jax.lax.conv_general_dilated(z.transpose(0, 2, 1), w, window_strides=(CF,), padding='VALID', dimension_numbers=('NCH', 'OIH', 'NCH'), feature_group_count=HEADS)
            return (y + bias[None, :, None]).transpose(0, 2, 1)
        key = jax.random.key(seed)
        ks = jax.random.split(key, 8)
        s = 0.02
        return {'x': jax.random.normal(ks[0], (B, T, DIM), jnp.float32), 'Wqkv': jax.random.normal(ks[1], (DIM, 3 * DIM), jnp.float32) * s, 'conv_w': jax.random.normal(ks[2], (DIM, DIM // HEADS, CF), jnp.float32) * s, 'conv_b': jax.random.normal(ks[3], (DIM,), jnp.float32) * s, 'null_k': jax.random.normal(ks[4], (1, 1, DIM), jnp.float32) * s, 'null_v': jax.random.normal(ks[5], (1, 1, DIM), jnp.float32) * s, 'W_out': jax.random.normal(ks[6], (DIM, DIM), jnp.float32) * s, 'b_out': jax.random.normal(ks[7], (DIM,), jnp.float32) * s}
    _L0_attn_all = _L0_attn_setup()
    _L0_attn_in = {k: v for k, v in _L0_attn_all.items() if k in ('Wqkv', 'conv_w', 'conv_b', 'null_k', 'null_v', 'W_out', 'b_out')}
    del _L0_attn_all

    def _L0_ffn_setup():
        import jax, jax.numpy as jnp
        import numpy as np
        N_EMBD = 256
        NUM_EXPERTS = 8
        TOP_K = 2

        def new_gelu(x):
            c = jnp.sqrt(2.0 / jnp.pi).astype(x.dtype)
            return 0.5 * x * (1.0 + jnp.tanh(c * (x + 0.044715 * x ** 3)))
        key = jax.random.key(seed)
        ks = jax.random.split(key, 6)
        C, E, H = (N_EMBD, NUM_EXPERTS, 4 * N_EMBD)
        x = jax.random.normal(ks[0], (4, 512, C), dtype=jnp.float32)
        router_w = 0.02 * jax.random.normal(ks[1], (E, C), dtype=jnp.float32)
        w1 = 0.02 * jax.random.normal(ks[2], (E, H, C), dtype=jnp.float32)
        b1 = jnp.zeros((E, H), dtype=jnp.float32)
        w2 = 0.02 * jax.random.normal(ks[3], (E, C, H), dtype=jnp.float32)
        b2 = jnp.zeros((E, C), dtype=jnp.float32)
        return {'x': x, 'router_w': router_w, 'w1': w1, 'b1': b1, 'w2': w2, 'b2': b2}
    _L0_ffn_all = _L0_ffn_setup()
    _L0_ffn_in = {k: v for k, v in _L0_ffn_all.items() if k in ('router_w', 'w1', 'b1', 'w2', 'b2')}
    del _L0_ffn_all

    def _L1_xattn_setup():
        import jax, jax.numpy as jnp
        import numpy as np
        DIM = 256
        N_HEADS = 16
        HEAD_DIM = DIM // N_HEADS
        EPS = 1e-06
        Q_THETA = 32.0
        K_THETA = 1000.0

        def precompute_freqs_1d(dim, seq_len, theta):
            freqs = theta ** (-jnp.arange(0, dim, 2, dtype=jnp.float32) / dim)
            t = jnp.arange(seq_len, dtype=jnp.float32)
            ang = t[:, None] * freqs[None, :]
            return (jnp.cos(ang), jnp.sin(ang))

        def rms_norm(x, w):
            var = jnp.mean(x * x, axis=-1, keepdims=True)
            return x * jax.lax.rsqrt(var + EPS) * w

        def apply_rope(t, cos, sin):
            cos = cos[None, None, :, :]
            sin = sin[None, None, :, :]
            t1, t2 = jnp.split(t, 2, axis=-1)
            return jnp.concatenate([t1 * cos - t2 * sin, t2 * cos + t1 * sin], axis=-1)
        key = jax.random.key(seed)
        ks = jax.random.split(key, 8)
        B, T, S = (128, 64, 96)
        s = 1.0 / np.sqrt(DIM)
        return {'x': jax.random.normal(ks[0], (B, T, DIM), jnp.float32), 'context': jax.random.normal(ks[1], (B, S, DIM), jnp.float32), 'Wq': jax.random.normal(ks[2], (DIM, DIM), jnp.float32) * s, 'Wk': jax.random.normal(ks[3], (DIM, DIM), jnp.float32) * s, 'Wv': jax.random.normal(ks[4], (DIM, DIM), jnp.float32) * s, 'Wo': jax.random.normal(ks[5], (DIM, DIM), jnp.float32) * s, 'q_norm_w': jnp.ones((HEAD_DIM,), jnp.float32), 'k_norm_w': jnp.ones((HEAD_DIM,), jnp.float32)}
    _L1_xattn_all = _L1_xattn_setup()
    _L1_xattn_in = {k: v for k, v in _L1_xattn_all.items() if k in ('Wq', 'Wk', 'Wv', 'Wo', 'q_norm_w', 'k_norm_w')}
    del _L1_xattn_all

    def _L1_attn_setup():
        import jax, jax.numpy as jnp
        import numpy as np
        D_MODEL = 256
        N_HEAD = 16
        SEQ = 512
        BATCH = 2
        key = jax.random.key(seed)
        x = jax.random.normal(key, (BATCH, SEQ, D_MODEL), dtype=jnp.float32)
        return {'x': x}
    _L1_attn_all = _L1_attn_setup()
    _L1_attn_in = {k: v for k, v in _L1_attn_all.items() if k in ()}
    del _L1_attn_all

    def _L1_ffn_setup():
        import jax, jax.numpy as jnp
        import numpy as np
        B, S, D = (4, 512, 256)
        E, H, TOP_K = (8, 512, 2)
        key = jax.random.key(seed)
        k_x, k_g, k_w1, k_w2, k_w3 = jax.random.split(key, 5)
        s_d = 1.0 / np.sqrt(D)
        s_h = 1.0 / np.sqrt(H)
        return {'x': jax.random.normal(k_x, (B, S, D), dtype=jnp.float32), 'w_gate': jax.random.normal(k_g, (D, E), dtype=jnp.float32) * s_d, 'w1': jax.random.normal(k_w1, (E, D, H), dtype=jnp.float32) * s_d, 'w3': jax.random.normal(k_w3, (E, D, H), dtype=jnp.float32) * s_d, 'w2': jax.random.normal(k_w2, (E, H, D), dtype=jnp.float32) * s_h}
    _L1_ffn_all = _L1_ffn_setup()
    _L1_ffn_in = {k: v for k, v in _L1_ffn_all.items() if k in ('w_gate', 'w1', 'w3', 'w2')}
    del _L1_ffn_all
    return {'x': x, 'ctx_1024': ctx_1024, 'mask_1x1xSxS2_fk1': mask_1x1xSxS2_fk1, 'L0_xattn_Wq': _L0_xattn_in['Wq'], 'L0_xattn_bq': _L0_xattn_in['bq'], 'L0_xattn_Wk': _L0_xattn_in['Wk'], 'L0_xattn_bk': _L0_xattn_in['bk'], 'L0_xattn_Wv': _L0_xattn_in['Wv'], 'L0_xattn_bv': _L0_xattn_in['bv'], 'L0_xattn_Wo': _L0_xattn_in['Wo'], 'L0_xattn_bo': _L0_xattn_in['bo'], 'L0_attn_Wqkv': _L0_attn_in['Wqkv'], 'L0_attn_conv_w': _L0_attn_in['conv_w'], 'L0_attn_conv_b': _L0_attn_in['conv_b'], 'L0_attn_null_k': _L0_attn_in['null_k'], 'L0_attn_null_v': _L0_attn_in['null_v'], 'L0_attn_W_out': _L0_attn_in['W_out'], 'L0_attn_b_out': _L0_attn_in['b_out'], 'L0_ffn_router_w': _L0_ffn_in['router_w'], 'L0_ffn_w1': _L0_ffn_in['w1'], 'L0_ffn_b1': _L0_ffn_in['b1'], 'L0_ffn_w2': _L0_ffn_in['w2'], 'L0_ffn_b2': _L0_ffn_in['b2'], 'L1_xattn_Wq': _L1_xattn_in['Wq'], 'L1_xattn_Wk': _L1_xattn_in['Wk'], 'L1_xattn_Wv': _L1_xattn_in['Wv'], 'L1_xattn_Wo': _L1_xattn_in['Wo'], 'L1_xattn_q_norm_w': _L1_xattn_in['q_norm_w'], 'L1_xattn_k_norm_w': _L1_xattn_in['k_norm_w'], 'L1_ffn_w_gate': _L1_ffn_in['w_gate'], 'L1_ffn_w1': _L1_ffn_in['w1'], 'L1_ffn_w3': _L1_ffn_in['w3'], 'L1_ffn_w2': _L1_ffn_in['w2']}

def reference(x, ctx_1024, mask_1x1xSxS2_fk1, L0_xattn_Wq, L0_xattn_bq, L0_xattn_Wk, L0_xattn_bk, L0_xattn_Wv, L0_xattn_bv, L0_xattn_Wo, L0_xattn_bo, L0_attn_Wqkv, L0_attn_conv_w, L0_attn_conv_b, L0_attn_null_k, L0_attn_null_v, L0_attn_W_out, L0_attn_b_out, L0_ffn_router_w, L0_ffn_w1, L0_ffn_b1, L0_ffn_w2, L0_ffn_b2, L1_xattn_Wq, L1_xattn_Wk, L1_xattn_Wv, L1_xattn_Wo, L1_xattn_q_norm_w, L1_xattn_k_norm_w, L1_ffn_w_gate, L1_ffn_w1, L1_ffn_w3, L1_ffn_w2):
    import jax
    import jax.numpy as jnp

    def _L0_xattn_ref(query, key, value, mask, Wq, bq, Wk, bk, Wv, bv, Wo, bo):
        import jax, jax.numpy as jnp
        import numpy as np
        B, T, C = (4, 512, 256)
        NH = 16
        HS = C // NH

        def _split_heads(x):
            Bq, Tq, Cq = x.shape
            return x.reshape(Bq, Tq, NH, Cq // NH).transpose(0, 2, 1, 3)
        q = _split_heads(query @ Wq + bq)
        k = _split_heads(key @ Wk + bk)
        v = _split_heads(value @ Wv + bv)
        scores = jnp.einsum('bhqd,bhkd->bhqk', q, k) / jnp.sqrt(jnp.asarray(HS, q.dtype))
        scores = scores + mask * -1000000000.0
        attn = jax.nn.softmax(scores, axis=-1)
        out = jnp.einsum('bhqk,bhkd->bhqd', attn, v)
        out = out.transpose(0, 2, 1, 3).reshape(query.shape[0], query.shape[1], -1)
        return out @ Wo + bo

    def _L0_attn_ref(x, Wqkv, conv_w, conv_b, null_k, null_v, W_out, b_out):
        import jax, jax.numpy as jnp
        import numpy as np
        B, T, DIM, HEADS, CF = (2, 1024, 256, 16, 4)

        def _compress(z, w, bias):
            y = jax.lax.conv_general_dilated(z.transpose(0, 2, 1), w, window_strides=(CF,), padding='VALID', dimension_numbers=('NCH', 'OIH', 'NCH'), feature_group_count=HEADS)
            return (y + bias[None, :, None]).transpose(0, 2, 1)
        b, t, d = x.shape
        h, cf = (HEADS, CF)
        dh = d // h
        qkv = x @ Wqkv
        q, k, v = jnp.split(qkv, 3, axis=-1)
        k = _compress(k, conv_w, conv_b)
        v = _compress(v, conv_w, conv_b)
        k = jnp.concatenate([jnp.broadcast_to(null_k, (b, 1, d)), k], axis=1)
        v = jnp.concatenate([jnp.broadcast_to(null_v, (b, 1, d)), v], axis=1)
        to_heads = lambda z: z.reshape(b, z.shape[1], h, dh).transpose(0, 2, 1, 3)
        q, k, v = (to_heads(q), to_heads(k), to_heads(v))
        dots = jnp.einsum('bhid,bhjd->bhij', q, k) * d ** (-0.5)
        mask_value = -jnp.finfo(dots.dtype).max
        q_idx = jnp.arange(t)
        k_idx = jnp.arange(t).reshape(-1, cf).max(axis=-1)
        mask = q_idx[:, None] < k_idx[None, :]
        mask = jnp.pad(mask, ((0, 0), (1, 0)), constant_values=False)
        dots = jnp.where(mask[None, None], mask_value, dots)
        attn = jax.nn.softmax(dots, axis=-1)
        out = jnp.einsum('bhij,bhjd->bhid', attn, v)
        out = out.transpose(0, 2, 1, 3).reshape(b, t, d)
        out = out @ W_out + b_out
        out = jnp.fft.fft(jnp.fft.fft(out.astype(jnp.float32), axis=-1), axis=-2).real
        return out

    def _L0_ffn_ref(x, router_w, w1, b1, w2, b2):
        import jax, jax.numpy as jnp
        import numpy as np
        N_EMBD = 256
        NUM_EXPERTS = 8
        TOP_K = 2

        def new_gelu(x):
            c = jnp.sqrt(2.0 / jnp.pi).astype(x.dtype)
            return 0.5 * x * (1.0 + jnp.tanh(c * (x + 0.044715 * x ** 3)))
        B, T, C = x.shape
        E = router_w.shape[0]
        x_flat = x.reshape(B * T, C)
        router_logits = x_flat @ router_w.T
        router_probs = jax.nn.softmax(router_logits, axis=-1)
        top_k_probs, top_k_idx = jax.lax.top_k(router_probs, TOP_K)
        top_k_probs = top_k_probs / (top_k_probs.sum(axis=-1, keepdims=True) + 1e-08)
        cw = (jax.nn.one_hot(top_k_idx, E, dtype=x.dtype) * top_k_probs[..., None]).sum(axis=1)
        output = jnp.zeros_like(x_flat)
        for e in range(E):
            h = new_gelu(x_flat @ w1[e].T + b1[e])
            out_e = h @ w2[e].T + b2[e]
            output = output + cw[:, e:e + 1] * out_e
        return output.reshape(B, T, C)

    def _L1_xattn_ref(x, context, Wq, Wk, Wv, Wo, q_norm_w, k_norm_w):
        import jax, jax.numpy as jnp
        import numpy as np
        DIM = 256
        N_HEADS = 16
        HEAD_DIM = DIM // N_HEADS
        EPS = 1e-06
        Q_THETA = 32.0
        K_THETA = 1000.0

        def precompute_freqs_1d(dim, seq_len, theta):
            freqs = theta ** (-jnp.arange(0, dim, 2, dtype=jnp.float32) / dim)
            t = jnp.arange(seq_len, dtype=jnp.float32)
            ang = t[:, None] * freqs[None, :]
            return (jnp.cos(ang), jnp.sin(ang))

        def rms_norm(x, w):
            var = jnp.mean(x * x, axis=-1, keepdims=True)
            return x * jax.lax.rsqrt(var + EPS) * w

        def apply_rope(t, cos, sin):
            cos = cos[None, None, :, :]
            sin = sin[None, None, :, :]
            t1, t2 = jnp.split(t, 2, axis=-1)
            return jnp.concatenate([t1 * cos - t2 * sin, t2 * cos + t1 * sin], axis=-1)
        B, T, C = x.shape
        S = context.shape[1]
        H, D = (N_HEADS, HEAD_DIM)
        q = (x @ Wq.T).reshape(B, T, H, D).transpose(0, 2, 1, 3)
        k = (context @ Wk.T).reshape(B, S, H, D).transpose(0, 2, 1, 3)
        v = (context @ Wv.T).reshape(B, S, H, D).transpose(0, 2, 1, 3)
        q = rms_norm(q, q_norm_w)
        k = rms_norm(k, k_norm_w)
        q_cos, q_sin = precompute_freqs_1d(D, T, Q_THETA)
        k_cos, k_sin = precompute_freqs_1d(D, S, K_THETA)
        q = apply_rope(q, q_cos, q_sin)
        k = apply_rope(k, k_cos, k_sin)
        scale = D ** (-0.5)
        attn = jnp.einsum('bhtd,bhsd->bhts', q, k) * scale
        attn = jax.nn.softmax(attn, axis=-1)
        out = jnp.einsum('bhts,bhsd->bhtd', attn, v)
        out = out.transpose(0, 2, 1, 3).reshape(B, T, C)
        return out @ Wo.T

    def _L1_attn_ref(x):
        import jax, jax.numpy as jnp
        import numpy as np
        D_MODEL = 256
        N_HEAD = 16
        SEQ = 512
        BATCH = 2
        B, S, D = x.shape
        H = N_HEAD
        hd = D // H
        qkv = x.reshape(B, S, H, hd).transpose(0, 2, 1, 3)
        q = k = v = qkv
        w = jnp.einsum('bhqd,bhkd->bhqk', q, k) / jnp.sqrt(jnp.asarray(hd, x.dtype))
        causal = jnp.tril(jnp.ones((S, S), dtype=bool))
        mask_value = jnp.finfo(w.dtype).min
        w = jnp.where(causal[None, None, :, :], w, mask_value)
        w = jax.nn.softmax(w, axis=-1)
        out = jnp.einsum('bhqk,bhkd->bhqd', w, v)
        return out.transpose(0, 2, 1, 3).reshape(B, S, D)

    def _L1_ffn_ref(x, w_gate, w1, w3, w2):
        import jax, jax.numpy as jnp
        import numpy as np
        B, S, D = (4, 512, 256)
        E, H, TOP_K = (8, 512, 2)
        bsz, seq_len, embed_dim = x.shape
        xt = x.reshape(-1, embed_dim)
        T = xt.shape[0]
        logits = xt @ w_gate
        top_logits, sel = jax.lax.top_k(logits, TOP_K)
        probs = jax.nn.softmax(top_logits, axis=-1).astype(x.dtype)
        h = jax.nn.silu(jnp.einsum('td,edh->eth', xt, w1)) * jnp.einsum('td,edh->eth', xt, w3)
        y = jnp.einsum('eth,ehd->etd', h, w2)
        t_idx = jnp.arange(T)
        yk = y[sel.T, t_idx[None, :], :]
        out = jnp.einsum('ktd,tk->td', yk, probs)
        return out.reshape(bsz, seq_len, embed_dim)
    x = x + _L0_xattn_ref(_layernorm(x, axis=-1), ctx_1024, ctx_1024, mask_1x1xSxS2_fk1, L0_xattn_Wq, L0_xattn_bq, L0_xattn_Wk, L0_xattn_bk, L0_xattn_Wv, L0_xattn_bv, L0_xattn_Wo, L0_xattn_bo)
    x = x + _L0_attn_ref(_layernorm(x, axis=-1), L0_attn_Wqkv, L0_attn_conv_w, L0_attn_conv_b, L0_attn_null_k, L0_attn_null_v, L0_attn_W_out, L0_attn_b_out)
    x = x + _L0_ffn_ref(_layernorm(x, axis=-1), L0_ffn_router_w, L0_ffn_w1, L0_ffn_b1, L0_ffn_w2, L0_ffn_b2)
    x = x + _L1_xattn_ref(_layernorm(x, axis=-1), ctx_1024, L1_xattn_Wq, L1_xattn_Wk, L1_xattn_Wv, L1_xattn_Wo, L1_xattn_q_norm_w, L1_xattn_k_norm_w)
    x = x + _L1_attn_ref(_layernorm(x, axis=-1))
    x = x + _L1_ffn_ref(_layernorm(x, axis=-1), L1_ffn_w_gate, L1_ffn_w1, L1_ffn_w3, L1_ffn_w2)
    return x

_drawn_inputs = setup_inputs


def setup_inputs(seed=0):
    import zlib

    import numpy as np

    out = dict(_drawn_inputs(seed))
    spreads = {'L0_xattn_bq': (0.0, 0.1),
     'L0_xattn_bk': (0.0, 2.0),
     'L0_xattn_bv': (0.0, 0.1),
     'L0_xattn_bo': (0.0, 0.1),
     'L0_ffn_b1': (0.0, 0.357),
     'L0_ffn_b2': (0.0, 0.1),
     'L1_xattn_q_norm_w': (1.0, 0.6),
     'L1_xattn_k_norm_w': (1.0, 0.561)}
    factors = {'L0_attn_null_k': 199.548}
    for name, (base, spread) in spreads.items():
        noise = np.random.default_rng([zlib.crc32(name.encode()), seed]).standard_normal(out[name].shape)
        drawn = base * np.exp(spread * noise) if base else spread * noise
        out[name] = jnp.asarray(drawn.astype(out[name].dtype))
    for name, factor in factors.items():
        out[name] = (out[name] * factor).astype(out[name].dtype)
    return out
```

```python
from contextlib import ExitStack

import concourse.bass as bass
import numpy as np
from concourse import mybir

F32 = mybir.dt.float32
U32 = mybir.dt.uint32
ALU = mybir.AluOpType
ACT = mybir.ActivationFunctionType
AX_X = mybir.AxisListType.X

P = 128
B, T, D = 32, 32, 256
S = 257
NH, HD = 16, 16
STAGES = 6
KC = D // P
NT = B * T // P
QB = P // T
QS = QB * S
VT = -(-QS // P)
WIN = 3 * P
TOK = B * T
E_ = 8
H0, H1 = 1024, 512
CF = 4
NKEY = T // CF + 1
KW = 32
MASK_VALUE = -3.0e38
GH = NH // 4

C_IDENT, C_STACK, C_BLK, C_HM1, C_HM4, C_HM16 = 0, 128, 160, 224, 232, 240
C_CS, C_BD, C_M0, C_M1, C_RQ, C_RK = 248, 1272, 1528, 1560, 1592, 1624
C_IOTA = C_RK + 32 * VT
NCONST = C_IOTA + E_
V_BQ, V_BK, V_BV, V_CB, V_BO, V_NK, V_NV = 0, 2, 4, 6, 8, 10, 12
NVEC = 14


def shape_constants():
    c = np.zeros((P, NCONST), np.float32)
    p = np.arange(P)
    c[:, C_IDENT:C_IDENT + P] = np.eye(P)
    c[:, C_STACK:C_STACK + T] = (p[:, None] % T == np.arange(T)[None])
    c[:, C_BLK:C_BLK + 64] = (p[:, None] // T == np.arange(64)[None] // HD)
    same = (p[:, None] // HD == np.arange(8)[None])
    c[:, C_HM1:C_HM1 + 8] = same
    c[:, C_HM4:C_HM4 + 8] = same * HD ** -0.5
    c[:, C_HM16:C_HM16 + 8] = same * D ** -0.5
    d = np.arange(D)
    turn = (np.outer(d, d) % D) * (2 * np.pi / D)
    cs = np.concatenate([np.cos(turn), np.sin(turn)], 1).reshape(KC, P, 2 * D)
    c[:, C_CS:C_CS + KC * 2 * D] = cs.transpose(1, 0, 2).reshape(P, -1)
    turn = (np.outer(p % T, p % T) % T) * (2 * np.pi / T)
    mine = (p[:, None] // T == p[None] // T)
    c[:, C_BD:C_BD + P] = np.cos(turn) * mine
    c[:, C_BD + P:C_BD + 2 * P] = -np.sin(turn) * mine
    q = (p % T)[:, None]
    j = np.arange(KW)[None]
    c[:, C_M0:C_M0 + KW] = np.where((j >= 1) & (j < NKEY) & (q < CF * (j - 1) + CF - 1), MASK_VALUE, 0.0)
    c[:, C_M1:C_M1 + KW] = np.where(j > q, MASK_VALUE, 0.0)

    def rope(pos, theta):
        freqs = np.float32(theta) ** (-np.arange(0, HD, 2, dtype=np.float32) / np.float32(HD))
        ang = pos.astype(np.float32)[:, None] * freqs[None]
        return np.concatenate([np.cos(ang), np.cos(ang), -np.sin(ang), np.sin(ang)], 1) * HD ** 0.5

    c[:, C_RQ:C_RQ + 32] = rope(p % T, 32.0)
    for m in range(VT):
        c[:, C_RK + 32 * m:C_RK + 32 * m + 32] = rope((P * m + p) % S, 1000.0)
    c[:, C_IOTA:] = np.arange(E_)[None]
    return c


class Tally:

    def __init__(self, sem):
        self.sem, self.n = sem, 0

    def inc(self, ins):
        ins.then_inc(self.sem, 1)
        self.n += 1
        return self.n


def perceiver_block(nc, io, out, stages=6):
    ctx = ExitStack()
    with ctx:
        def sb(name, shape, dt=F32):
            return ctx.enter_context(nc.sbuf_tensor(name, shape, dt))

        def sem(name):
            return ctx.enter_context(nc.semaphore(name))

        bank = [ctx.enter_context(nc.psum_tensor(f"bank{i}", [P, 512], F32)) for i in range(8)]

        const = sb("const", [P, NCONST])
        vec = sb("vec", [P, NVEC])
        ident = const[:, C_IDENT:C_IDENT + P]
        stack = const[:, C_STACK:C_STACK + T]
        blk = const[:, C_BLK:C_BLK + 64]
        x = sb("x", [P, NT, D])
        xn = sb("xn", [P, NT, D])
        xnT = sb("xnT", [P, KC, TOK])
        qT = sb("qT", [P, KC, TOK])
        outT = sb("outT", [P, KC, TOK])
        ln_stats = sb("ln_stats", [P, NT, 6])
        ln_mv = sb("ln_mv", [P, NT, 2])
        ln_ve = sb("ln_ve", [P, NT])
        ln_sd = sb("ln_sd", [P, NT])
        ln_rs = sb("ln_rs", [P, NT])

        wq = [sb(f"wq{l}", [P, KC, D]) for l in range(2)]
        wkv = [sb(f"wkv{l}", [P, KC, 2 * D]) for l in range(2)]
        wo = [sb(f"wo{l}", [P, KC, D]) for l in range(2)]
        bo_bc = sb("bo_bc", [P, D])
        negmask = sb("negmask", [P, S])
        wqkv = sb("wqkv", [P, KC, 3 * D])
        wout = sb("wout", [P, KC, D])
        cw = sb("cw", [P, KC * CF, HD])
        normw = sb("normw", [P, 2, HD])
        ropew = sb("ropew", [P, 2 * HD * (1 + VT)])

        arena = sb("arena", [P, 26000])

        class Arena:
            def __init__(self):
                self.at = 0

            def take(self, *shape):
                n = int(np.prod(shape))
                v = arena[:, self.at:self.at + n]
                self.at += n
                assert self.at <= 26000, self.at
                if len(shape) == 1:
                    return v
                names = "abcd"[:len(shape)]
                return v.rearrange(f"p ({' '.join(names)}) -> p {' '.join(names)}",
                                   **{m: s for m, s in zip(names, shape)})

        const_loaded = sem("const_loaded")
        x_loaded = sem("x_loaded")
        wx_loaded = [sem(f"wx{l}_loaded") for l in range(2)]
        mask_loaded = sem("mask_loaded")
        wa_loaded = sem("wa_loaded")
        normw_loaded = sem("normw_loaded")
        x_ready = sem("x_ready")
        ln_own = sem("ln_own")
        ln_var = sem("ln_var")
        ln_std = sem("ln_std")
        ln_norm = sem("ln_norm")
        ln_turned = sem("ln_turned")
        ln_copied = sem("ln_copied")
        out_stored = sem("out_stored")

        XS = "xadd ctx0 ctx1 qw qc kvw kvc qbd scores masked negmax probs ptw pta ptd pvw recip normed colw colc postw own"
        xs = [{n: sem(f"x{l}_{n}") for n in (XS +(" sq ss r kn kab krope qsq qss qr qn qrope qtw qtc rw" if l else " nm bo")).split()}
              for l in range(2)]
        SS = "qbd vq sw sum own sub exp pn ptw ptc pvw om colw colc"
        ss_ = [{n: sem(f"s{l}_{n}") for n in (SS + (" prw prc bdw null z zeroed cvw cvc vtw vtc zw zc aw ac yw yc" if l == 0 else "")).split()}
               for l in range(2)]
        MS = "w0 w1 lgw gate0 gexp ge gate cwt cwtc cwb cwbc cwe upw upc mul dnw dnc rl b"
        ms = [{n: sem(f"m{l}_{n}") for n in MS.split()} for l in range(2)]

        ar = Arena()
        ctxb = [ar.take(KC, QS) for _ in range(2)]
        ktb = [ar.take(KC, QS) for _ in range(2)]
        vb = [ar.take(VT, D) for _ in range(2)]
        xqbd = [ar.take(KC, QB, 8, T) for _ in range(2)]
        smask = [ar.take(2, S) for _ in range(2)]
        pwin = [[ar.take(2, WIN) for _ in range(2)] for _ in range(QB)]
        pTb = [ar.take(2, WIN) for _ in range(2)]
        omb = [ar.take(P) for _ in range(2)]
        xsmall = ar.take(64)
        negmax = [xsmall[:, 2 * i:2 * i + 2] for i in range(2)]
        rowsum = [xsmall[:, 4 + 2 * i:6 + 2 * i] for i in range(2)]
        rcp = [xsmall[:, 8 + 2 * i:10 + 2 * i] for i in range(2)]
        xarena_end = ar.at
        kraw = sb("kraw", [P, 3, D])
        ksq = sb("ksq", [P, 3, D])
        kn = sb("kn", [P, D])
        ka = sb("ka", [P, D])
        kb_ = sb("kb", [P, D])
        krope = sb("krope", [P, 3, D])
        kss = sb("kss", [P, 3, NH])
        kvar = sb("kvar", [P, NH])
        kr = sb("kr", [P, NH])
        mhalf = sb("mhalf", [P, NH * NT])
        eps16 = sb("eps16", [P, NH * NT])
        qss = sb("qss", [P, NT * NH])
        qvar = sb("qvar", [P, NT * NH])
        qr = sb("qr", [P, NT * NH])

        rope_q = ropew[:, 0:32]

        def rope_k(m):
            return ropew[:, 32 + 32 * m:64 + 32 * m]

        def parts(l):
            if l == 0:
                order = [("K", i) for i in range(8)] + [("V", i) for i in range(VT)]
                cut = [2, 2, 2, 2, 2, 2, 2, 3]
            else:
                order = [("A", 0), ("A", 1), ("A", 2), ("T", 0), ("A", 3), ("A", 4), ("T", 1), ("A", 5), ("T", 2),
                         ("A", 6), ("T", 3), ("A", 7), ("T", 4), ("A", 8), ("T", 5), ("T", 6), ("T", 7), ("T", 8)]
                cut = [2, 3, 4, 3, 3, 2, 1, 0]
            steps, at = [], 0
            for n in cut:
                steps.append([(at + i, *order[at + i]) for i in range(n)])
                at += n
            assert at == len(order)
            return steps, len(order), {o: i for i, o in enumerate(order)}

        ar = Arena()
        kT = ar.take(KC, TOK)
        vT = ar.take(KC, TOK)
        kcT = ar.take(KC, B, KW)
        vcT = ar.take(KC, B, KW)
        bdw = ar.take(KC * CF, P)
        vall = ar.take(NT, D)
        sqbd = [ar.take(KC, QB, 8, T) for _ in range(2)]
        vq = [ar.take(D) for _ in range(2)]
        sprob = [ar.take(NH, KW) for _ in range(2)]
        pn = [ar.take(GH, QB, KW) for _ in range(2)]
        spT = [ar.take(GH, P) for _ in range(2)]
        som = ar.take(QB, D)
        zT = kT
        af = [vT[:, i, 0:2 * D] for i in range(2)]
        rowmax = sb("rowmax", [P, 2])
        spare = sb("spare", [1, 1])
        mark = sb("mark", [1, 1])
        smx = sb("smx", [P, NH])
        ssum = sb("ssum", [P, NH])
        srcp = sb("srcp", [P, NH])

        ar = Arena()
        m0_up = [[ar.take(KC, H0)] for _ in range(2)]
        m0_down = [ar.take(H0 // P, D) for _ in range(2)]
        m0_h = [ar.take(H0 // P, 512) for _ in range(2)]
        ar = Arena()
        m1_up = [[ar.take(KC, H1), ar.take(KC, H1)] for _ in range(2)]
        m1_down = [ar.take(H1 // P, D) for _ in range(2)]
        m1_h = [ar.take(H1 // P, 512) for _ in range(2)]
        m1_silu = [ar.take(512) for _ in range(2)]
        rw0 = sb("rw0", [P, KC, E_])
        rw1 = sb("rw1", [P, KC, E_])
        b1sb = sb("b1sb", [P, E_, H0 // P])
        b2sb = sb("b2sb", [E_, D])
        lg = sb("lg", [P, NT, E_])
        pr = sb("pr", [P, NT, E_])
        top = sb("top", [P, NT, 8])
        topi = sb("topi", [P, NT, 8], U32)
        topf = sb("topf", [P, NT, 8])
        gsm = sb("gsm", [P, 4, NT])
        gate1 = sb("gate1", [P, NT, E_])
        gate = sb("gate", [P, NT, E_])
        gate_e = [sb(f"gate_e{i}", [P, NT]) for i in range(2)]
        b1_e = [sb(f"b1_e{i}", [P, H0 // P]) for i in range(2)]
        gateT = sb("gateT", [E_, TOK])

        block = ctx.enter_context(nc.Block())

        def slot_plan(items):
            return items[0:1], items[1:2], items[2:]

        @block.sync
        def _(sp):
            sp.dma_start(x[:, :, :], io["x"].rearrange("(t p) d -> p t d", p=P)).then_inc(x_loaded, 16)
            sp.dma_start(const[:, :], io["const"]).then_inc(const_loaded, 16)
            sp.dma_start(vec[:, :], io["vec"]).then_inc(const_loaded, 16)

            def cross_weights(l):
                for dst, src in ((wq[l], "q"), (wkv[l], "kv"), (wo[l], "o")):
                    sp.dma_start(dst[:, :, :], io[f"w{l}{src}"].rearrange("(c p) n -> p c n", p=P)).then_inc(wx_loaded[l], 16)

            cross_weights(0)

            def load_ctx(l, k, n):
                sp.dma_start(ctxb[k], io["ctxT"].rearrange("(c p) n -> p c n", p=P)[:, :, bass.ds(n * QS, QS)])\
                  .then_inc(xs[l][f"ctx{k}"], 16)

            def cross_loads(l):
                load_ctx(l, 0, 0)
                load_ctx(l, 1, 1)
                if l == 0:
                    for h in range(QB):
                        sp.dma_start(negmask[T * h:T * h + T, :], io["mask"]).then_inc(mask_loaded, 16)
                    sp.dma_start(bo_bc[:, :], io["bo"]).then_inc(mask_loaded, 16)
                    sp.dma_start(wqkv[:, :, :], io["wqkv"].rearrange("(c p) n -> p c n", p=P)).then_inc(wa_loaded, 16)
                    sp.dma_start(wout[:, :, :], io["wout"].rearrange("(c p) n -> p c n", p=P)).then_inc(wa_loaded, 16)
                    sp.dma_start(cw[:, :, :], io["conv"]).then_inc(wa_loaded, 16)
                    cross_weights(1)
                    sp.dma_start(normw[:, :, :], io["normw"]).then_inc(normw_loaded, 16)
                nit = parts(l)[1]
                with sp.Fori(1, NT // 2) as it:
                    for k in range(2):
                        sp.wait_ge(xs[l]["kvw"], (2 * it + k - 1) * nit)
                        load_ctx(l, k, 2 * it + k)

            def expert_loads(l, wa, wb_, up, down):
                def load(k, e):
                    for dst, src in zip(up[k], wa):
                        sp.dma_start(dst, io[src].rearrange("e (c p) n -> p (e c) n", p=P)[:, bass.ds(e * dst.shape[1], dst.shape[1]), :])\
                          .then_inc(ms[l][f"w{k}"], 16)
                    sp.dma_start(down[k], io[wb_].rearrange("e (c p) n -> p (e c) n", p=P)[:, bass.ds(e * down[k].shape[1], down[k].shape[1]), :])\
                      .then_inc(ms[l][f"w{k}"], 16)
                load(0, 0)
                load(1, 1)
                with sp.Fori(1, E_ // 2) as it:
                    for k in range(2):
                        sp.wait_ge(ms[l]["dnw"], (2 * it + k - 1) * NT)
                        load(k, 2 * it + k)

            cross_loads(0)
            if stages > 2:
                sp.dma_start(rw0[:, :, :], io["rw0"].rearrange("(c p) n -> p c n", p=P)).then_inc(ms[0]["rl"], 16)
                sp.dma_start(b1sb[:, :, :], io["b1"]).then_inc(ms[0]["rl"], 16)
                sp.dma_start(b2sb[:, :], io["b2"]).then_inc(ms[0]["rl"], 16)
                sp.dma_start(rw1[:, :, :], io["rw1"].rearrange("(c p) n -> p c n", p=P)).then_inc(ms[1]["rl"], 16)
                sp.wait_ge(x_ready, 2)
                expert_loads(0, ["w1a"], "w2a", m0_up, m0_down)
            if stages > 3:
                sp.wait_ge(x_ready, 3)
                cross_loads(1)
            if stages > 5:
                sp.wait_ge(x_ready, 5)
                expert_loads(1, ["w1b", "w3b"], "w2b", m1_up, m1_down)
            sp.wait_ge(x_ready, stages)
            sp.dma_start(out.rearrange("(t p) d -> p t d", p=P), x[:, :, :]).then_inc(out_stored, 16)
            sp.wait_ge(out_stored, 16)

        def after(eng, sem, value):
            if not isinstance(value, int) or value > 0:
                eng.wait_ge(sem, value)

        def before(n, k, u, back):
            u -= back
            if u < 0:
                n, k, u = n - 1, k ^ 1, u + 8
            return None if isinstance(n, int) and n < 0 else (n, k, u)

        def quads(eng, body):
            for k in range(2):
                body(k, k, True)
            with eng.Fori(1, NT // 2 - 1) as it:
                for k in range(2):
                    body(2 * it + k, k, True)
            for k in range(2):
                body(NT - 2 + k, k, k == 0)

        @block.tensor
        def _(pe):
            mm = nc.tensor.matmul

            def turn_xn(s):
                if s == 0:
                    pe.wait_ge(const_loaded, 32)
                for b in range(4):
                    pe.wait_ge(ln_norm, 8 * s + 2 * b + 2)
                    for t in range(2):
                        for c in range(KC):
                            ins = nc.tensor.transpose(bank[b][:, (2 * t + c) * P:(2 * t + c + 1) * P],
                                                      xn[:, 2 * b + t, c * P:c * P + P], ident)
                    ins.then_inc(ln_turned, 1)

            def cross(l):
                q = xs[l]
                steps, nit, place = parts(l)

                def item(n, k, idx, kind, i, pair):
                    after(pe, q["kvc"], n * nit + idx)
                    if idx == 0:
                        pe.wait_ge(q[f"ctx{k}"], 16 * (pair + 1))
                    r = min(P, QS - P * i) if kind != "K" else P
                    if kind == "T":
                        pe.wait_ge(q["krope"], VT * n + i + 1)
                        for c in range(KC):
                            ins = nc.tensor.transpose(bank[7][:, c * P:c * P + P], krope[:, i % 3, c * P:c * P + P], ident)
                    else:
                        for c in range(KC):
                            if kind == "K":
                                j, m = divmod(i, 2)
                                o, a, b = bank[7][:, 0:S], wkv[l][:, c, m * P:m * P + P], ctxb[k][:, c, j * S:j * S + S]
                            elif kind == "V":
                                o, a, b = bank[7][0:r, 0:D], ctxb[k][:, c, P * i:P * i + r], wkv[l][:, c, D:2 * D]
                            else:
                                o, a, b = bank[7][0:r, :], ctxb[k][:, c, P * i:P * i + r], wkv[l][:, c, :]
                            ins = mm(o, a, b, start=(c == 0), stop=(c == KC - 1))
                    ins.then_inc(q["kvw"], 1)

                def scores(n, k, u):
                    j, c = divmod(u, 2)
                    if u == 0:
                        pe.wait_ge(q["kvc"], n * nit + (8 if l == 0 else nit))
                        pe.wait_ge(q["qbd"], 2 * n + 2)
                    after(pe, q["masked" if l == 0 else "probs"], 8 * n + u - 1)
                    for g in range(2):
                        ins = mm(bank[2 * (u % 2) + g][:, 0:S], xqbd[k][:, c, j, 4 * g:4 * g + 4, :],
                                 ktb[k][:, c, j * S:j * S + S], start=True, stop=True)
                    ins.then_inc(q["scores"], 1)

                def turns(n, k, u):
                    j, c = divmod(u, 2)
                    pe.wait_ge(q["probs"], 8 * n + u + 1)
                    after(pe, q["pta"], 8 * n + u)
                    after(pe, q["ptd"], 8 * n + u)
                    for g in range(2):
                        for w in range(3):
                            ins = nc.tensor.transpose(bank[4 + g][:, w * P:w * P + P],
                                                      pwin[j][c][:, g, w * P:w * P + P], ident)
                    ins.then_inc(q["ptw"], 1)

                def collapse(n, k, u):
                    pe.wait_ge(q["normed"], 8 * n + u + 1)
                    mm(bank[6][:, 256:256 + T], omb[u % 2], stack, start=True, stop=True).then_inc(q["colw"], 1)

                def weigh(n, k, u):
                    j, c = divmod(u, 2)
                    if u == 0:
                        pe.wait_ge(q["kvc"], (n + 1) * nit)
                    pe.wait_ge(q["pta"], 8 * n + u + 1)
                    pe.wait_ge(q["ptd"], 8 * n + u + 1)
                    after(pe, q["colc"], 8 * n + u)
                    for g in range(2):
                        for w in range(3):
                            r = P if w < 2 else j + 1
                            ins = mm(bank[6][:, 64 * g:64 * g + 64], pTb[u % 2][0:r, g, w * P:w * P + P],
                                     vb[k][0:r, 2 * j + w, 64 * (2 * c + g):64 * (2 * c + g) + 64],
                                     start=(w == 0), stop=(w == 2))
                    ins.then_inc(q["pvw"], 1)

                pe.wait_ge(wx_loaded[l], 48)
                if l == 0:
                    for i in range(4):
                        m, h = divmod(i, 2)
                        pe.wait_ge(ln_copied, 4 * 0 + 2 * h + 2)
                        after(pe, q["qc"], i - 1)
                        for c in range(KC):
                            ins = mm(bank[4 + i % 2][:, :], wq[0][:, c, m * P:m * P + P], xnT[:, c, h * 512:h * 512 + 512],
                                     start=(c == 0), stop=(c == KC - 1))
                        ins.then_inc(q["qw"], 1)
                else:
                    for t in range(NT):
                        pe.wait_ge(ln_copied, 4 * 3 + t // 2 + 1)
                        after(pe, q["qc"], t - 1)
                        for c in range(KC):
                            ins = mm(bank[4 + t % 2][:, 0:D], xnT[:, c, t * P:t * P + P], wq[1][:, c, :],
                                     start=(c == 0), stop=(c == KC - 1))
                        ins.then_inc(q["qw"], 1)
                for st in steps:
                    for it_ in st:
                        item(0, 0, *it_, 0)
                if l == 1:
                    pe.wait_ge(q["qrope"], 1)
                    for b in range(4):
                        for t in range(2):
                            for c in range(KC):
                                ins = nc.tensor.transpose(bank[b][:, (2 * t + c) * P:(2 * t + c + 1) * P],
                                                          xn[:, 2 * b + t, c * P:c * P + P], ident)
                        ins.then_inc(q["qtw"], 1)
                scores(0, 0, 0)

                def body(n, k, more):
                    for u in range(8):
                        if u < 7:
                            scores(n, k, u + 1)
                        elif more:
                            scores(n + 1, k ^ 1, 0)
                        a, b, c = slot_plan(steps[u] if more else [])
                        pair = (n - k) // 2 if isinstance(n, int) else body.it
                        nxt = [(n + 1, k ^ 1), pair + k]
                        for it_ in a:
                            item(*nxt[0], *it_, nxt[1])
                        turns(n, k, u)
                        past = before(n, k, u, 2)
                        if past:
                            collapse(*past)
                        for it_ in b:
                            item(*nxt[0], *it_, nxt[1])
                        past = before(n, k, u, 1)
                        if past:
                            weigh(*past)
                        for it_ in c:
                            item(*nxt[0], *it_, nxt[1])

                for k in range(2):
                    body(k, k, True)
                with pe.Fori(1, NT // 2 - 1) as it:
                    body.it = it
                    for k in range(2):
                        body(2 * it + k, k, True)
                for k in range(2):
                    body(NT - 2 + k, k, k == 0)
                collapse(NT - 1, 1, 6)
                weigh(NT - 1, 1, 7)
                collapse(NT - 1, 1, 7)
                pe.wait_ge(q["colc"], 8 * NT)
                for t in range(NT):
                    for c in range(KC):
                        ins = mm(bank[t][:, 0:D], outT[:, c, t * P:t * P + P], wo[l][:, c, :],
                                 start=(c == 0), stop=(c == KC - 1))
                    ins.then_inc(q["postw"], 1)

            def selfattn(l):
                q = ss_[l]
                w = NKEY if l == 0 else T
                src = kcT if l == 0 else None
                if l == 0:
                    pe.wait_ge(wa_loaded, 48)
                    for i in range(12):
                        m, h = divmod(i, 2)
                        pe.wait_ge(ln_copied, 4 + 2 * h + 2)
                        after(pe, q["prc"], i - 1)
                        for c in range(KC):
                            ins = mm(bank[4 + i % 2][:, :], wqkv[:, c, m * P:m * P + P], xnT[:, c, h * 512:h * 512 + 512],
                                     start=(c == 0), stop=(c == KC - 1))
                        ins.then_inc(q["prw"], 1)
                    pe.wait_ge(q["bdw"], 1)
                    pe.wait_ge(q["prc"], 12)
                    for i in range(4):
                        kind, c = divmod(i, 2)
                        zsrc = (kT, vT)[kind]
                        for f in range(CF):
                            ins = mm(bank[6 + i % 2][:, (i // 2) * 256:(i // 2) * 256 + 256], bdw[:, c * CF + f, :],
                                     zsrc[:, c, f:TOK:CF], start=(f == 0), stop=(f == CF - 1))
                        ins.then_inc(q["cvw"], 1)
                        if i == 1:
                            pe.wait_ge(q["cvc"], 2)
                    pe.wait_ge(q["cvc"], 4)
                    pe.wait_ge(q["null"], 4)
                    for b in range(4):
                        for t in range(2):
                            for c in range(KC):
                                ins = nc.tensor.transpose(bank[b][:, (2 * t + c) * P:(2 * t + c + 1) * P],
                                                          vcT[:, c, 4 * (2 * b + t):4 * (2 * b + t) + 4, :], ident)
                        ins.then_inc(q["vtw"], 1)
                    pe.wait_ge(q["vtc"], 4)
                else:
                    pe.wait_ge(ln_copied, 4 * 5)

                def scores(n, k):
                    pe.wait_ge(q["qbd"], 2 * n + 2)
                    after(pe, q["sub"], n - 1)
                    for j in range(QB):
                        for g in range(GH):
                            if l == 0:
                                keys = kcT.rearrange("p c b w -> p c (b w)")[:, g // 2, bass.ds(n * P + KW * j, w)]
                            else:
                                keys = xnT[:, g // 2, bass.ds(n * P + T * j, w)]
                            at = (4 * j + g) * KW
                            ins = mm(bank[k][:, at:at + w], sqbd[k][:, g // 2, j, 4 * (g % 2):4 * (g % 2) + 4, :], keys,
                                     start=True, stop=True)
                    ins.then_inc(q["sw"], 1)

                def rest(n, k):
                    pe.wait_ge(q["pn"], n + 1)
                    after(pe, q["colc"], n - 1)
                    for g in range(GH):
                        ins = nc.tensor.transpose(bank[2 + k][:, g * P:g * P + P], pn[k][:, g, :, :], ident)
                    ins.then_inc(q["ptw"], 1)
                    pe.wait_ge(q["ptc"], n + 1)
                    pe.wait_ge(q["vq"], n + 1)
                    after(pe, q["om"], n)
                    for j in range(QB):
                        for g in range(GH):
                            ins = mm(bank[4 + j][:, 64 * g:64 * g + 64], spT[k][T * j:T * j + w, g, :],
                                     vq[k][T * j:T * j + w, 64 * g:64 * g + 64], start=True, stop=True)
                    ins.then_inc(q["pvw"], 1)
                    pe.wait_ge(q["om"], n + 1)
                    if l == 0:
                        for j in range(QB):
                            for c in range(KC):
                                ins = mm(bank[2 + k][:, c * P + T * j:c * P + T * j + T], som[:, j, c * P:c * P + P], stack,
                                         start=True, stop=True)
                    else:
                        for j in range(QB):
                            ins = mm(bank[2 + k][T * j:T * j + T, 0:D], stack, som[:, j, :], start=True, stop=True)
                    ins.then_inc(q["colw"], 1)

                def body(n, k, more):
                    if more:
                        scores(n + 1, k ^ 1)
                    rest(n, k)

                scores(0, 0)
                quads(pe, body)
                if l == 0:
                    pe.wait_ge(q["colc"], NT)
                    for i in range(4):
                        m, h = divmod(i, 2)
                        for c in range(KC):
                            ins = mm(bank[i][:, :], wout[:, c, m * P:m * P + P], outT[:, c, h * 512:h * 512 + 512],
                                     start=(c == 0), stop=(c == KC - 1))
                        ins.then_inc(q["zw"], 1)
                    pe.wait_ge(q["zc"], 4)

                    def along_channels(t):
                        after(pe, q["ac"], t - 1)
                        for c in range(KC):
                            ins = mm(bank[4 + t % 2][:, :], zT[:, c, t * P:t * P + P],
                                     const[:, C_CS + c * 2 * D:C_CS + (c + 1) * 2 * D], start=(c == 0), stop=(c == KC - 1))
                        ins.then_inc(q["aw"], 1)

                    def along_tokens(t):
                        pe.wait_ge(q["ac"], t + 1)
                        after(pe, q["yc"], t - 1)
                        for c in range(2):
                            ins = mm(bank[6 + t % 2][:, 0:D], const[:, C_BD + c * P:C_BD + c * P + P],
                                     af[t % 2][:, c * D:c * D + D], start=(c == 0), stop=(c == 1))
                        ins.then_inc(q["yw"], 1)

                    along_channels(0)
                    for t in range(NT):
                        if t + 1 < NT:
                            along_channels(t + 1)
                        along_tokens(t)

            def experts(l, s):
                q = ms[l]
                up, down, h = ((m0_up, m0_down, m0_h), (m1_up, m1_down, m1_h))[l]
                nh = (H0, H1)[l] // P
                rw = (rw0, rw1)[l]
                pe.wait_ge(ln_copied, 4 * (s + 1))
                pe.wait_ge(q["rl"], 48 if l == 0 else 16)
                for t in range(NT):
                    for c in range(KC):
                        ins = mm(bank[7][:, t * E_:t * E_ + E_], xnT[:, c, t * P:t * P + P], rw[:, c, :],
                                 start=(c == 0), stop=(c == KC - 1))
                ins.then_inc(q["lgw"], 1)

                def raise_(i, k, pair, half):
                    if half % 2 == 0:
                        pe.wait_ge(q[f"w{k}"], (32 if l == 0 else 48) * (pair + 1))
                    for m in range(nh):
                        after(pe, q["upc"], i * nh + m - 1)
                        for v in range(len(up[k])):
                            for c in range(KC):
                                ins = mm(bank[2 * v + m % 2][:, :], up[k][v][:, c, m * P:m * P + P],
                                         xnT[:, c, (half % 2) * 512:(half % 2) * 512 + 512],
                                         start=(c == 0), stop=(c == KC - 1))
                        ins.then_inc(q["upw"], 1)

                def lower(i, k, half):
                    pe.wait_ge(q["upc"], (i + 1) * nh)
                    for t in range(4):
                        after(pe, q["dnc"], 4 * i + t - 1)
                        for m in range(nh):
                            ins = mm(bank[4 + t % 2][:, 0:D], h[half % 2][:, m, t * P:t * P + P], down[k][:, m, :],
                                     start=(m == 0), stop=(m == nh - 1))
                        ins.then_inc(q["dnw"], 1)

                def body(i0, pair, more):
                    for half in range(4):
                        if half < 3:
                            raise_(i0 + half + 1, (half + 1) // 2, pair, half + 1)
                        elif more:
                            raise_(i0 + 4, 0, pair + 1, 0)
                        lower(i0 + half, half // 2, half)

                raise_(0, 0, 0, 0)
                if l == 0:
                    pe.wait_ge(q["gate"], 1)
                    for t in range(NT):
                        ins = nc.tensor.transpose(bank[6 + t // 4][0:E_, (t % 4) * P:(t % 4) * P + P], gate[:, t, :], ident)
                    ins.then_inc(q["cwt"], 1)
                    pe.wait_ge(q["cwtc"], 2)
                    for t in range(NT):
                        after(pe, q["cwbc"], t - 1)
                        mm(bank[6 + t % 2][:, 0:D], gateT[:, t * P:t * P + P], b2sb[:, :], start=True, stop=True)\
                            .then_inc(q["cwb"], 1)
                body(0, 0, True)
                with pe.Fori(1, E_ // 2 - 1) as it:
                    body(4 * it, it, True)
                body(2 * E_ - 4, E_ // 2 - 1, False)

            turn_xn(0)
            cross(0)
            if stages > 1:
                turn_xn(1)
                selfattn(0)
            if stages > 2:
                turn_xn(2)
                experts(0, 2)
            if stages > 3:
                turn_xn(3)
                cross(1)
            if stages > 4:
                turn_xn(4)
                selfattn(1)
            if stages > 5:
                turn_xn(5)
                experts(1, 5)

        @block.scalar
        def _(act):
            copy = ACT.Copy
            A = nc.scalar.activation

            def ln_root(s):
                act.wait_ge(ln_var, s + 1)
                A(ln_sd[:, :], ln_ve[:, :], ACT.Sqrt).then_inc(ln_std, 1)

            def ln_copy(s):
                for b in range(4):
                    act.wait_ge(ln_turned, 4 * s + b + 1)
                    A(xnT[:, :, 256 * b:256 * b + 256].rearrange("p c (t q) -> p t c q", t=2),
                      bank[b][:, :].rearrange("p (t c q) -> p t c q", t=2, c=KC), copy).then_inc(ln_copied, 1)

            def cross(l):
                q = xs[l]
                steps, nit, place = parts(l)

                def item(n, k, idx, kind, i):
                    act.wait_ge(q["kvw"], n * nit + idx + 1)
                    r = min(P, QS - P * i)
                    if kind == "K":
                        j, m = divmod(i, 2)
                        ins = A(ktb[k][:, m, j * S:j * S + S], bank[7][:, 0:S], ACT.Identity, bias=vec[:, V_BK + m:V_BK + m + 1])
                    elif kind == "V":
                        ins = A(vb[k][0:r, i, :], bank[7][0:r, 0:D], copy)
                    elif kind == "A":
                        after(act, q["krope"], VT * n + i - 2)
                        A(ksq[0:r, i % 3, :], bank[7][0:r, 0:D], ACT.Square).then_inc(q["sq"], 1)
                        A(kraw[0:r, i % 3, :], bank[7][0:r, 0:D], copy)
                        ins = A(vb[k][0:r, i, :], bank[7][0:r, D:2 * D], copy)
                    else:
                        ins = A(ktb[k][:, :, P * i:P * i + r],
                                bank[7][:, 0:2 * P].rearrange("p (c r) -> p c r", c=KC)[:, :, 0:r], copy)
                    ins.then_inc(q["kvc"], 1)

                def exps(n, k, u):
                    j, c = divmod(u, 2)
                    act.wait_ge(q["negmax"], 8 * n + u + 1)
                    after(act, q["recip"], 8 * n + u - 1)
                    for g in range(2):
                        src = smask[u % 2][:, g, :] if l == 0 else bank[2 * (u % 2) + g][:, 0:S]
                        ins = A(pwin[j][c][:, g, j:j + S], src, ACT.Exp, bias=negmax[u % 2][:, g:g + 1],
                                accum_out=rowsum[u % 2][:, g:g + 1])
                    ins.then_inc(q["probs"], 1)

                def turned(n, k, u):
                    act.wait_ge(q["ptw"], 8 * n + u + 1)
                    A(pTb[u % 2][:, 0, :], bank[4][:, 0:WIN], copy).then_inc(q["pta"], 1)

                if l == 0:
                    for i in range(4):
                        m, h = divmod(i, 2)
                        act.wait_ge(q["qw"], i + 1)
                        A(qT[:, m, h * 512:h * 512 + 512], bank[4 + i % 2][:, :], ACT.Identity,
                          bias=vec[:, V_BQ + m:V_BQ + m + 1]).then_inc(q["qc"], 1)
                else:
                    qsq = outT.rearrange("p c n -> p (c n)").rearrange("p (t d) -> p t d", t=NT)
                    for t in range(NT):
                        act.wait_ge(q["qw"], t + 1)
                        A(qsq[:, t, :], bank[4 + t % 2][:, 0:D], ACT.Square)
                        A(xn[:, t, :], bank[4 + t % 2][:, 0:D], copy).then_inc(q["qc"], 1)
                for st in steps:
                    for it_ in st:
                        item(0, 0, *it_)
                if l == 1:
                    for b in range(4):
                        act.wait_ge(q["qtw"], b + 1)
                        A(qT[:, :, 256 * b:256 * b + 256].rearrange("p c (t q) -> p t c q", t=2),
                          bank[b][:, :].rearrange("p (t c q) -> p t c q", t=2, c=KC), copy).then_inc(q["qtc"], 1)
                exps(0, 0, 0)

                def body(n, k, more):
                    for u in range(8):
                        a, b, c = slot_plan(steps[u] if more else [])
                        for it_ in a:
                            item(n + 1, k ^ 1, *it_)
                        if u < 7:
                            exps(n, k, u + 1)
                        elif more:
                            exps(n + 1, k ^ 1, 0)
                        turned(n, k, u)
                        for it_ in b + c:
                            item(n + 1, k ^ 1, *it_)

                quads(act, body)

            def selfattn(l):
                q = ss_[l]
                w = NKEY if l == 0 else T
                if l == 0:
                    for i in range(12):
                        m, h = divmod(i, 2)
                        act.wait_ge(q["prw"], i + 1)
                        dst = (qT, kT, vT)[m // 2][:, m % 2, h * 512:h * 512 + 512]
                        A(dst, bank[4 + i % 2][:, :], copy).then_inc(q["prc"], 1)
                    act.wait_ge(q["zeroed"], 1)
                    for i in range(4):
                        kind, c = divmod(i, 2)
                        act.wait_ge(q["cvw"], i + 1)
                        A((kcT, vcT)[kind][:, c, :, 1:NKEY],
                          bank[6 + i % 2][:, (i // 2) * 256:(i // 2) * 256 + 256].rearrange("p (b k) -> p b k", b=B),
                          ACT.Identity, bias=vec[:, V_CB + c:V_CB + c + 1]).then_inc(q["cvc"], 1)
                    for b in range(4):
                        act.wait_ge(q["vtw"], b + 1)
                        A(vall[:, 2 * b:2 * b + 2, :], bank[b][:, :].rearrange("p (t d) -> p t d", t=2), copy)\
                            .then_inc(q["vtc"], 1)

                def exps(n, k):
                    act.wait_ge(q["sub"], n + 1)
                    A(sprob[k][:, :, 0:w], sprob[k][:, :, 0:w], ACT.Exp).then_inc(q["exp"], 1)

                def body(n, k, more):
                    if more:
                        exps(n + 1, k ^ 1)
                    act.wait_ge(q["ptw"], n + 1)
                    A(spT[k].rearrange("p g q -> p (g q)"), bank[2 + k][:, :], copy).then_inc(q["ptc"], 1)

                exps(0, 0)
                quads(act, body)
                if l == 0:
                    for i in range(4):
                        m, h = divmod(i, 2)
                        act.wait_ge(q["zw"], i + 1)
                        A(zT[:, m, h * 512:h * 512 + 512], bank[i][:, :], ACT.Identity,
                          bias=vec[:, V_BO + m:V_BO + m + 1]).then_inc(q["zc"], 1)
                    for t in range(NT):
                        act.wait_ge(q["aw"], t + 1)
                        after(act, q["yw"], t - 1)
                        A(af[t % 2], bank[4 + t % 2][:, :], copy).then_inc(q["ac"], 1)

            def experts(l):
                q = ms[l]
                h = (m0_h, m1_h)[l]
                nh = (H0, H1)[l] // P
                if l == 0:
                    act.wait_ge(q["lgw"], 1)
                    act.wait_ge(q["gate0"], 1)
                    A(lg[:, :, :], lg[:, :, :], ACT.Exp).then_inc(q["gexp"], 1)
                else:
                    act.wait_ge(q["gate0"], 1)
                    A(gsm[:, 1, :], gsm[:, 0, :], ACT.Exp).then_inc(q["gexp"], 1)

                def half_(i, k, half):
                    if l == 0 and half % 2 == 0:
                        act.wait_ge(q["b"], i // 2 + 1 if isinstance(i, int) else half_.expert + 1)
                    for m in range(nh):
                        act.wait_ge(q["upw"], i * nh + m + 1)
                        if l == 0:
                            A(h[half % 2][:, m, :], bank[m % 2][:, :], ACT.Gelu_apprx_tanh, bias=b1_e[k][:, m:m + 1])\
                                .then_inc(q["upc"], 1)
                        else:
                            after(act, q["upc"], i * nh + m - 1)
                            A(m1_silu[m % 2], bank[m % 2][:, :], ACT.Silu).then_inc(q["mul"], 1)

                def body(i0, pair, more):
                    for half in range(4):
                        half_.expert = 2 * pair + half // 2
                        half_(i0 + half, half // 2, half)

                body(0, 0, True)
                with act.Fori(1, E_ // 2) as it:
                    body(4 * it, it, True)

            for s in range(stages):
                ln_root(s)
                ln_copy(s)
                (lambda: cross(0), lambda: selfattn(0), lambda: experts(0),
                 lambda: cross(1), lambda: selfattn(1), lambda: experts(1))[s]()

        @block.vector
        def _(dve):
            V = nc.vector
            own = Tally(ln_own)

            def mine(ins):
                dve.wait_ge(ln_own, own.inc(ins))

            def ln(s):
                if s == 0:
                    dve.wait_ge(x_loaded, 16)
                else:
                    dve.wait_ge(x_ready, s)
                for t in range(NT):
                    ins = V.bn_stats(ln_stats[:, t, :], x[:, t, :])
                mine(ins)
                for t in range(NT):
                    ins = V.bn_aggr(ln_mv[:, t, :], ln_stats[:, t, :])
                mine(ins)
                V.tensor_scalar(ln_ve[:, :], ln_mv[:, :, 1], 1e-5, None, ALU.add).then_inc(ln_var, 1)
                dve.wait_ge(ln_std, s + 1)
                mine(V.reciprocal(ln_rs[:, :], ln_sd[:, :]))
                for t in range(NT):
                    V.tensor_scalar(xn[:, t, :], x[:, t, :], ln_mv[:, t, 0:1], ln_rs[:, t:t + 1],
                                    ALU.subtract, ALU.mult).then_inc(ln_norm, 1)

            def finish(ins, q, t):
                ins.then_inc(x_ready if t == NT - 1 else q, 1)

            def cross(l):
                q = xs[l]
                steps, nit, place = parts(l)

                def item(n, idx, kind, i):
                    if kind == "A":
                        r = min(P, QS - P * i)
                        dve.wait_ge(q["sq"], VT * n + i + 1)
                        V.tensor_reduce(kss[0:r, i % 3, :], ksq[0:r, i % 3, :].rearrange("p (h d) -> p h d", d=HD),
                                        AX_X, ALU.add).then_inc(q["ss"], 1)

                def maxima(n, u):
                    p = u % 2
                    after(dve, q["negmax"], 8 * n + u)
                    dve.wait_ge(q["scores"], 8 * n + u + 1)
                    if l == 0:
                        V.memset(spare[:, :], 0.0)
                        for g in range(2):
                            ins = V.tensor_tensor_reduce(smask[p][:, g, :], bank[2 * p + g][:, 0:S], negmask[:, :],
                                                         1.0, float(np.finfo(np.float32).min), ALU.add, ALU.max,
                                                         rowmax[:, g:g + 1])
                        ins.then_inc(q["masked"], 1)
                        dve.wait_ge(q["masked"], 8 * n + u + 1)
                        V.tensor_scalar(negmax[p], rowmax[:, :], -1.0, None, ALU.mult).then_inc(q["negmax"], 1)
                    else:
                        for g in range(2):
                            ins = V.tensor_reduce(negmax[p][:, g:g + 1], bank[2 * p + g][:, 0:S], AX_X, ALU.max, negate=True)
                        ins.then_inc(q["negmax"], 1)

                def invert(n, u):
                    after(dve, q["normed"], 8 * n + u - 1)
                    dve.wait_ge(q["probs"], 8 * n + u + 1)
                    V.reciprocal(rcp[u % 2], rowsum[u % 2]).then_inc(q["recip"], 1)

                def turned(n, u):
                    dve.wait_ge(q["ptw"], 8 * n + u + 1)
                    V.tensor_copy(pTb[u % 2][:, 1, :], bank[5][:, 0:WIN]).then_inc(q["ptd"], 1)

                def norm(n, u):
                    dve.wait_ge(q["pvw"], 8 * n + u + 1)
                    dve.wait_ge(q["recip"], 8 * n + u + 1)
                    for g in range(2):
                        ins = V.scalar_tensor_tensor(omb[u % 2][:, 64 * g:64 * g + 64], bank[6][:, 64 * g:64 * g + 64],
                                                     rcp[u % 2][:, g:g + 1], blk, ALU.mult, ALU.mult)
                    ins.then_inc(q["normed"], 1)

                def collapsed(n, u):
                    j, c = divmod(u, 2)
                    dve.wait_ge(q["colw"], 8 * n + u + 1)
                    dst = outT[:, c, bass.ds(n * P + T * j, T)]
                    if l == 0:
                        ins = V.tensor_scalar(dst, bank[6][:, 256:256 + T], vec[:, V_BV + c:V_BV + c + 1], None, ALU.add)
                    else:
                        ins = V.tensor_copy(dst, bank[6][:, 256:256 + T])
                    ins.then_inc(q["colc"], 1)

                if l == 0:
                    dve.wait_ge(mask_loaded, 16 * (QB + 1))
                    mine(V.tensor_scalar(negmask[:, :], negmask[:, :], -1e9, None, ALU.mult))
                    for t in range(NT):
                        ins = V.tensor_tensor(x[:, t, :], x[:, t, :], bo_bc[:, :], ALU.add)
                    mine(ins)
                else:
                    q1 = outT.rearrange("p c n -> p (c n)")
                    q2 = qT.rearrange("p c n -> p (c n)")
                    q0 = xn.rearrange("p t d -> p (t d)")
                    h3 = lambda v: v.rearrange("p (a d) -> p a d", d=HD)
                    bc = lambda v, n: v.unsqueeze(1).to_broadcast([P, NT * NH, n])
                    dve.wait_ge(q["qc"], NT)
                    V.tensor_reduce(qss[:, :], h3(q1), AX_X, ALU.add).then_inc(q["qss"], 1)
                    dve.wait_ge(q["qr"], 1)
                    mine(V.tensor_tensor(h3(q0), h3(q0), qr[:, :].unsqueeze(2).to_broadcast([P, NT * NH, HD]), ALU.mult))
                    dve.wait_ge(q["rw"], 1)
                    V.tensor_tensor(h3(q1), h3(q0), bc(rope_q[:, 0:HD], HD), ALU.mult)
                    V.tensor_tensor(h3(q2)[:, :, 0:8], h3(q0)[:, :, 8:16], bc(rope_q[:, HD:HD + 8], 8), ALU.mult)
                    mine(V.tensor_tensor(h3(q2)[:, :, 8:16], h3(q0)[:, :, 0:8], bc(rope_q[:, HD + 8:2 * HD], 8), ALU.mult))
                    V.tensor_tensor(q0, q1, q2, ALU.add).then_inc(q["qrope"], 1)
                    for st in steps:
                        for it_ in st:
                            item(0, *it_)
                maxima(0, 0)

                def body(n, k, more):
                    for u in range(8):
                        a, b, c = slot_plan(steps[u] if more else [])
                        if u < 7:
                            maxima(n, u + 1)
                        elif more:
                            maxima(n + 1, 0)
                        for it_ in a:
                            item(n + 1, *it_)
                        invert(n, u)
                        turned(n, u)
                        past = before(n, k, u, 2)
                        if past:
                            collapsed(past[0], past[2])
                        for it_ in b:
                            item(n + 1, *it_)
                        past = before(n, k, u, 1)
                        if past:
                            norm(past[0], past[2])
                        for it_ in c:
                            item(n + 1, *it_)

                quads(dve, body)
                collapsed(NT - 1, 6)
                norm(NT - 1, 7)
                collapsed(NT - 1, 7)
                for t in range(NT):
                    dve.wait_ge(q["postw"], t + 1)
                    finish(V.tensor_tensor(x[:, t, :], x[:, t, :], bank[t][:, 0:D], ALU.add), q["xadd"], t)

            def selfattn(l):
                q = ss_[l]
                w = NKEY if l == 0 else T
                step = Tally(q["own"])

                def scores(n, k):
                    after(dve, q["sub"], n)
                    after(dve, q["pn"], n)
                    dve.wait_ge(q["sw"], n + 1)
                    s3 = sprob[k][:, :, 0:w]
                    raw = bank[k][:, :].rearrange("p (a w) -> p a w", w=KW)[:, :, 0:w]
                    mcol = const[:, (C_M0, C_M1)[l]:(C_M0, C_M1)[l] + w]
                    V.tensor_tensor(s3, raw, mcol.unsqueeze(1).to_broadcast([P, NH, w]), ALU.add).then_inc(q["own"], 1)
                    dve.wait_ge(q["own"], 2 * n + 1)
                    V.tensor_reduce(smx[:, :], s3, AX_X, ALU.max).then_inc(q["own"], 1)
                    dve.wait_ge(q["own"], 2 * n + 2)
                    V.tensor_tensor(s3, s3, smx[:, :].unsqueeze(2).to_broadcast([P, NH, w]), ALU.subtract)\
                        .then_inc(q["sub"], 1)

                def norm(n, k):
                    dve.wait_ge(q["exp"], n + 1)
                    s3 = sprob[k][:, :, 0:w]
                    V.tensor_reduce(ssum[:, :], s3, AX_X, ALU.add).then_inc(q["sum"], 1)
                    dve.wait_ge(q["sum"], 2 * n + 1)
                    V.reciprocal(srcp[:, :], ssum[:, :]).then_inc(q["sum"], 1)
                    dve.wait_ge(q["sum"], 2 * n + 2)
                    V.tensor_tensor(pn[k].rearrange("p g j w -> p j g w")[:, :, :, 0:w],
                                    s3.rearrange("p (j g) w -> p j g w", j=QB),
                                    srcp[:, :].rearrange("p (j g) -> p j g", j=QB).unsqueeze(3).to_broadcast([P, QB, GH, w]),
                                    ALU.mult).then_inc(q["pn"], 1)

                def mask_heads(n, k):
                    dve.wait_ge(q["pvw"], n + 1)
                    for j in range(QB):
                        ins = V.tensor_tensor(som[:, j, :].rearrange("p (g d) -> p g d", d=64),
                                              bank[4 + j][:, 0:D].rearrange("p (g d) -> p g d", d=64),
                                              blk.unsqueeze(1).to_broadcast([P, GH, 64]), ALU.mult)
                    ins.then_inc(q["om"], 1)

                def collapsed(n, k):
                    dve.wait_ge(q["colw"], n + 1)
                    if l == 0:
                        V.tensor_copy(outT[:, :, bass.ds(n * P, P)],
                                      bank[2 + k][:, 0:2 * P].rearrange("p (c q) -> p c q", c=KC)).then_inc(q["colc"], 1)
                    else:
                        xv = x.rearrange("p t d -> p (t d)")[:, bass.ds(n * D, D)]
                        V.tensor_tensor(xv, xv, bank[2 + k][:, 0:D], ALU.add).then_inc(q["colc"], 1)

                def body(n, k, more):
                    if more:
                        scores(n + 1, k ^ 1)
                    mask_heads(n, k)
                    if more:
                        norm(n + 1, k ^ 1)
                    collapsed(n, k)

                if l == 0:
                    for i in range(4):
                        kind, c = divmod(i, 2)
                        if i == 0:
                            dve.wait_ge(q["zeroed"], 1)
                        V.tensor_copy((kcT, vcT)[kind][:, c, :, 0:1],
                                      vec[:, (V_NK, V_NV)[kind] + c:(V_NK, V_NV)[kind] + c + 1].unsqueeze(1)
                                      .to_broadcast([P, B, 1])).then_inc(q["null"], 1)
                scores(0, 0)
                norm(0, 0)
                quads(dve, body)
                if l == 0:
                    for t in range(NT):
                        dve.wait_ge(q["yw"], t + 1)
                        finish(V.tensor_tensor(x[:, t, :], x[:, t, :], bank[6 + t % 2][:, 0:D], ALU.add), q["yc"], t)
                else:
                    dve.wait_ge(q["colc"], NT)
                    V.memset(spare[:, :], 0.0).then_inc(x_ready, 1)

            def experts(l, s):
                q = ms[l]
                nh = (H0, H1)[l] // P
                dve.wait_ge(q["lgw"], 1)
                raw = bank[7][:, 0:NT * E_].rearrange("p (t e) -> p t e", e=E_)
                mine(V.tensor_copy(pr[:, :, :], raw))
                b3 = lambda v: v.unsqueeze(2).to_broadcast([P, NT, E_])
                if l == 0:
                    mine(V.tensor_reduce(gsm[:, 0, :], pr[:, :, :], AX_X, ALU.max))
                    V.tensor_tensor(lg[:, :, :], pr[:, :, :], b3(gsm[:, 0, :]), ALU.subtract).then_inc(q["gate0"], 1)
                    dve.wait_ge(q["gexp"], 1)
                    mine(V.tensor_reduce(gsm[:, 0, :], lg[:, :, :], AX_X, ALU.add))
                    mine(V.reciprocal(gsm[:, 1, :], gsm[:, 0, :]))
                    mine(V.tensor_tensor(pr[:, :, :], lg[:, :, :], b3(gsm[:, 1, :]), ALU.mult))
                for t in range(NT):
                    ins = V.max(top[:, t, :], pr[:, t, :])
                mine(ins)
                for t in range(NT):
                    ins = V.max_index(topi[:, t, :], top[:, t, :], pr[:, t, :])
                mine(ins)
                mine(V.tensor_copy(topf[:, :, 0:2], topi[:, :, 0:2]))
                if l == 0:
                    mine(V.tensor_tensor(gsm[:, 0, :], top[:, :, 0], top[:, :, 1], ALU.add))
                    mine(V.tensor_scalar(gsm[:, 0, :], gsm[:, 0, :], 1e-8, None, ALU.add))
                    mine(V.reciprocal(gsm[:, 1, :], gsm[:, 0, :]))
                    V.tensor_tensor(gsm[:, 2, :], top[:, :, 0], gsm[:, 1, :], ALU.mult)
                    mine(V.tensor_tensor(gsm[:, 3, :], top[:, :, 1], gsm[:, 1, :], ALU.mult))
                else:
                    V.tensor_tensor(gsm[:, 0, :], top[:, :, 1], top[:, :, 0], ALU.subtract).then_inc(q["gate0"], 1)
                    dve.wait_ge(q["gexp"], 1)
                    mine(V.tensor_scalar(gsm[:, 0, :], gsm[:, 1, :], 1.0, None, ALU.add))
                    mine(V.reciprocal(gsm[:, 2, :], gsm[:, 0, :]))
                    mine(V.tensor_tensor(gsm[:, 3, :], gsm[:, 1, :], gsm[:, 2, :], ALU.mult))
                iota = const[:, C_IOTA:C_IOTA + E_].unsqueeze(1).to_broadcast([P, NT, E_])
                for i, dst in enumerate((gate, gate1)):
                    mine(V.tensor_tensor(dst[:, :, :], iota, b3(topf[:, :, i]), ALU.is_equal))
                    mine(V.tensor_tensor(dst[:, :, :], dst[:, :, :], b3(gsm[:, 2 + i, :]), ALU.mult))
                V.tensor_tensor(gate[:, :, :], gate[:, :, :], gate1[:, :, :], ALU.add).then_inc(q["gate"], 1)
                dve.wait_ge(q["gate"], 1)
                if l == 0:
                    dve.wait_ge(q["rl"], 48)
                bcol = b1sb.rearrange("p e m -> p (e m)")

                def expert(e, k):
                    if not (isinstance(e, int) and e < 2):
                        dve.wait_ge(q["dnc"], 8 * (e - 1))
                    V.tensor_copy(gate_e[k][:, :], gate.rearrange("p t e -> p e t")[:, bass.ds(e, 1), :]).then_inc(q["ge"], 1)
                    if l == 0:
                        V.tensor_copy(b1_e[k][:, :], bcol[:, bass.ds(e * nh, nh)]).then_inc(q["b"], 1)

                def prod(i, k, half):
                    if l == 1:
                        for m in range(nh):
                            dve.wait_ge(q["mul"], i * nh + m + 1)
                            V.tensor_tensor(m1_h[half % 2][:, m, :], bank[2 + m % 2][:, :], m1_silu[m % 2], ALU.mult)\
                                .then_inc(q["upc"], 1)

                def add(i, k, half, pair):
                    if half % 2 == 0:
                        dve.wait_ge(q["ge"], 2 * pair + half // 2 + 1)
                    for t in range(4):
                        tt = 4 * (half % 2) + t
                        dve.wait_ge(q["dnw"], 4 * i + t + 1)
                        if not (isinstance(i, int) and i == 0 and t == 0):
                            dve.wait_ge(q["dnc"], 4 * i + t)
                        V.scalar_tensor_tensor(x[:, tt, :], bank[4 + t % 2][:, 0:D], gate_e[k][:, tt:tt + 1], x[:, tt, :],
                                               ALU.mult, ALU.add).then_inc(q["dnc"], 1)

                def body(i0, pair, more):
                    for half in range(4):
                        if half == 1:
                            expert(2 * pair + 1, 1)
                        if half < 3:
                            prod(i0 + half + 1, (half + 1) // 2, half + 1)
                        elif more:
                            expert(2 * pair + 2, 0)
                            prod(i0 + 4, 0, 0)
                        add(i0 + half, half // 2, half, pair)

                expert(0, 0)
                prod(0, 0, 0)
                if l == 0:
                    dve.wait_ge(q["cwt"], 1)
                    for b in range(2):
                        V.tensor_copy(gateT[:, 512 * b:512 * b + 512], bank[6 + b][0:E_, :]).then_inc(q["cwtc"], 1)
                    for t in range(NT):
                        dve.wait_ge(q["cwb"], t + 1)
                        V.tensor_tensor(x[:, t, :], x[:, t, :], bank[6 + t % 2][:, 0:D], ALU.add).then_inc(q["cwbc"], 1)
                    dve.wait_ge(q["cwbc"], NT)
                body(0, 0, True)
                with dve.Fori(1, E_ // 2 - 1) as it:
                    body(4 * it, it, True)
                body(2 * E_ - 4, E_ // 2 - 1, False)
                dve.wait_ge(q["dnc"], 8 * E_)
                V.memset(spare[:, :], 0.0).then_inc(x_ready, 1)

            for s in range(stages):
                ln(s)
                (lambda: cross(0), lambda: selfattn(0), lambda: experts(0, 2),
                 lambda: cross(1), lambda: selfattn(1), lambda: experts(1, 5))[s]()

        @block.gpsimd
        def _(pool):
            G = nc.gpsimd

            def spread(dst, src, n, col, q):
                for c in range(KC):
                    G.tensor_tensor(dst[:, c, :, :, :],
                                    src[:, c, bass.ds(n * P, P)].rearrange("p (j q) -> p j q", j=QB).unsqueeze(2)
                                    .to_broadcast([P, QB, 8, T]),
                                    const[:, col:col + 8].unsqueeze(1).unsqueeze(3).to_broadcast([P, QB, 8, T]),
                                    ALU.mult).then_inc(q["qbd"], 1)

            def cross(l, s):
                q = xs[l]
                steps, nit, place = parts(l)
                own = Tally(q["own"])
                if s:
                    pool.wait_ge(x_ready, s)
                for j in range(QB):
                    for c in range(KC):
                        own.inc(G.memset(pwin[j][c], 0.0))
                if l == 1:
                    pool.wait_ge(normw_loaded, 16)
                    pool.wait_ge(const_loaded, 32)
                    own.inc(G.memset(mhalf[:, :], -0.5))
                    own.inc(G.memset(eps16[:, :], 1e-6 * HD))
                    for base, m_, dst in ((C_RQ, 1, 0), (C_RK, VT, 32)):
                        which = 0 if base == C_RQ else 1
                        tab = const[:, base:base + 32 * m_].rearrange("p (m k) -> p m k", k=32)
                        o = ropew[:, dst:dst + 32 * m_].rearrange("p (m k) -> p m k", k=32)
                        for a, b, wa in ((0, 16, 0), (16, 24, 8), (24, 32, 0)):
                            wv = normw[:, which, wa:wa + b - a].unsqueeze(1).to_broadcast([P, m_, b - a])
                            ins = G.tensor_tensor(o[:, :, a:b], tab[:, :, a:b], wv, ALU.mult)
                            own.inc(ins)
                    pool.wait_ge(q["own"], own.n)
                    G.memset(mark[:, :], 0.0).then_inc(q["rw"], 1)
                    pool.wait_ge(q["qss"], 1)
                    own.inc(G.tensor_tensor(qvar[:, :], qss[:, :], eps16[:, :], ALU.add))
                    pool.wait_ge(q["own"], own.n)
                    G.tensor_tensor(qr[:, :], qvar[:, :], mhalf[:, :], ALU.pow).then_inc(q["qr"], 1)
                pool.wait_ge(q["own"], own.n)

                def rotate(n, i):
                    r = min(P, QS - P * i)
                    base = (VT * n + i) * 5
                    rt = rope_k(i)
                    h3 = lambda v: v[0:r, :].rearrange("p (h d) -> p h d", d=HD)
                    bc = lambda v, m: v[0:r, :].unsqueeze(1).to_broadcast([r, NH, m])
                    after(pool, q["krope"], VT * n + i)
                    pool.wait_ge(q["ss"], VT * n + i + 1)
                    G.tensor_tensor(kvar[0:r, :], kss[0:r, i % 3, :], eps16[0:r, 0:NH], ALU.add).then_inc(q["kn"], 1)
                    pool.wait_ge(q["kn"], base + 1)
                    G.tensor_tensor(kr[0:r, :], kvar[0:r, :], mhalf[0:r, 0:NH], ALU.pow).then_inc(q["kn"], 1)
                    pool.wait_ge(q["kn"], base + 2)
                    pool.wait_ge(q["kvc"], nit * n + place["A", i] + 1)
                    G.tensor_tensor(h3(kn), h3(kraw[:, i % 3, :]), kr[0:r, :].unsqueeze(2).to_broadcast([r, NH, HD]),
                                    ALU.mult).then_inc(q["kn"], 1)
                    pool.wait_ge(q["kn"], base + 3)
                    G.tensor_tensor(h3(ka), h3(kn), bc(rt[:, 0:HD], HD), ALU.mult)
                    G.tensor_tensor(h3(kb_)[:, :, 0:8], h3(kn)[:, :, 8:16], bc(rt[:, HD:HD + 8], 8), ALU.mult)\
                        .then_inc(q["kn"], 1)
                    G.tensor_tensor(h3(kb_)[:, :, 8:16], h3(kn)[:, :, 0:8], bc(rt[:, HD + 8:2 * HD], 8), ALU.mult)\
                        .then_inc(q["kn"], 1)
                    pool.wait_ge(q["kn"], base + 5)
                    if i >= 3:
                        pool.wait_ge(q["kvw"], nit * n + place["T", i - 3] + 1)
                    elif not (isinstance(n, int) and n == 0):
                        pool.wait_ge(q["kvw"], nit * (n - 1) + place["T", i + VT - 3] + 1)
                    G.tensor_tensor(krope[0:r, i % 3, :], ka[0:r, :], kb_[0:r, :], ALU.add).then_inc(q["krope"], 1)

                if l == 1:
                    for i in range(VT):
                        rotate(0, i)
                pool.wait_ge(q["qc"] if l == 0 else q["qtc"], 4)
                pool.wait_ge(const_loaded, 32)
                spread(xqbd[0], qT, 0, C_HM4, q)

                def body(n, k, more):
                    if more:
                        after(pool, q["scores"], 8 * n)
                        spread(xqbd[k ^ 1], qT, n + 1, C_HM4, q)
                        if l == 1:
                            for i in range(VT):
                                rotate(n + 1, i)

                quads(pool, body)

            def selfattn(l, s):
                q = ss_[l]
                src, vsrc, col = ((qT, vall, C_HM16), (xnT, xn, C_HM4))[l]
                pool.wait_ge(x_ready, s)
                if l == 0:
                    own = Tally(q["z"])
                    for v in (vcT.rearrange("p c b w -> p (c b w)"), kcT.rearrange("p c b w -> p (c b w)")):
                        own.inc(G.memset(v, 0.0))
                    for v in pn:
                        own.inc(G.memset(v.rearrange("p g j w -> p (g j w)"), 0.0))
                    pool.wait_ge(q["z"], own.n)
                    G.memset(mark[:, :], 0.0).then_inc(q["zeroed"], 1)
                    pool.wait_ge(wa_loaded, 48)
                    G.tensor_tensor(bdw.rearrange("p a (h o) -> p a h o", o=HD),
                                    cw[:, :, :].unsqueeze(2).to_broadcast([P, KC * CF, 8, HD]),
                                    const[:, C_HM1:C_HM1 + 8].unsqueeze(1).unsqueeze(3).to_broadcast([P, KC * CF, 8, HD]),
                                    ALU.mult).then_inc(q["bdw"], 1)
                    pool.wait_ge(q["prc"], 4)
                else:
                    pool.wait_ge(ln_copied, 4 * 5)

                def body(n, k):
                    after(pool, q["sw"], n - 1)
                    spread(sqbd[k], src, n, col, q)
                    after(pool, q["pvw"], n - 1)
                    if l == 0 and isinstance(n, int) and n == 0:
                        pool.wait_ge(q["vtc"], 4)
                    G.tensor_copy(vq[k], vsrc.rearrange("p t d -> p (t d)")[:, bass.ds(n * D, D)]).then_inc(q["vq"], 1)

                for k in range(2):
                    body(k, k)
                with pool.Fori(1, NT // 2) as it:
                    for k in range(2):
                        body(2 * it + k, k)

            cross(0, 0)
            if stages > 1:
                selfattn(0, 1)
            if stages > 3:
                cross(1, 3)
            if stages > 4:
                selfattn(1, 4)


def kernel(**inputs):
    import concourse.bacc as _bacc
    from concourse.bass_utils import run_bass_kernel_spmd as _run

    a = {k: np.asarray(v) for k, v in inputs.items()}
    cols = lambda v: v.reshape(-1, KC, P).transpose(2, 0, 1).reshape(P, -1)
    rows = lambda v: np.broadcast_to(v.reshape(1, -1), (P, v.size))
    kv = lambda k, v: np.concatenate([k, v], 1)
    arrays = {
        "x": a["x"].reshape(TOK, D),
        "ctxT": a["ctx_1024"].reshape(B * S, D).T,
        "mask": a["mask_1x1xSxS2_fk1"].reshape(T, S),
        "const": shape_constants(),
        "vec": np.concatenate([cols(a[n]) for n in ("L0_xattn_bq", "L0_xattn_bk", "L0_xattn_bv", "L0_attn_conv_b",
                                                    "L0_attn_b_out", "L0_attn_null_k", "L0_attn_null_v")], 1),
        "bo": rows(a["L0_xattn_bo"]),
        "w0q": a["L0_xattn_Wq"], "w0kv": kv(a["L0_xattn_Wk"], a["L0_xattn_Wv"]), "w0o": a["L0_xattn_Wo"],
        "w1q": a["L1_xattn_Wq"].T, "w1kv": kv(a["L1_xattn_Wk"].T, a["L1_xattn_Wv"].T), "w1o": a["L1_xattn_Wo"].T,
        "wqkv": a["L0_attn_Wqkv"], "wout": a["L0_attn_W_out"],
        "conv": a["L0_attn_conv_w"].reshape(KC, 8, HD, HD, CF).transpose(1, 3, 0, 4, 2).reshape(P, KC * CF, HD),
        "normw": np.stack([rows(a["L1_xattn_q_norm_w"]), rows(a["L1_xattn_k_norm_w"])], 1),
        "rw0": a["L0_ffn_router_w"].T, "rw1": a["L1_ffn_w_gate"],
        "b1": a["L0_ffn_b1"].reshape(E_, H0 // P, P).transpose(2, 0, 1), "b2": a["L0_ffn_b2"],
        "w1a": a["L0_ffn_w1"].transpose(0, 2, 1), "w2a": a["L0_ffn_w2"].transpose(0, 2, 1),
        "w1b": a["L1_ffn_w1"], "w3b": a["L1_ffn_w3"], "w2b": a["L1_ffn_w2"],
    }
    nc = _bacc.Bacc("TRN2", target_bir_lowering=False, num_devices=1)
    named, io = {}, {}
    for name, v in arrays.items():
        v = np.ascontiguousarray(v)
        named[f"in_{name}_dram"] = v
        io[name] = nc.dram_tensor(f"in_{name}_dram", v.shape, mybir.dt.from_np(v.dtype), kind="ExternalInput").ap()
    out = nc.dram_tensor("out_0_dram", (TOK, D), F32, kind="ExternalOutput").ap()
    perceiver_block(nc, io, out, stages=STAGES)
    r = _run(nc, [named], core_ids=[0])
    return r.results[0]["out_0_dram"].reshape(B, T, D)
```

```python
from contextlib import ExitStack

import concourse.bass as bass
import numpy as np
from concourse import mybir

F32 = mybir.dt.float32
U32 = mybir.dt.uint32
I32 = mybir.dt.int32
ALU = mybir.AluOpType
ACT = mybir.ActivationFunctionType
AX_X = mybir.AxisListType.X

P = 128
B, T, D = 32, 32, 256
S = 257
NH, HD = 16, 16
STAGES = 6
KC = D // P
NT = B * T // P
QB = P // T
QS = QB * S
VT = -(-QS // P)
WIN = 3 * P
TOK = B * T
E_ = 8
H0, H1 = 1024, 512
TOPK = 2
EB = 4
NTILE = -(-((TOPK * TOK + E_ * (P - 1)) // P) // EB) * EB
CF = 4
NKEY = T // CF + 1
KRAW = 4
BATCH = 3
KW = 32
ROOT_STEPS = 12
MASK_VALUE = -3.0e38
GH = NH // 4

C_IDENT, C_STACK, C_BLK, C_HM1, C_HM4, C_HM16 = 0, 128, 160, 224, 232, 240
C_CS, C_BD, C_M0, C_M1, C_RQ, C_RK = 248, 1272, 1528, 1560, 1592, 1624
C_IOTA = C_RK + 32 * VT
C_TRI, C_ONES = C_IOTA + E_, C_IOTA + E_ + P
C_THR = C_ONES + P
C_TILE = C_THR + NT
NCONST = C_TILE + NTILE
V_BQ, V_BK, V_BV, V_CB, V_BO, V_NK, V_NV = 0, 2, 4, 6, 8, 10, 12
NVEC = 14


def shape_constants():
    c = np.zeros((P, NCONST), np.float32)
    p = np.arange(P)
    c[:, C_IDENT:C_IDENT + P] = np.eye(P)
    c[:, C_STACK:C_STACK + T] = (p[:, None] % T == np.arange(T)[None])
    c[:, C_BLK:C_BLK + 64] = (p[:, None] // T == np.arange(64)[None] // HD)
    same = (p[:, None] // HD == np.arange(8)[None])
    c[:, C_HM1:C_HM1 + 8] = same
    c[:, C_HM4:C_HM4 + 8] = same * HD ** -0.5
    c[:, C_HM16:C_HM16 + 8] = same * D ** -0.5
    d = np.arange(D)
    turn = (np.outer(d, d) % D) * (2 * np.pi / D)
    cs = np.concatenate([np.cos(turn), np.sin(turn)], 1).reshape(KC, P, 2 * D)
    c[:, C_CS:C_CS + KC * 2 * D] = cs.transpose(1, 0, 2).reshape(P, -1)
    turn = (np.outer(p % T, p % T) % T) * (2 * np.pi / T)
    mine = (p[:, None] // T == p[None] // T)
    c[:, C_BD:C_BD + P] = np.cos(turn) * mine
    c[:, C_BD + P:C_BD + 2 * P] = -np.sin(turn) * mine
    q = (p % T)[:, None]
    j = np.arange(KW)[None]
    c[:, C_M0:C_M0 + KW] = np.where((j >= 1) & (j < NKEY) & (q < CF * (j - 1) + CF - 1), MASK_VALUE, 0.0)
    c[:, C_M1:C_M1 + KW] = np.where(j > q, MASK_VALUE, 0.0)

    def rope(pos, theta):
        freqs = np.float32(theta) ** (-np.arange(0, HD, 2, dtype=np.float32) / np.float32(HD))
        ang = pos.astype(np.float32)[:, None] * freqs[None]
        return np.concatenate([np.cos(ang), np.cos(ang), -np.sin(ang), np.sin(ang)], 1) * HD ** 0.5

    c[:, C_RQ:C_RQ + 32] = rope(p % T, 32.0)
    for m in range(VT):
        c[:, C_RK + 32 * m:C_RK + 32 * m + 32] = rope((P * m + p) % S, 1000.0)
    c[:, C_IOTA:C_IOTA + E_] = np.arange(E_)[None]
    c[:, C_TRI:C_TRI + P] = p[:, None] < p[None]
    c[:, C_ONES:C_ONES + P] = 1.0
    c[:, C_THR:C_THR + NT] = P * np.arange(NT)[None]
    c[:, C_TILE:C_TILE + NTILE] = np.arange(NTILE)[None]
    return c


class Tally:

    def __init__(self, sem):
        self.sem, self.n = sem, 0

    def inc(self, ins):
        ins.then_inc(self.sem, 1)
        self.n += 1
        return self.n


class Signals(dict):

    def __init__(self, make, stage):
        super().__init__()
        self.make, self.stage = make, stage

    def __missing__(self, name):
        self[name] = self.make(self.stage + name)
        return self[name]


def perceiver_block(nc, io, out, stages=6):
    ctx = ExitStack()
    with ctx:
        def sb(name, shape, dt=F32):
            return ctx.enter_context(nc.sbuf_tensor(name, shape, dt))

        def sem(name):
            return ctx.enter_context(nc.semaphore(name))

        bank = [ctx.enter_context(nc.psum_tensor(f"bank{i}", [P, 512], F32)) for i in range(8)]

        const = sb("const", [P, NCONST])
        vec = sb("vec", [P, NVEC])
        ident = const[:, C_IDENT:C_IDENT + P]
        stack = const[:, C_STACK:C_STACK + T]
        blk = const[:, C_BLK:C_BLK + 64]
        x = sb("x", [P, NT, D])
        xn = sb("xn", [P, NT, D])
        xnT = sb("xnT", [P, KC, TOK])
        qT = sb("qT", [P, KC, TOK])
        outT = sb("outT", [P, KC, TOK])
        ln_stats = sb("ln_stats", [P, NT, 6])
        ln_mv = sb("ln_mv", [P, NT, 2])
        ln_ve = sb("ln_ve", [P, NT])
        ln_sd = sb("ln_sd", [P, NT])
        ln_rs = sb("ln_rs", [P, NT])

        wq = [sb(f"wq{l}", [P, KC, D]) for l in range(2)]
        wkv = [sb(f"wkv{l}", [P, KC, 2 * D]) for l in range(2)]
        wo = [sb(f"wo{l}", [P, KC, D]) for l in range(2)]
        bo_bc = sb("bo_bc", [P, D])
        negmask = sb("negmask", [P, S])
        wqkv = sb("wqkv", [P, KC, 3 * D])
        wout = sb("wout", [P, KC, D])
        cw = sb("cw", [P, KC * CF, HD])
        normw = sb("normw", [P, 2, HD])
        ropew = sb("ropew", [P, 2 * HD * (1 + VT)])

        arena = sb("arena", [P, 26000])

        class Arena:
            def __init__(self):
                self.at = 0

            def take(self, *shape):
                n = int(np.prod(shape))
                v = arena[:, self.at:self.at + n]
                self.at += n
                assert self.at <= 26000, self.at
                if len(shape) == 1:
                    return v
                names = "abcd"[:len(shape)]
                return v.rearrange(f"p ({' '.join(names)}) -> p {' '.join(names)}",
                                   **{m: s for m, s in zip(names, shape)})

        const_loaded = sem("const_loaded")
        x_loaded = sem("x_loaded")
        wx_loaded = [sem(f"wx{l}_loaded") for l in range(2)]
        mask_loaded = sem("mask_loaded")
        wa_loaded = sem("wa_loaded")
        normw_loaded = sem("normw_loaded")
        x_ready = sem("x_ready")
        ln_own = sem("ln_own")
        ln_var = sem("ln_var")
        ln_std = sem("ln_std")
        ln_norm = sem("ln_norm")
        ln_turned = sem("ln_turned")
        ln_copied = sem("ln_copied")
        out_stored = sem("out_stored")

        zeroed = sem("zeroed")
        blank = sem("blank")
        gathered = [sem(f"gathered{h}") for h in range(2)]
        weights_in = sem("router_loaded")
        scattered = sem("scattered")
        gate_exp = sem("gate_exp")
        pool_own = sem("pool_own")
        routed = sem("routed")
        ranked = sem("ranked")
        ROUTED = [{m: i + 1 for i, m in enumerate(("less_max", "hot", "gate", "slots", "tiles"))},
                  {m: i + 6 for i, m in enumerate(("less_max", "hot", "slots", "tiles"))}]
        RANKED = [{"logits": 1, "ranks": 2, "gates": 3}, {"logits": 4, "ranks": 5}]
        xs = [Signals(sem, f"cross{l}_") for l in range(2)]
        ss_ = [Signals(sem, f"self{l}_") for l in range(2)]
        ms = [Signals(sem, f"experts{l}_") for l in range(2)]

        ar = Arena()
        ctxb = [ar.take(KC, QS) for _ in range(2)]
        ktb = [ar.take(KC, QS) for _ in range(2)]
        vb = [ar.take(VT, D) for _ in range(2)]
        xqbd = [ar.take(KC, QB, 8, T) for _ in range(2)]
        smask = [ar.take(2, S) for _ in range(2)]
        pwin = [[ar.take(2, WIN) for _ in range(2)] for _ in range(QB)]
        pTb = [ar.take(2, WIN) for _ in range(2)]
        omb = [ar.take(P) for _ in range(2)]
        xsmall = ar.take(64)
        negmax = [xsmall[:, 2 * i:2 * i + 2] for i in range(2)]
        rowsum = [xsmall[:, 4 + 2 * i:6 + 2 * i] for i in range(2)]
        rcp = [xsmall[:, 8 + 2 * i:10 + 2 * i] for i in range(2)]
        xarena_end = ar.at
        kraw = sb("kraw", [P, KRAW, D])
        ksq = sb("ksq", [P, 3, D])
        kn = sb("kn", [P, 3, D])
        ka = sb("ka", [P, D])
        kb_ = sb("kb", [P, D])
        krope = sb("krope", [P, 3, D])
        kss = sb("kss", [P, VT, NH])
        root_v = sb("root_v", [P, NT * NH])
        root_t = sb("root_t", [P, NT * NH])
        root_y = sb("root_y", [P, NT * NH], I32)
        kr = sb("kr", [P, VT, NH])
        qss = root_t
        qr = sb("qr", [P, NT * NH])

        rope_q = ropew[:, 0:32]

        def rope_k(m):
            return ropew[:, 32 + 32 * m:64 + 32 * m]

        def parts(l):
            if l == 0:
                order = [("K", i) for i in range(8)] + [("V", i) for i in range(VT)]
                cut = [2, 2, 2, 2, 2, 2, 2, 3]
            else:
                order = [("A", 0), ("A", 1), ("A", 2), ("A", 3), ("A", 4), ("T", 0), ("A", 5), ("T", 1), ("A", 6),
                         ("T", 2), ("A", 7), ("A", 8), ("T", 3), ("T", 4), ("T", 5), ("T", 6), ("T", 7), ("T", 8)]
                cut = [3, 2, 3, 3, 3, 1, 3, 0]
            steps, at = [], 0
            for n in cut:
                steps.append([(at + i, *order[at + i]) for i in range(n)])
                at += n
            assert at == len(order)
            return steps, len(order), {o: i for i, o in enumerate(order)}

        ar = Arena()
        kT = ar.take(KC, TOK)
        vT = ar.take(KC, TOK)
        kcT = ar.take(KC, B, KW)
        vcT = ar.take(KC, B, KW)
        bdw = ar.take(KC * CF, P)
        vall = ar.take(NT, D)
        sqbd = [ar.take(KC, QB, 8, T) for _ in range(2)]
        vq = [ar.take(D) for _ in range(2)]
        sprob = [ar.take(NH, KW) for _ in range(2)]
        pn = [ar.take(GH, QB, KW) for _ in range(2)]
        spT = [ar.take(GH, P) for _ in range(2)]
        som = ar.take(QB, D)
        zT = kT
        af = [vT[:, i, 0:2 * D] for i in range(2)]
        rowmax = sb("rowmax", [P, 2])
        spare = sb("spare", [1, 1])
        mark = sb("mark", [1, 1])
        smx = sb("smx", [P, NH])
        ssum = sb("ssum", [P, NH])
        srcp = sb("srcp", [P, NH])

        ar = Arena()
        HC = (H0 // P, H1 // P)
        EW = (KC * H0 + H0 // P * D, 2 * KC * H1 + H1 // P * D)
        ew = [ar.take(max(EW)) for _ in range(EB)]
        eb1 = [ar.take(H0 // P) for _ in range(EB)]
        eh = [ar.take(H0 // P, P) for _ in range(2)]
        esilu = [ar.take(H1) for _ in range(2)]
        exs = [ar.take(D) for _ in range(EB)]
        exT = [ar.take(KC, P) for _ in range(2)]
        eys = [ar.take(D) for _ in range(2)]
        eyg = [[ar.take(D) for _ in range(TOPK)] for _ in range(NT)]
        zero = sb("zero", [P, D])
        onehot = [sb(f"onehot{i}", [P, NT, E_]) for i in range(TOPK)]
        chosen = sb("chosen", [P, NT * E_])
        seen = [sb(f"seen{i}", [P, 2 * NT, E_]) for i in range(4)]
        used = [sb(f"used{i}", [P, 2 * E_]) for i in range(4)]
        more_than = sb("more_than", [P, E_, NT])
        place_ = sb("place", [P, NT, E_])
        picked = sb("picked", [P, NT, E_])
        slotf = sb("slotf", [P, TOPK, NT])
        slot = sb("slot", [P, TOPK, NT], U32)
        ends = sb("ends", [P, NTILE, E_])
        tilef = sb("tilef", [P, NTILE])
        tile_expert = sb("tile_expert", [P, NTILE], I32)
        xslot = [nc.dram_tensor(f"xslot{l}", [NTILE * P, D], F32, kind="Internal").ap() for l in range(2)]
        yslot = [nc.dram_tensor(f"yslot{l}", [NTILE * P, D], F32, kind="Internal").ap() for l in range(2)]
        rw0 = sb("rw0", [P, KC, E_])
        rw1 = sb("rw1", [P, KC, E_])
        b2sb = sb("b2sb", [E_, D])
        lg = sb("lg", [P, NT, E_])
        pr = sb("pr", [P, NT, E_])
        top = sb("top", [P, NT, 8])
        topi = sb("topi", [P, NT, 8], U32)
        topf = sb("topf", [P, NT, 8])
        gsm = sb("gsm", [P, 4, NT])
        gate = sb("gate", [P, NT, E_])
        gateT = qT[0:E_, 0, :]

        block = ctx.enter_context(nc.Block())

        def slot_plan(items):
            return items[0:1], items[1:2], items[2:]

        @block.sync
        def _(sp):
            sp.dma_start(x[:, :, :], io["x"].rearrange("(t p) d -> p t d", p=P)).then_inc(x_loaded, 16)
            sp.dma_start(const[:, :], io["const"]).then_inc(const_loaded, 16)
            sp.dma_start(vec[:, :], io["vec"]).then_inc(const_loaded, 16)

            def cross_weights(l):
                for dst, src in ((wq[l], "q"), (wkv[l], "kv"), (wo[l], "o")):
                    sp.dma_start(dst[:, :, :], io[f"w{l}{src}"].rearrange("(c p) n -> p c n", p=P)).then_inc(wx_loaded[l], 16)

            cross_weights(0)

            def load_ctx(l, k, n):
                sp.dma_start(ctxb[k], io["ctxT"].rearrange("(c p) n -> p c n", p=P)[:, :, bass.ds(n * QS, QS)])\
                  .then_inc(xs[l][f"ctx{k}"], 16)

            def cross_loads(l):
                load_ctx(l, 0, 0)
                load_ctx(l, 1, 1)
                if l == 0:
                    for h in range(QB):
                        sp.dma_start(negmask[T * h:T * h + T, :], io["mask"]).then_inc(mask_loaded, 16)
                    sp.dma_start(bo_bc[:, :], io["bo"]).then_inc(mask_loaded, 16)
                    sp.dma_start(wqkv[:, :, :], io["wqkv"].rearrange("(c p) n -> p c n", p=P)).then_inc(wa_loaded, 16)
                    sp.dma_start(wout[:, :, :], io["wout"].rearrange("(c p) n -> p c n", p=P)).then_inc(wa_loaded, 16)
                    sp.dma_start(cw[:, :, :], io["conv"]).then_inc(wa_loaded, 16)
                    cross_weights(1)
                    sp.dma_start(normw[:, :, :], io["normw"]).then_inc(normw_loaded, 16)
                nit = parts(l)[1]
                with sp.Fori(1, NT // 2) as it:
                    for k in range(2):
                        sp.wait_ge(xs[l]["kvw"], (2 * it + k - 1) * nit)
                        load_ctx(l, k, 2 * it + k)

            def expert_traffic(l):
                q = ms[l]

                def weights(m, k):
                    e = sp.value_load(tile_expert[0:1, bass.ds(m, 1)], min_val=0, max_val=E_ - 1)
                    sp.dma_start(ew[k][:, 0:EW[l]], io[f"ew{l}"][:, bass.ds(e * EW[l], EW[l])]).then_inc(q[f"w{k}"], 16)
                    if l == 0:
                        sp.dma_start(eb1[k], io["b1"][:, bass.ds(e * (H0 // P), H0 // P)]).then_inc(q[f"w{k}"], 16)

                def tokens(m, k):
                    sp.dma_start(exs[k], xslot[l][bass.ds(m * P, P), :]).then_inc(q[f"xs{k}"], 16)

                def store(m, k):
                    sp.wait_ge(q["dnc"], m + 1)
                    sp.dma_start(yslot[l][bass.ds(m * P, P), :], eys[k % 2]).then_inc(q[f"ys{k % 2}"], 16)

                sp.wait_ge(routed, ROUTED[l]["tiles"])
                for k in range(EB):
                    weights(k, k)
                sp.wait_ge(scattered, 16 * TOPK * NT * (l + 1))
                for k in range(EB):
                    tokens(k, k)
                with sp.Fori(0, NTILE // EB - 1) as it:
                    for k in range(EB):
                        m = EB * it + k
                        sp.wait_ge(q["xst"], m + 1)
                        tokens(m + EB, k)
                        sp.wait_ge(q["dnw"], m + 1)
                        weights(m + EB, k)
                        store(m, k)
                for m in range(NTILE - EB, NTILE):
                    store(m, m % EB)

            cross_loads(0)
            if stages > 2:
                sp.dma_start(rw0[:, :, :], io["rw0"].rearrange("(c p) n -> p c n", p=P)).then_inc(weights_in, 16)
                sp.dma_start(b2sb[:, :], io["b2"]).then_inc(weights_in, 16)
                sp.dma_start(rw1[:, :, :], io["rw1"].rearrange("(c p) n -> p c n", p=P)).then_inc(weights_in, 16)
                sp.wait_ge(blank, 1)
                for l in range(2):
                    sp.dma_start(xslot[l].rearrange("(t p) d -> p t d", p=P),
                                 zero[:, :].unsqueeze(1).to_broadcast([P, NTILE, D])).then_inc(zeroed, 16)
                expert_traffic(0)
            if stages > 3:
                sp.wait_ge(x_ready, 3)
                cross_loads(1)
            if stages > 5:
                expert_traffic(1)
            sp.wait_ge(x_ready, stages)
            sp.dma_start(out.rearrange("(t p) d -> p t d", p=P), x[:, :, :]).then_inc(out_stored, 16)
            sp.wait_ge(out_stored, 16)

        def after(eng, sem, value):
            if not isinstance(value, int) or value > 0:
                eng.wait_ge(sem, value)

        def before(n, k, u, back):
            u -= back
            if u < 0:
                n, k, u = n - 1, k ^ 1, u + 8
            return None if isinstance(n, int) and n < 0 else (n, k, u)

        def quads(eng, body):
            for k in range(2):
                body(k, k, True)
            with eng.Fori(1, NT // 2 - 1) as it:
                for k in range(2):
                    body(2 * it + k, k, True)
            for k in range(2):
                body(NT - 2 + k, k, k == 0)

        def tiles(eng, body):
            for k in range(EB):
                body(k, k, 0, 2)
            with eng.Fori(1, NTILE // EB - 1) as it:
                for k in range(EB):
                    body(EB * it + k, k, it, 2)
            for k in range(EB):
                body(NTILE - EB + k, k, NTILE // EB - 1, min(2, EB - 1 - k))

        @block.tensor
        def _(pe):
            mm = nc.tensor.matmul

            def turn_xn(s):
                if s == 0:
                    pe.wait_ge(const_loaded, 32)
                for b in range(4):
                    pe.wait_ge(ln_norm, 8 * s + 2 * b + 2)
                    for t in range(2):
                        for c in range(KC):
                            ins = nc.tensor.transpose(bank[b][:, (2 * t + c) * P:(2 * t + c + 1) * P],
                                                      xn[:, 2 * b + t, c * P:c * P + P], ident)
                    ins.then_inc(ln_turned, 1)

            def cross(l):
                q = xs[l]
                steps, nit, place = parts(l)

                def item(n, k, idx, kind, i, pair):
                    after(pe, q["kvc"], n * nit + idx)
                    if idx == 0:
                        pe.wait_ge(q[f"ctx{k}"], 16 * (pair + 1))
                    r = min(P, QS - P * i) if kind != "K" else P
                    if kind == "T":
                        pe.wait_ge(q["krope"], VT * n + i + 1)
                        for c in range(KC):
                            ins = nc.tensor.transpose(bank[7][:, c * P:c * P + P], krope[:, i % 3, c * P:c * P + P], ident)
                    else:
                        for c in range(KC):
                            if kind == "K":
                                j, m = divmod(i, 2)
                                o, a, b = bank[7][:, 0:S], wkv[l][:, c, m * P:m * P + P], ctxb[k][:, c, j * S:j * S + S]
                            elif kind == "V":
                                o, a, b = bank[7][0:r, 0:D], ctxb[k][:, c, P * i:P * i + r], wkv[l][:, c, D:2 * D]
                            else:
                                o, a, b = bank[7][0:r, :], ctxb[k][:, c, P * i:P * i + r], wkv[l][:, c, :]
                            ins = mm(o, a, b, start=(c == 0), stop=(c == KC - 1))
                    ins.then_inc(q["kvw"], 1)

                def scores(n, k, u):
                    j, c = divmod(u, 2)
                    if u == 0:
                        pe.wait_ge(q["kvc"], n * nit + (8 if l == 0 else nit))
                    if u < 2:
                        pe.wait_ge(q["qbd"], 2 * n + u + 1)
                    after(pe, q["masked" if l == 0 else "probs"], 8 * n + u - 1)
                    for g in range(2):
                        ins = mm(bank[2 * (u % 2) + g][:, 0:S], xqbd[k][:, c, j, 4 * g:4 * g + 4, :],
                                 ktb[k][:, c, j * S:j * S + S], start=True, stop=True)
                    ins.then_inc(q["scores"], 1)

                def turns(n, k, u):
                    j, c = divmod(u, 2)
                    pe.wait_ge(q["probs"], 8 * n + u + 1)
                    after(pe, q["pta"], 8 * n + u)
                    after(pe, q["ptd"], 8 * n + u)
                    for g in range(2):
                        for w in range(3):
                            ins = nc.tensor.transpose(bank[4 + g][:, w * P:w * P + P],
                                                      pwin[j][c][:, g, w * P:w * P + P], ident)
                    ins.then_inc(q["ptw"], 1)

                def collapse(n, k, u):
                    pe.wait_ge(q["normed"], 8 * n + u + 1)
                    mm(bank[6][:, 256:256 + T], omb[u % 2], stack, start=True, stop=True).then_inc(q["colw"], 1)

                def weigh(n, k, u):
                    j, c = divmod(u, 2)
                    if u == 0:
                        pe.wait_ge(q["kvc"], (n + 1) * nit)
                    pe.wait_ge(q["pta"], 8 * n + u + 1)
                    pe.wait_ge(q["ptd"], 8 * n + u + 1)
                    after(pe, q["colc"], 8 * n + u)
                    for g in range(2):
                        for w in range(3):
                            r = P if w < 2 else j + 1
                            ins = mm(bank[6][:, 64 * g:64 * g + 64], pTb[u % 2][0:r, g, w * P:w * P + P],
                                     vb[k][0:r, 2 * j + w, 64 * (2 * c + g):64 * (2 * c + g) + 64],
                                     start=(w == 0), stop=(w == 2))
                    ins.then_inc(q["pvw"], 1)

                pe.wait_ge(wx_loaded[l], 48)
                if l == 0:
                    for i in range(4):
                        m, h = divmod(i, 2)
                        pe.wait_ge(ln_copied, 4 * 0 + 2 * h + 2)
                        after(pe, q["qc"], i - 1)
                        for c in range(KC):
                            ins = mm(bank[4 + i % 2][:, :], wq[0][:, c, m * P:m * P + P], xnT[:, c, h * 512:h * 512 + 512],
                                     start=(c == 0), stop=(c == KC - 1))
                        ins.then_inc(q["qw"], 1)
                else:
                    for t in range(NT):
                        pe.wait_ge(ln_copied, 4 * 3 + t // 2 + 1)
                        after(pe, q["qc"], t - 1)
                        for c in range(KC):
                            ins = mm(bank[4 + t % 2][:, 0:D], xnT[:, c, t * P:t * P + P], wq[1][:, c, :],
                                     start=(c == 0), stop=(c == KC - 1))
                        ins.then_inc(q["qw"], 1)
                for st in steps:
                    for it_ in st:
                        item(0, 0, *it_, 0)
                if l == 1:
                    pe.wait_ge(q["qrope"], 1)
                    for b in range(4):
                        for t in range(2):
                            for c in range(KC):
                                ins = nc.tensor.transpose(bank[b][:, (2 * t + c) * P:(2 * t + c + 1) * P],
                                                          xn[:, 2 * b + t, c * P:c * P + P], ident)
                        ins.then_inc(q["qtw"], 1)
                scores(0, 0, 0)

                def body(n, k, more):
                    for u in range(8):
                        if u < 7:
                            scores(n, k, u + 1)
                        elif more:
                            scores(n + 1, k ^ 1, 0)
                        a, b, c = slot_plan(steps[u] if more else [])
                        pair = (n - k) // 2 if isinstance(n, int) else body.it
                        nxt = [(n + 1, k ^ 1), pair + k]
                        for it_ in a:
                            item(*nxt[0], *it_, nxt[1])
                        turns(n, k, u)
                        past = before(n, k, u, 2)
                        if past:
                            collapse(*past)
                        for it_ in b:
                            item(*nxt[0], *it_, nxt[1])
                        past = before(n, k, u, 1)
                        if past:
                            weigh(*past)
                        for it_ in c:
                            item(*nxt[0], *it_, nxt[1])

                for k in range(2):
                    body(k, k, True)
                with pe.Fori(1, NT // 2 - 1) as it:
                    body.it = it
                    for k in range(2):
                        body(2 * it + k, k, True)
                for k in range(2):
                    body(NT - 2 + k, k, k == 0)
                collapse(NT - 1, 1, 6)
                weigh(NT - 1, 1, 7)
                collapse(NT - 1, 1, 7)
                pe.wait_ge(q["colc"], 8 * NT)
                for t in range(NT):
                    for c in range(KC):
                        ins = mm(bank[t][:, 0:D], outT[:, c, t * P:t * P + P], wo[l][:, c, :],
                                 start=(c == 0), stop=(c == KC - 1))
                    ins.then_inc(q["postw"], 1)

            def selfattn(l):
                q = ss_[l]
                w = NKEY if l == 0 else T
                src = kcT if l == 0 else None
                if l == 0:
                    pe.wait_ge(wa_loaded, 48)
                    for i in range(12):
                        m, h = divmod(i, 2)
                        pe.wait_ge(ln_copied, 4 + 2 * h + 2)
                        after(pe, q["prc"], i - 1)
                        for c in range(KC):
                            ins = mm(bank[4 + i % 2][:, :], wqkv[:, c, m * P:m * P + P], xnT[:, c, h * 512:h * 512 + 512],
                                     start=(c == 0), stop=(c == KC - 1))
                        ins.then_inc(q["prw"], 1)
                    pe.wait_ge(q["bdw"], 1)
                    pe.wait_ge(q["prc"], 12)
                    for i in range(4):
                        kind, c = divmod(i, 2)
                        zsrc = (kT, vT)[kind]
                        for f in range(CF):
                            ins = mm(bank[6 + i % 2][:, (i // 2) * 256:(i // 2) * 256 + 256], bdw[:, c * CF + f, :],
                                     zsrc[:, c, f:TOK:CF], start=(f == 0), stop=(f == CF - 1))
                        ins.then_inc(q["cvw"], 1)
                        if i == 1:
                            pe.wait_ge(q["cvc"], 2)
                    pe.wait_ge(q["cvc"], 4)
                    pe.wait_ge(q["null"], 4)
                    for b in range(4):
                        for t in range(2):
                            for c in range(KC):
                                ins = nc.tensor.transpose(bank[b][:, (2 * t + c) * P:(2 * t + c + 1) * P],
                                                          vcT[:, c, 4 * (2 * b + t):4 * (2 * b + t) + 4, :], ident)
                        ins.then_inc(q["vtw"], 1)
                    pe.wait_ge(q["vtc"], 4)
                else:
                    pe.wait_ge(ln_copied, 4 * 5)

                def scores(n, k):
                    pe.wait_ge(q["qbd"], n + 1)
                    pe.wait_ge(q["qbd1"], n + 1)
                    after(pe, q["sub"], n - 1)
                    for j in range(QB):
                        for g in range(GH):
                            if l == 0:
                                keys = kcT.rearrange("p c b w -> p c (b w)")[:, g // 2, bass.ds(n * P + KW * j, w)]
                            else:
                                keys = xnT[:, g // 2, bass.ds(n * P + T * j, w)]
                            at = (4 * j + g) * KW
                            ins = mm(bank[k][:, at:at + w], sqbd[k][:, g // 2, j, 4 * (g % 2):4 * (g % 2) + 4, :], keys,
                                     start=True, stop=True)
                    ins.then_inc(q["sw"], 1)

                def rest(n, k):
                    pe.wait_ge(q["pn"], n + 1)
                    after(pe, q["colc"], n - 1)
                    for g in range(GH):
                        ins = nc.tensor.transpose(bank[2 + k][:, g * P:g * P + P], pn[k][:, g, :, :], ident)
                    ins.then_inc(q["ptw"], 1)
                    pe.wait_ge(q["ptc"], n + 1)
                    pe.wait_ge(q["vq"], n + 1)
                    after(pe, q["om"], n)
                    for j in range(QB):
                        for g in range(GH):
                            ins = mm(bank[4 + j][:, 64 * g:64 * g + 64], spT[k][T * j:T * j + w, g, :],
                                     vq[k][T * j:T * j + w, 64 * g:64 * g + 64], start=True, stop=True)
                    ins.then_inc(q["pvw"], 1)
                    pe.wait_ge(q["om"], n + 1)
                    if l == 0:
                        for j in range(QB):
                            for c in range(KC):
                                ins = mm(bank[2 + k][:, c * P + T * j:c * P + T * j + T], som[:, j, c * P:c * P + P], stack,
                                         start=True, stop=True)
                    else:
                        for j in range(QB):
                            ins = mm(bank[2 + k][T * j:T * j + T, 0:D], stack, som[:, j, :], start=True, stop=True)
                    ins.then_inc(q["colw"], 1)

                def body(n, k, more):
                    if more:
                        scores(n + 1, k ^ 1)
                    rest(n, k)

                scores(0, 0)
                quads(pe, body)
                if l == 0:
                    pe.wait_ge(q["colc"], NT)
                    for i in range(4):
                        m, h = divmod(i, 2)
                        for c in range(KC):
                            ins = mm(bank[i][:, :], wout[:, c, m * P:m * P + P], outT[:, c, h * 512:h * 512 + 512],
                                     start=(c == 0), stop=(c == KC - 1))
                        ins.then_inc(q["zw"], 1)
                    pe.wait_ge(q["zc"], 4)

                    def along_channels(t):
                        after(pe, q["ac"], t - 1)
                        for c in range(KC):
                            ins = mm(bank[4 + t % 2][:, :], zT[:, c, t * P:t * P + P],
                                     const[:, C_CS + c * 2 * D:C_CS + (c + 1) * 2 * D], start=(c == 0), stop=(c == KC - 1))
                        ins.then_inc(q["aw"], 1)

                    def along_tokens(t):
                        pe.wait_ge(q["ac"], t + 1)
                        after(pe, q["yc"], t - 1)
                        for c in range(2):
                            ins = mm(bank[6 + t % 2][:, 0:D], const[:, C_BD + c * P:C_BD + c * P + P],
                                     af[t % 2][:, c * D:c * D + D], start=(c == 0), stop=(c == 1))
                        ins.then_inc(q["yw"], 1)

                    along_channels(0)
                    for t in range(NT):
                        if t + 1 < NT:
                            along_channels(t + 1)
                        along_tokens(t)

            def experts(l, s):
                q = ms[l]
                nh = HC[l]
                rw = (rw0, rw1)[l]
                pe.wait_ge(ln_copied, 4 * (s + 1))
                pe.wait_ge(weights_in, 48)
                for t in range(NT):
                    for c in range(KC):
                        ins = mm(bank[7][:, t * E_:t * E_ + E_], xnT[:, c, t * P:t * P + P], rw[:, c, :],
                                 start=(c == 0), stop=(c == KC - 1))
                ins.then_inc(ranked, 1)
                pe.wait_ge(routed, ROUTED[l]["hot"])
                mm(bank[6][:, 0:NT * E_], const[:, C_TRI:C_TRI + P], chosen[:, :], start=True, stop=True)
                mm(bank[6][:, P:P + NT * E_], const[:, C_ONES:C_ONES + P], chosen[:, :], start=True, stop=True)\
                    .then_inc(ranked, 1)
                if l == 0:
                    pe.wait_ge(routed, ROUTED[l]["gate"])
                    for t in range(NT):
                        ins = nc.tensor.transpose(bank[4 + t // 4][0:E_, (t % 4) * P:(t % 4) * P + P], gate[:, t, :], ident)
                    ins.then_inc(ranked, 1)
                    pe.wait_ge(q["cwtc"], 2)
                    for t in range(NT):
                        after(pe, q["cwbc"], t - 1)
                        mm(bank[4 + t % 2][:, 0:D], gateT[:, t * P:t * P + P], b2sb[:, :], start=True, stop=True)\
                            .then_inc(q["cwb"], 1)
                    pe.wait_ge(q["cwbc"], NT)

                def turn(m, k, it):
                    pe.wait_ge(q[f"xs{k}"], 16 * (it + 1))
                    after(pe, q["xsc"], m)
                    for c in range(KC):
                        ins = nc.tensor.transpose(bank[0][:, c * P:c * P + P], exs[k][:, c * P:c * P + P], ident)
                    ins.then_inc(q["xst"], 1)

                def raise_(m, k, it):
                    pe.wait_ge(q["xsc"], m + 1)
                    pe.wait_ge(q[f"w{k}"], (32 if l == 0 else 16) * (it + 1))
                    for half in range(2):
                        if l == 0:
                            after(pe, q["upc"], 2 * m + half - 1)
                        else:
                            after(pe, q["silu" if half == 0 else "upc"], m)
                        for i in range(4):
                            for c in range(KC):
                                at = c * H0 + (4 * half + i) * P if l == 0 else half * KC * H1 + c * H1 + i * P
                                ins = mm(bank[1 + half][:, i * P:i * P + P], ew[k][:, at:at + P], exT[k % 2][:, c, :],
                                         start=(c == 0), stop=(c == KC - 1))
                        ins.then_inc(q["upw"], 1)

                def lower(m, k):
                    pe.wait_ge(q["upc"], (2 if l == 0 else 1) * (m + 1))
                    after(pe, q["dnc"], m - 1)
                    for i in range(nh):
                        at = EW[l] - nh * D + i * D
                        ins = mm(bank[4 + k % 2][:, 0:D], eh[k % 2][:, i, :], ew[k][:, at:at + D], start=(i == 0), stop=(i == nh - 1))
                    ins.then_inc(q["dnw"], 1)

                def ahead(by, m, k, it):
                    return m + by, (k + by) % EB, it + (k + by) // EB

                def body(m, k, it, more=2):
                    if more > 0:
                        raise_(*ahead(1, m, k, it))
                    if more > 1:
                        turn(*ahead(2, m, k, it))
                    lower(m, k)

                turn(0, 0, 0)
                raise_(0, 0, 0)
                turn(1, 1, 0)
                tiles(pe, body)

            turn_xn(0)
            cross(0)
            if stages > 1:
                turn_xn(1)
                selfattn(0)
            if stages > 2:
                turn_xn(2)
                experts(0, 2)
            if stages > 3:
                turn_xn(3)
                cross(1)
            if stages > 4:
                turn_xn(4)
                selfattn(1)
            if stages > 5:
                turn_xn(5)
                experts(1, 5)

        @block.scalar
        def _(act):
            copy = ACT.Copy
            A = nc.scalar.activation

            def ln_root(s):
                act.wait_ge(ln_var, s + 1)
                A(ln_sd[:, :], ln_ve[:, :], ACT.Sqrt).then_inc(ln_std, 1)

            def ln_copy(s):
                for b in range(4):
                    act.wait_ge(ln_turned, 4 * s + b + 1)
                    A(xnT[:, :, 256 * b:256 * b + 256].rearrange("p c (t q) -> p t c q", t=2),
                      bank[b][:, :].rearrange("p (t c q) -> p t c q", t=2, c=KC), copy).then_inc(ln_copied, 1)

            def cross(l):
                q = xs[l]
                steps, nit, place = parts(l)

                def item(n, k, idx, kind, i):
                    act.wait_ge(q["kvw"], n * nit + idx + 1)
                    r = min(P, QS - P * i)
                    if kind == "K":
                        j, m = divmod(i, 2)
                        ins = A(ktb[k][:, m, j * S:j * S + S], bank[7][:, 0:S], ACT.Identity, bias=vec[:, V_BK + m:V_BK + m + 1])
                    elif kind == "V":
                        ins = A(vb[k][0:r, i, :], bank[7][0:r, 0:D], copy)
                    elif kind == "A":
                        after(act, q["ss"], VT * n + i - 2)
                        after(act, q["kw"], VT * n + (i - KRAW + 1 if i else 0))
                        A(ksq[0:r, i % 3, :], bank[7][0:r, 0:D], ACT.Square).then_inc(q["sq"], 1)
                        A(kraw[0:r, i % KRAW, :], bank[7][0:r, 0:D], copy)
                        ins = A(vb[k][0:r, i, :], bank[7][0:r, D:2 * D], copy)
                    else:
                        ins = A(ktb[k][:, :, P * i:P * i + r],
                                bank[7][:, 0:2 * P].rearrange("p (c r) -> p c r", c=KC)[:, :, 0:r], copy)
                    ins.then_inc(q["kvc"], 1)

                def exps(n, k, u):
                    j, c = divmod(u, 2)
                    act.wait_ge(q["negmax"], 8 * n + u + 1)
                    after(act, q["recip"], 8 * n + u - 1)
                    for g in range(2):
                        src = smask[u % 2][:, g, :] if l == 0 else bank[2 * (u % 2) + g][:, 0:S]
                        ins = A(pwin[j][c][:, g, j:j + S], src, ACT.Exp, bias=negmax[u % 2][:, g:g + 1],
                                accum_out=rowsum[u % 2][:, g:g + 1])
                    ins.then_inc(q["probs"], 1)

                def turned(n, k, u):
                    act.wait_ge(q["ptw"], 8 * n + u + 1)
                    A(pTb[u % 2][:, 0, :], bank[4][:, 0:WIN], copy).then_inc(q["pta"], 1)

                if l == 0:
                    for i in range(4):
                        m, h = divmod(i, 2)
                        act.wait_ge(q["qw"], i + 1)
                        A(qT[:, m, h * 512:h * 512 + 512], bank[4 + i % 2][:, :], ACT.Identity,
                          bias=vec[:, V_BQ + m:V_BQ + m + 1]).then_inc(q["qc"], 1)
                else:
                    qsq = outT.rearrange("p c n -> p (c n)").rearrange("p (t d) -> p t d", t=NT)
                    for t in range(NT):
                        act.wait_ge(q["qw"], t + 1)
                        A(qsq[:, t, :], bank[4 + t % 2][:, 0:D], ACT.Square)
                        A(xn[:, t, :], bank[4 + t % 2][:, 0:D], copy).then_inc(q["qc"], 1)
                for st in steps:
                    for it_ in st:
                        item(0, 0, *it_)
                if l == 1:
                    for b in range(4):
                        act.wait_ge(q["qtw"], b + 1)
                        A(qT[:, :, 256 * b:256 * b + 256].rearrange("p c (t q) -> p t c q", t=2),
                          bank[b][:, :].rearrange("p (t c q) -> p t c q", t=2, c=KC), copy).then_inc(q["qtc"], 1)
                exps(0, 0, 0)

                def body(n, k, more):
                    for u in range(8):
                        a, b, c = slot_plan(steps[u] if more else [])
                        for it_ in a:
                            item(n + 1, k ^ 1, *it_)
                        if u < 7:
                            exps(n, k, u + 1)
                        elif more:
                            exps(n + 1, k ^ 1, 0)
                        turned(n, k, u)
                        for it_ in b + c:
                            item(n + 1, k ^ 1, *it_)

                quads(act, body)

            def selfattn(l):
                q = ss_[l]
                w = NKEY if l == 0 else T
                if l == 0:
                    for i in range(12):
                        m, h = divmod(i, 2)
                        act.wait_ge(q["prw"], i + 1)
                        dst = (qT, kT, vT)[m // 2][:, m % 2, h * 512:h * 512 + 512]
                        A(dst, bank[4 + i % 2][:, :], copy).then_inc(q["prc"], 1)
                    act.wait_ge(q["zeroed"], 1)
                    for i in range(4):
                        kind, c = divmod(i, 2)
                        act.wait_ge(q["cvw"], i + 1)
                        A((kcT, vcT)[kind][:, c, :, 1:NKEY],
                          bank[6 + i % 2][:, (i // 2) * 256:(i // 2) * 256 + 256].rearrange("p (b k) -> p b k", b=B),
                          ACT.Identity, bias=vec[:, V_CB + c:V_CB + c + 1]).then_inc(q["cvc"], 1)
                    for b in range(4):
                        act.wait_ge(q["vtw"], b + 1)
                        A(vall[:, 2 * b:2 * b + 2, :], bank[b][:, :].rearrange("p (t d) -> p t d", t=2), copy)\
                            .then_inc(q["vtc"], 1)

                src, vsrc, col = ((qT, vall, C_HM16), (xnT, xn, C_HM4))[l]

                def spread(n, k):
                    after(act, q["sw"], n - 1)
                    for h in range(8):
                        ins = A(sqbd[k][:, 1, :, h, :], src[:, 1, bass.ds(n * P, P)].rearrange("p (j q) -> p j q", j=QB),
                                copy, scale=const[:, col + h:col + h + 1])
                    ins.then_inc(q["qbd1"], 1)
                    after(act, q["pvw"], n - 1)
                    A(vq[k], vsrc.rearrange("p t d -> p (t d)")[:, bass.ds(n * D, D)], copy).then_inc(q["vq"], 1)

                def exps(n, k):
                    act.wait_ge(q["sub"], n + 1)
                    A(sprob[k][:, :, 0:w], sprob[k][:, :, 0:w], ACT.Exp).then_inc(q["exp"], 1)

                def body(n, k, more):
                    if more:
                        exps(n + 1, k ^ 1)
                    act.wait_ge(q["ptw"], n + 1)
                    A(spT[k].rearrange("p g q -> p (g q)"), bank[2 + k][:, :], copy).then_inc(q["ptc"], 1)
                    if not (isinstance(n, int) and n + 2 >= NT):
                        spread(n + 2, k)

                if l == 0:
                    act.wait_ge(q["vtc"], 4)
                else:
                    act.wait_ge(ln_copied, 4 * 5)
                spread(0, 0)
                spread(1, 1)
                exps(0, 0)
                quads(act, body)
                if l == 0:
                    for i in range(4):
                        m, h = divmod(i, 2)
                        act.wait_ge(q["zw"], i + 1)
                        A(zT[:, m, h * 512:h * 512 + 512], bank[i][:, :], ACT.Identity,
                          bias=vec[:, V_BO + m:V_BO + m + 1]).then_inc(q["zc"], 1)
                    for t in range(NT):
                        act.wait_ge(q["aw"], t + 1)
                        after(act, q["yw"], t - 1)
                        A(af[t % 2], bank[4 + t % 2][:, :], copy).then_inc(q["ac"], 1)

            def experts(l):
                q = ms[l]
                if l == 0:
                    act.wait_ge(routed, ROUTED[l]["less_max"])
                    A(lg[:, :, :], lg[:, :, :], ACT.Exp).then_inc(gate_exp, 1)
                else:
                    act.wait_ge(routed, ROUTED[l]["less_max"])
                    A(gsm[:, 1, :], gsm[:, 0, :], ACT.Exp).then_inc(gate_exp, 1)

                def body(m, k, it, more=True):
                    if l == 0:
                        act.wait_ge(q[f"w{k}"], 32 * (it + 1))
                        for half in range(2):
                            act.wait_ge(q["upw"], 2 * m + half + 1)
                            for i in range(4):
                                c = 4 * half + i
                                ins = A(eh[k % 2][:, c, :], bank[1 + half][:, i * P:i * P + P], ACT.Gelu_apprx_tanh,
                                        bias=eb1[k][:, c:c + 1])
                            ins.then_inc(q["upc"], 1)
                    else:
                        after(act, q["upc"], m - 1)
                        act.wait_ge(q["upw"], 2 * m + 1)
                        A(esilu[k % 2], bank[1][:, :], ACT.Silu).then_inc(q["silu"], 1)

                tiles(act, body)

            for s in range(stages):
                ln_root(s)
                ln_copy(s)
                (lambda: cross(0), lambda: selfattn(0), lambda: experts(0),
                 lambda: cross(1), lambda: selfattn(1), lambda: experts(1))[s]()

        @block.vector
        def _(dve):
            V = nc.vector
            own = Tally(ln_own)

            def mine(ins):
                dve.wait_ge(ln_own, own.inc(ins))

            def ln(s):
                if s == 0:
                    dve.wait_ge(x_loaded, 16)
                else:
                    dve.wait_ge(x_ready, s)
                for t in range(NT):
                    ins = V.bn_stats(ln_stats[:, t, :], x[:, t, :])
                mine(ins)
                for t in range(NT):
                    ins = V.bn_aggr(ln_mv[:, t, :], ln_stats[:, t, :])
                mine(ins)
                V.tensor_scalar(ln_ve[:, :], ln_mv[:, :, 1], 1e-5, None, ALU.add).then_inc(ln_var, 1)
                dve.wait_ge(ln_std, s + 1)
                mine(V.reciprocal(ln_rs[:, :], ln_sd[:, :]))
                for t in range(NT):
                    V.tensor_scalar(xn[:, t, :], x[:, t, :], ln_mv[:, t, 0:1], ln_rs[:, t:t + 1],
                                    ALU.subtract, ALU.mult).then_inc(ln_norm, 1)

            def finish(ins, q, t):
                ins.then_inc(x_ready if t == NT - 1 else q, 1)

            def cross(l):
                q = xs[l]
                steps, nit, place = parts(l)

                def sums(n, idx, kind, i):
                    if kind == "A":
                        r = min(P, QS - P * i)
                        dve.wait_ge(q["sq"], VT * n + i + 1)
                        after(dve, q["root"], ROOT_STEPS * (VT // BATCH) * n)
                        V.tensor_reduce(kss[0:r, i, :], ksq[0:r, i % 3, :].rearrange("p (h d) -> p h d", d=HD),
                                        AX_X, ALU.add).then_inc(q["ss"], 1)

                def norms(n, idx, kind, i):
                    if kind == "A":
                        if i % BATCH == BATCH - 1:
                            dve.wait_ge(q["ss"], VT * n + i + 1)
                            first = i + 1 - BATCH
                            step = iter(range(1, ROOT_STEPS + 1))
                            base = ROOT_STEPS * ((VT // BATCH) * n + i // BATCH)

                            def rooted(ins):
                                ins.then_inc(q["root"], 1)
                                dve.wait_ge(q["root"], base + next(step))

                            flat = lambda v: v[:, first:i + 1, :].rearrange("p t h -> p (t h)")
                            inv_root(flat(kr), flat(kss), BATCH * NH, rooted)
                        if i >= BATCH - 1:
                            weigh_keys(n, i + 1 - BATCH)
                    elif kind == "T" and i in (VT - 6, VT - 5):
                        weigh_keys(n, i + 4)

                def weigh_keys(n, i):
                    r = min(P, QS - P * i)
                    t = VT * n + i
                    h3 = lambda v: v.rearrange("p (h d) -> p h d", d=HD)
                    after(dve, q["krope"], t - 2)
                    dve.wait_ge(q["kvc"], nit * n + place["A", i] + 1)
                    V.tensor_tensor(h3(kn[0:r, i % 3, :]), h3(kraw[0:r, i % KRAW, :]),
                                    kr[0:r, i, :].unsqueeze(2).to_broadcast([r, NH, HD]), ALU.mult).then_inc(q["kw"], 1)

                def maxima(n, u):
                    p = u % 2
                    after(dve, q["negmax"], 8 * n + u)
                    dve.wait_ge(q["scores"], 8 * n + u + 1)
                    if l == 0:
                        V.memset(spare[:, :], 0.0)
                        for g in range(2):
                            ins = V.tensor_tensor_reduce(smask[p][:, g, :], bank[2 * p + g][:, 0:S], negmask[:, :],
                                                         1.0, float(np.finfo(np.float32).min), ALU.add, ALU.max,
                                                         rowmax[:, g:g + 1])
                        ins.then_inc(q["masked"], 1)
                        dve.wait_ge(q["masked"], 8 * n + u + 1)
                        V.tensor_scalar(negmax[p], rowmax[:, :], -1.0, None, ALU.mult).then_inc(q["negmax"], 1)
                    else:
                        for g in range(2):
                            ins = V.tensor_reduce(negmax[p][:, g:g + 1], bank[2 * p + g][:, 0:S], AX_X, ALU.max, negate=True)
                        ins.then_inc(q["negmax"], 1)

                def invert(n, u):
                    after(dve, q["normed"], 8 * n + u - 1)
                    dve.wait_ge(q["probs"], 8 * n + u + 1)
                    V.reciprocal(rcp[u % 2], rowsum[u % 2]).then_inc(q["recip"], 1)

                def turned(n, u):
                    dve.wait_ge(q["ptw"], 8 * n + u + 1)
                    V.tensor_copy(pTb[u % 2][:, 1, :], bank[5][:, 0:WIN]).then_inc(q["ptd"], 1)

                def norm(n, u):
                    dve.wait_ge(q["pvw"], 8 * n + u + 1)
                    dve.wait_ge(q["recip"], 8 * n + u + 1)
                    for g in range(2):
                        ins = V.scalar_tensor_tensor(omb[u % 2][:, 64 * g:64 * g + 64], bank[6][:, 64 * g:64 * g + 64],
                                                     rcp[u % 2][:, g:g + 1], blk, ALU.mult, ALU.mult)
                    ins.then_inc(q["normed"], 1)

                def collapsed(n, u):
                    j, c = divmod(u, 2)
                    dve.wait_ge(q["colw"], 8 * n + u + 1)
                    dst = outT[:, c, bass.ds(n * P + T * j, T)]
                    if l == 0:
                        ins = V.tensor_scalar(dst, bank[6][:, 256:256 + T], vec[:, V_BV + c:V_BV + c + 1], None, ALU.add)
                    else:
                        ins = V.tensor_copy(dst, bank[6][:, 256:256 + T])
                    ins.then_inc(q["colc"], 1)

                def inv_root(dst, src, w, step):
                    v, t = root_v[:, 0:w], root_t[:, 0:w]
                    yi = root_y[:, 0:w]
                    y = yi.bitcast(F32)
                    step(V.tensor_scalar(v, src, 1e-6 * HD, None, ALU.add))
                    step(V.tensor_scalar(yi, v.bitcast(I32), 1, None, ALU.logical_shift_right))
                    step(V.tensor_scalar(yi, yi, -1.0, float(0x5f3759df - 2 ** 31), ALU.mult, ALU.add))
                    for i in range(3):
                        step(V.scalar_tensor_tensor(t, v, 0.5, y, ALU.mult, ALU.mult))
                        step(V.tensor_tensor(t, t, y, ALU.mult))
                        step(V.scalar_tensor_tensor(dst if i == 2 else y, t, 1.5, y, ALU.subtract, ALU.mult))

                if l == 0:
                    dve.wait_ge(mask_loaded, 16 * (QB + 1))
                    mine(V.tensor_scalar(negmask[:, :], negmask[:, :], -1e9, None, ALU.mult))
                    for t in range(NT):
                        ins = V.tensor_tensor(x[:, t, :], x[:, t, :], bo_bc[:, :], ALU.add)
                    mine(ins)
                else:
                    q1 = outT.rearrange("p c n -> p (c n)")
                    q2 = qT.rearrange("p c n -> p (c n)")
                    q0 = xn.rearrange("p t d -> p (t d)")
                    h3 = lambda v: v.rearrange("p (a d) -> p a d", d=HD)
                    bc = lambda v, n: v.unsqueeze(1).to_broadcast([P, NT * NH, n])
                    dve.wait_ge(q["qc"], NT)
                    V.memset(kss[:, :, :], 1.0)
                    mine(V.tensor_reduce(qss[:, :], h3(q1), AX_X, ALU.add))
                    inv_root(qr[:, :], qss[:, :], NT * NH, mine)
                    mine(V.tensor_tensor(h3(q0), h3(q0), qr[:, :].unsqueeze(2).to_broadcast([P, NT * NH, HD]), ALU.mult))
                    dve.wait_ge(q["rw"], 1)
                    V.tensor_tensor(h3(q1), h3(q0), bc(rope_q[:, 0:HD], HD), ALU.mult)
                    V.tensor_tensor(h3(q2)[:, :, 0:8], h3(q0)[:, :, 8:16], bc(rope_q[:, HD:HD + 8], 8), ALU.mult)
                    mine(V.tensor_tensor(h3(q2)[:, :, 8:16], h3(q0)[:, :, 0:8], bc(rope_q[:, HD + 8:2 * HD], 8), ALU.mult))
                    V.tensor_tensor(q0, q1, q2, ALU.add).then_inc(q["qrope"], 1)
                    for st in steps:
                        for it_ in st:
                            sums(0, *it_)
                            norms(0, *it_)
                maxima(0, 0)

                def body(n, k, more):
                    for u in range(8):
                        a, b, c = slot_plan(steps[u] if more else [])
                        if u < 7:
                            maxima(n, u + 1)
                        elif more:
                            maxima(n + 1, 0)
                        invert(n, u)
                        turned(n, u)
                        for it_ in a:
                            sums(n + 1, *it_)
                        past = before(n, k, u, 2)
                        if past:
                            collapsed(past[0], past[2])
                        for it_ in b:
                            sums(n + 1, *it_)
                        past = before(n, k, u, 1)
                        if past:
                            norm(past[0], past[2])
                        for it_ in c:
                            sums(n + 1, *it_)
                        for it_ in a + b + c:
                            norms(n + 1, *it_)

                quads(dve, body)
                collapsed(NT - 1, 6)
                norm(NT - 1, 7)
                collapsed(NT - 1, 7)
                for t in range(NT):
                    dve.wait_ge(q["postw"], t + 1)
                    finish(V.tensor_tensor(x[:, t, :], x[:, t, :], bank[t][:, 0:D], ALU.add), q["xadd"], t)

            def selfattn(l):
                q = ss_[l]
                w = NKEY if l == 0 else T

                def scores(n, k):
                    after(dve, q["sub"], n)
                    after(dve, q["pn"], n)
                    dve.wait_ge(q["sw"], n + 1)
                    s3 = sprob[k][:, :, 0:w]
                    raw = bank[k][:, :].rearrange("p (a w) -> p a w", w=KW)[:, :, 0:w]
                    mcol = const[:, (C_M0, C_M1)[l]:(C_M0, C_M1)[l] + w]
                    V.tensor_tensor(s3, raw, mcol.unsqueeze(1).to_broadcast([P, NH, w]), ALU.add).then_inc(q["own"], 1)
                    dve.wait_ge(q["own"], 2 * n + 1)
                    V.tensor_reduce(smx[:, :], s3, AX_X, ALU.max).then_inc(q["own"], 1)
                    dve.wait_ge(q["own"], 2 * n + 2)
                    V.tensor_tensor(s3, s3, smx[:, :].unsqueeze(2).to_broadcast([P, NH, w]), ALU.subtract)\
                        .then_inc(q["sub"], 1)

                def norm(n, k):
                    dve.wait_ge(q["exp"], n + 1)
                    s3 = sprob[k][:, :, 0:w]
                    V.tensor_reduce(ssum[:, :], s3, AX_X, ALU.add).then_inc(q["sum"], 1)
                    dve.wait_ge(q["sum"], 2 * n + 1)
                    V.reciprocal(srcp[:, :], ssum[:, :]).then_inc(q["sum"], 1)
                    dve.wait_ge(q["sum"], 2 * n + 2)
                    V.tensor_tensor(pn[k].rearrange("p g j w -> p j g w")[:, :, :, 0:w],
                                    s3.rearrange("p (j g) w -> p j g w", j=QB),
                                    srcp[:, :].rearrange("p (j g) -> p j g", j=QB).unsqueeze(3).to_broadcast([P, QB, GH, w]),
                                    ALU.mult).then_inc(q["pn"], 1)

                def mask_heads(n, k):
                    dve.wait_ge(q["pvw"], n + 1)
                    for j in range(QB):
                        ins = V.tensor_tensor(som[:, j, :].rearrange("p (g d) -> p g d", d=64),
                                              bank[4 + j][:, 0:D].rearrange("p (g d) -> p g d", d=64),
                                              blk.unsqueeze(1).to_broadcast([P, GH, 64]), ALU.mult)
                    ins.then_inc(q["om"], 1)

                def collapsed(n, k):
                    dve.wait_ge(q["colw"], n + 1)
                    if l == 0:
                        V.tensor_copy(outT[:, :, bass.ds(n * P, P)],
                                      bank[2 + k][:, 0:2 * P].rearrange("p (c q) -> p c q", c=KC)).then_inc(q["colc"], 1)
                    else:
                        xv = x.rearrange("p t d -> p (t d)")[:, bass.ds(n * D, D)]
                        V.tensor_tensor(xv, xv, bank[2 + k][:, 0:D], ALU.add).then_inc(q["colc"], 1)

                def body(n, k, more):
                    if more:
                        scores(n + 1, k ^ 1)
                    mask_heads(n, k)
                    if more:
                        norm(n + 1, k ^ 1)
                    collapsed(n, k)

                if l == 0:
                    for i in range(4):
                        kind, c = divmod(i, 2)
                        if i == 0:
                            dve.wait_ge(q["zeroed"], 1)
                        V.tensor_copy((kcT, vcT)[kind][:, c, :, 0:1],
                                      vec[:, (V_NK, V_NV)[kind] + c:(V_NK, V_NV)[kind] + c + 1].unsqueeze(1)
                                      .to_broadcast([P, B, 1])).then_inc(q["null"], 1)
                scores(0, 0)
                norm(0, 0)
                quads(dve, body)
                if l == 0:
                    for t in range(NT):
                        dve.wait_ge(q["yw"], t + 1)
                        finish(V.tensor_tensor(x[:, t, :], x[:, t, :], bank[6 + t % 2][:, 0:D], ALU.add), q["yc"], t)
                else:
                    dve.wait_ge(q["colc"], NT)
                    V.memset(spare[:, :], 0.0).then_inc(x_ready, 1)

            def experts(l, s):
                q = ms[l]
                nh = HC[l]
                if l == 0:
                    for v in seen + used:
                        ins = V.memset(v[:, 0:8] if v in used else v[:, 0:NT, :], 0.0)
                    mine(ins)
                dve.wait_ge(ranked, RANKED[l]["logits"])
                raw = bank[7][:, 0:NT * E_].rearrange("p (t e) -> p t e", e=E_)
                mine(V.tensor_copy(pr[:, :, :], raw))
                b3 = lambda v: v.unsqueeze(2).to_broadcast([P, NT, E_])
                if l == 0:
                    mine(V.tensor_reduce(gsm[:, 0, :], pr[:, :, :], AX_X, ALU.max))
                    V.tensor_tensor(lg[:, :, :], pr[:, :, :], b3(gsm[:, 0, :]), ALU.subtract).then_inc(routed, 1)
                    dve.wait_ge(gate_exp, l + 1)
                    mine(V.tensor_reduce(gsm[:, 0, :], lg[:, :, :], AX_X, ALU.add))
                    mine(V.reciprocal(gsm[:, 1, :], gsm[:, 0, :]))
                    mine(V.tensor_tensor(pr[:, :, :], lg[:, :, :], b3(gsm[:, 1, :]), ALU.mult))
                for t in range(NT):
                    ins = V.max(top[:, t, :], pr[:, t, :])
                mine(ins)
                for t in range(NT):
                    ins = V.max_index(topi[:, t, :], top[:, t, :], pr[:, t, :])
                mine(ins)
                mine(V.tensor_copy(topf[:, :, 0:2], topi[:, :, 0:2]))
                if l == 0:
                    mine(V.tensor_tensor(gsm[:, 0, :], top[:, :, 0], top[:, :, 1], ALU.add))
                    mine(V.tensor_scalar(gsm[:, 0, :], gsm[:, 0, :], 1e-8, None, ALU.add))
                    mine(V.reciprocal(gsm[:, 1, :], gsm[:, 0, :]))
                    V.tensor_tensor(gsm[:, 2, :], top[:, :, 0], gsm[:, 1, :], ALU.mult)
                    mine(V.tensor_tensor(gsm[:, 3, :], top[:, :, 1], gsm[:, 1, :], ALU.mult))
                else:
                    V.tensor_tensor(gsm[:, 0, :], top[:, :, 1], top[:, :, 0], ALU.subtract).then_inc(routed, 1)
                    dve.wait_ge(gate_exp, l + 1)
                    mine(V.tensor_scalar(gsm[:, 0, :], gsm[:, 1, :], 1.0, None, ALU.add))
                    mine(V.reciprocal(gsm[:, 2, :], gsm[:, 0, :]))
                    mine(V.tensor_tensor(gsm[:, 3, :], gsm[:, 1, :], gsm[:, 2, :], ALU.mult))
                iota = const[:, C_IOTA:C_IOTA + E_].unsqueeze(1).to_broadcast([P, NT, E_])
                for i in range(TOPK):
                    ins = V.tensor_tensor(onehot[i][:, :, :], iota, b3(topf[:, :, i]), ALU.is_equal)
                mine(ins)
                flat = lambda v: v.rearrange("p t e -> p (t e)")
                V.tensor_tensor(chosen[:, :], flat(onehot[0]), flat(onehot[1]), ALU.add).then_inc(routed, 1)
                if l == 0:
                    V.tensor_tensor(gate[:, :, :], onehot[0][:, :, :], b3(gsm[:, 2, :]), ALU.mult)
                    mine(V.tensor_tensor(lg[:, :, :], onehot[1][:, :, :], b3(gsm[:, 3, :]), ALU.mult))
                    V.tensor_tensor(gate[:, :, :], gate[:, :, :], lg[:, :, :], ALU.add).then_inc(routed, 1)

                dve.wait_ge(ranked, RANKED[l]["ranks"])
                mine(V.tensor_copy(seen[0][:, NT:, :], bank[6][:, P:P + NT * E_].rearrange("p (t e) -> p t e", e=E_)))
                for i in range(3):
                    mine(V.tensor_tensor(seen[i + 1][:, NT:, :], seen[i][:, NT:, :],
                                         seen[i][:, NT - 2 ** i:2 * NT - 2 ** i, :], ALU.add))
                total = seen[3][:, 2 * NT - 1, :]
                mine(V.tensor_tensor(more_than[:, :, :], total.unsqueeze(2).to_broadcast([P, E_, NT]),
                                     const[:, C_THR:C_THR + NT].unsqueeze(1).to_broadcast([P, E_, NT]), ALU.is_gt))
                mine(V.tensor_reduce(used[0][:, E_:], more_than[:, :, :], AX_X, ALU.add))
                for i in range(3):
                    mine(V.tensor_tensor(used[i + 1][:, E_:], used[i][:, E_:], used[i][:, E_ - 2 ** i:2 * E_ - 2 ** i], ALU.add))
                mine(V.tensor_tensor(place_[:, :, :], bank[6][:, 0:NT * E_].rearrange("p (t e) -> p t e", e=E_),
                                     seen[3][:, NT - 1:2 * NT - 1, :], ALU.add))
                mine(V.scalar_tensor_tensor(place_[:, :, :], used[3][:, E_ - 1:2 * E_ - 1].unsqueeze(1)
                                            .to_broadcast([P, NT, E_]), float(P), place_[:, :, :], ALU.mult, ALU.add))
                for i in range(TOPK):
                    mine(V.tensor_tensor(picked[:, :, :], onehot[i][:, :, :], place_[:, :, :], ALU.mult))
                    mine(V.tensor_reduce(slotf[:, i, :], picked[:, :, :], AX_X, ALU.add))
                V.tensor_copy(slot[:, :, :], slotf[:, :, :]).then_inc(routed, 1)
                mine(V.tensor_tensor(ends[:, :, :], const[:, C_TILE:C_TILE + NTILE].unsqueeze(2).to_broadcast([P, NTILE, E_]),
                                     used[3][:, E_:].unsqueeze(1).to_broadcast([P, NTILE, E_]), ALU.is_ge))
                mine(V.tensor_reduce(tilef[:, :], ends[:, :, :], AX_X, ALU.add))
                V.tensor_scalar(tile_expert[:, :], tilef[:, :], float(E_ - 1), None, ALU.min).then_inc(routed, 1)
                if l == 0:
                    dve.wait_ge(ranked, RANKED[l]["gates"])
                    for b in range(2):
                        V.tensor_copy(gateT[:, 512 * b:512 * b + 512], bank[4 + b][0:E_, :]).then_inc(q["cwtc"], 1)
                    for t in range(NT):
                        dve.wait_ge(q["cwb"], t + 1)
                        V.tensor_tensor(x[:, t, :], x[:, t, :], bank[4 + t % 2][:, 0:D], ALU.add).then_inc(q["cwbc"], 1)

                def turned(m, k):
                    dve.wait_ge(q["xst"], m + 1)
                    V.tensor_copy(exT[k % 2].rearrange("p c q -> p (c q)"), bank[0][:, 0:D]).then_inc(q["xsc"], 1)

                def prod(m, k):
                    if l == 1:
                        dve.wait_ge(q["silu"], m + 1)
                        dve.wait_ge(q["upw"], 2 * m + 2)
                        V.tensor_tensor(eh[k % 2][:, 0:nh, :].rearrange("p c q -> p (c q)"), bank[2][:, :], esilu[k % 2],
                                        ALU.mult).then_inc(q["upc"], 1)

                def out_(m, k, it):
                    after(dve, q[f"ys{k % 2}"], 16 * (EB // 2 * it + k // 2))
                    dve.wait_ge(q["dnw"], m + 1)
                    V.tensor_copy(eys[k % 2], bank[4 + k % 2][:, 0:D]).then_inc(q["dnc"], 1)

                def body(m, k, it, more=2):
                    if more > 0:
                        prod(m + 1, (k + 1) % EB)
                    if more > 1:
                        turned(m + 2, (k + 2) % EB)
                    out_(m, k, it)

                turned(0, 0)
                prod(0, 0)
                turned(1, 1)
                tiles(dve, body)
                for t in range(NT):
                    dve.wait_ge(gathered[t // (NT // 2)], 16 * TOPK * (NT // 2) * (l + 1))
                    for i in range(TOPK):
                        if t == 0 and i == 0 and l == 0:
                            dve.wait_ge(q["cwbc"], NT)
                        ins = V.scalar_tensor_tensor(x[:, t, :], eyg[t][i], gsm[:, 2 + i, t:t + 1], x[:, t, :],
                                                     ALU.mult, ALU.add)
                        if i == 0:
                            mine(ins)
                if t == NT - 1:
                    ins.then_inc(x_ready, 1)

            V.memset(zero[:, :], 0.0).then_inc(blank, 1)
            for s in range(stages):
                ln(s)
                (lambda: cross(0), lambda: selfattn(0), lambda: experts(0, 2),
                 lambda: cross(1), lambda: selfattn(1), lambda: experts(1, 5))[s]()

        @block.gpsimd
        def _(pool):
            G = nc.gpsimd
            own = Tally(pool_own)

            def spread(dst, src, n, c, col, q):
                G.tensor_tensor(dst[:, c, :, :, :],
                                src[:, c, bass.ds(n * P, P)].rearrange("p (j q) -> p j q", j=QB).unsqueeze(2)
                                .to_broadcast([P, QB, 8, T]),
                                const[:, col:col + 8].unsqueeze(1).unsqueeze(3).to_broadcast([P, QB, 8, T]),
                                ALU.mult).then_inc(q["qbd"], 1)

            def cross(l, s):
                q = xs[l]
                steps, nit, place = parts(l)
                if s:
                    pool.wait_ge(x_ready, s)
                for j in range(QB):
                    for c in range(KC):
                        own.inc(G.memset(pwin[j][c], 0.0))
                if l == 1:
                    pool.wait_ge(normw_loaded, 16)
                    pool.wait_ge(const_loaded, 32)
                    for base, m_, dst in ((C_RQ, 1, 0), (C_RK, VT, 32)):
                        which = 0 if base == C_RQ else 1
                        tab = const[:, base:base + 32 * m_].rearrange("p (m k) -> p m k", k=32)
                        o = ropew[:, dst:dst + 32 * m_].rearrange("p (m k) -> p m k", k=32)
                        for a, b, wa in ((0, 16, 0), (16, 24, 8), (24, 32, 0)):
                            wv = normw[:, which, wa:wa + b - a].unsqueeze(1).to_broadcast([P, m_, b - a])
                            ins = G.tensor_tensor(o[:, :, a:b], tab[:, :, a:b], wv, ALU.mult)
                            own.inc(ins)
                    pool.wait_ge(pool_own, own.n)
                    G.memset(mark[:, :], 0.0).then_inc(q["rw"], 1)
                pool.wait_ge(pool_own, own.n)

                def rotate(n, i):
                    r = min(P, QS - P * i)
                    t = VT * n + i
                    rt = rope_k(i)
                    h3 = lambda v: v.rearrange("p (h d) -> p h d", d=HD)
                    bc = lambda v: v[0:r, :].unsqueeze(1).to_broadcast([r, NH, v.shape[-1]])
                    after(pool, q["krope"], t)
                    pool.wait_ge(q["kw"], t + 1)
                    kn3, kb3 = h3(kn[0:r, i % 3, :]), h3(kb_[0:r, :])
                    G.tensor_tensor(kb3[:, :, 0:8], kn3[:, :, 8:16], bc(rt[:, HD:HD + 8]), ALU.mult).then_inc(q["kn"], 1)
                    G.tensor_tensor(kb3[:, :, 8:16], kn3[:, :, 0:8], bc(rt[:, HD + 8:2 * HD]), ALU.mult).then_inc(q["kn"], 1)
                    G.tensor_tensor(h3(ka[0:r, :]), kn3, bc(rt[:, 0:HD]), ALU.mult).then_inc(q["kn"], 1)
                    pool.wait_ge(q["kn"], 3 * t + 3)
                    if i >= 3:
                        pool.wait_ge(q["kvw"], nit * n + place["T", i - 3] + 1)
                    elif not (isinstance(n, int) and n == 0):
                        pool.wait_ge(q["kvw"], nit * (n - 1) + place["T", i + VT - 3] + 1)
                    G.tensor_tensor(krope[0:r, i % 3, :], ka[0:r, :], kb_[0:r, :], ALU.add).then_inc(q["krope"], 1)

                def rotated_keys(n):
                    for i in range(VT):
                        rotate(n, i)

                if l == 1:
                    rotated_keys(0)
                pool.wait_ge(q["qc"] if l == 0 else q["qtc"], 4)
                pool.wait_ge(const_loaded, 32)
                for c in range(KC):
                    spread(xqbd[0], qT, 0, c, C_HM4, q)

                def body(n, k, more):
                    if more:
                        after(pool, q["scores"], 8 * n)
                        spread(xqbd[k ^ 1], qT, n + 1, 0, C_HM4, q)
                        if l == 1:
                            rotated_keys(n + 1)
                        spread(xqbd[k ^ 1], qT, n + 1, 1, C_HM4, q)

                quads(pool, body)

            def selfattn(l, s):
                q = ss_[l]
                src, col = ((qT, C_HM16), (xnT, C_HM4))[l]
                pool.wait_ge(x_ready, s)
                if l == 0:
                    for v in (vcT.rearrange("p c b w -> p (c b w)"), kcT.rearrange("p c b w -> p (c b w)")):
                        own.inc(G.memset(v, 0.0))
                    for v in pn:
                        own.inc(G.memset(v.rearrange("p g j w -> p (g j w)"), 0.0))
                    pool.wait_ge(pool_own, own.n)
                    G.memset(mark[:, :], 0.0).then_inc(q["zeroed"], 1)
                    pool.wait_ge(wa_loaded, 48)
                    G.tensor_tensor(bdw.rearrange("p a (h o) -> p a h o", o=HD),
                                    cw[:, :, :].unsqueeze(2).to_broadcast([P, KC * CF, 8, HD]),
                                    const[:, C_HM1:C_HM1 + 8].unsqueeze(1).unsqueeze(3).to_broadcast([P, KC * CF, 8, HD]),
                                    ALU.mult).then_inc(q["bdw"], 1)
                    pool.wait_ge(q["prc"], 4)
                else:
                    pool.wait_ge(ln_copied, 4 * 5)

                def body(n, k):
                    after(pool, q["sw"], n - 1)
                    spread(sqbd[k], src, n, 0, col, q)

                for k in range(2):
                    body(k, k)
                with pool.Fori(1, NT // 2) as it:
                    for k in range(2):
                        body(2 * it + k, k)

            def experts(l, s):
                q = ms[l]
                pool.wait_ge(zeroed, 32)
                pool.wait_ge(routed, ROUTED[l]["slots"])
                pool.wait_ge(ln_norm, NT * (s + 1))
                at = lambda i, t: bass.IndirectOffsetOnAxis(ap=slot[:, i, t:t + 1], axis=0)
                for t in range(NT):
                    for i in range(TOPK):
                        G.indirect_dma_start(out=xslot[l], out_offset=at(i, t), in_=xn[:, t, :], in_offset=None)\
                            .then_inc(scattered, 16)
                for k in range(2):
                    pool.wait_ge(q[f"ys{k}"], 16 * (NTILE // 2))
                for t in range(NT):
                    for i in range(TOPK):
                        G.indirect_dma_start(out=eyg[t][i], out_offset=None, in_=yslot[l], in_offset=at(i, t))\
                            .then_inc(gathered[t // (NT // 2)], 16)

            cross(0, 0)
            if stages > 1:
                selfattn(0, 1)
            if stages > 2:
                experts(0, 2)
            if stages > 3:
                cross(1, 3)
            if stages > 4:
                selfattn(1, 4)
            if stages > 5:
                experts(1, 5)


def kernel(**inputs):
    import concourse.bacc as _bacc
    from concourse.bass_utils import run_bass_kernel_spmd as _run

    a = {k: np.asarray(v) for k, v in inputs.items()}
    cols = lambda v: v.reshape(-1, KC, P).transpose(2, 0, 1).reshape(P, -1)
    rows = lambda v: np.broadcast_to(v.reshape(1, -1), (P, v.size))
    chunks = lambda w: w.reshape(E_, -1, P, w.shape[2]).transpose(2, 0, 1, 3).reshape(P, E_, -1)
    expert_rows = lambda *w: np.concatenate([chunks(m) for m in w], 2).reshape(P, -1)
    kv = lambda k, v: np.concatenate([k, v], 1)
    arrays = {
        "x": a["x"].reshape(TOK, D),
        "ctxT": a["ctx_1024"].reshape(B * S, D).T,
        "mask": a["mask_1x1xSxS2_fk1"].reshape(T, S),
        "const": shape_constants(),
        "vec": np.concatenate([cols(a[n]) for n in ("L0_xattn_bq", "L0_xattn_bk", "L0_xattn_bv", "L0_attn_conv_b",
                                                    "L0_attn_b_out", "L0_attn_null_k", "L0_attn_null_v")], 1),
        "bo": rows(a["L0_xattn_bo"]),
        "w0q": a["L0_xattn_Wq"], "w0kv": kv(a["L0_xattn_Wk"], a["L0_xattn_Wv"]), "w0o": a["L0_xattn_Wo"],
        "w1q": a["L1_xattn_Wq"].T, "w1kv": kv(a["L1_xattn_Wk"].T, a["L1_xattn_Wv"].T), "w1o": a["L1_xattn_Wo"].T,
        "wqkv": a["L0_attn_Wqkv"], "wout": a["L0_attn_W_out"],
        "conv": a["L0_attn_conv_w"].reshape(KC, 8, HD, HD, CF).transpose(1, 3, 0, 4, 2).reshape(P, KC * CF, HD),
        "normw": np.stack([rows(a["L1_xattn_q_norm_w"]), rows(a["L1_xattn_k_norm_w"])], 1),
        "rw0": a["L0_ffn_router_w"].T, "rw1": a["L1_ffn_w_gate"],
        "b1": a["L0_ffn_b1"].reshape(E_, H0 // P, P).transpose(2, 0, 1).reshape(P, -1), "b2": a["L0_ffn_b2"],
        "ew0": expert_rows(a["L0_ffn_w1"].transpose(0, 2, 1), a["L0_ffn_w2"].transpose(0, 2, 1)),
        "ew1": expert_rows(a["L1_ffn_w1"], a["L1_ffn_w3"], a["L1_ffn_w2"]),
    }
    nc = _bacc.Bacc("TRN2", target_bir_lowering=False, num_devices=1)
    named, io = {}, {}
    for name, v in arrays.items():
        v = np.ascontiguousarray(v)
        named[f"in_{name}_dram"] = v
        io[name] = nc.dram_tensor(f"in_{name}_dram", v.shape, mybir.dt.from_np(v.dtype), kind="ExternalInput").ap()
    out = nc.dram_tensor("out_0_dram", (TOK, D), F32, kind="ExternalOutput").ap()
    perceiver_block(nc, io, out, stages=STAGES)
    r = _run(nc, [named], core_ids=[0])
    return r.results[0]["out_0_dram"].reshape(B, T, D)
```

```python
from contextlib import ExitStack

import concourse.bass as bass
import numpy as np
from concourse import mybir

F32 = mybir.dt.float32
U32 = mybir.dt.uint32
I32 = mybir.dt.int32
ALU = mybir.AluOpType
ACT = mybir.ActivationFunctionType
AX_X = mybir.AxisListType.X

P = 128
B, T, D = 32, 32, 256
S = 257
NH, HD = 16, 16
KC = D // P
NT = B * T // P
QB = P // T
QS = QB * S
VT = -(-QS // P)
WIN = 3 * P
TOK = B * T
E_ = 8
H0, H1 = 1024, 512
TOPK = 2
EB = 4
NTILE = (TOPK * TOK + E_ * (P - 1)) // P
ROUNDS = -(-NTILE // EB)
LAST = NTILE - (ROUNDS - 1) * EB
assert LAST > 1
CF = 4
NKEY = T // CF + 1
KRAW = 4
BATCH = 3
KW = 32
ROOT_STEPS = 12
MASK_VALUE = -3.0e38
GH = NH // 4

C_IDENT, C_STACK, C_BLK, C_HM1, C_HM4, C_HM16 = 0, 128, 160, 224, 232, 240
C_CS, C_BD, C_M0, C_M1, C_RQ, C_RK = 248, 1272, 1528, 1560, 1592, 1624
C_IOTA = C_RK + 32 * VT
C_TRI, C_ONES = C_IOTA + E_, C_IOTA + E_ + P
C_THR = C_ONES + P
C_TILE = C_THR + NT
NCONST = C_TILE + NTILE
V_BQ, V_BK, V_BV, V_CB, V_BO, V_NK, V_NV = 0, 2, 4, 6, 8, 10, 12
NVEC = 14


def shape_constants():
    c = np.zeros((P, NCONST), np.float32)
    p = np.arange(P)
    c[:, C_IDENT:C_IDENT + P] = np.eye(P)
    c[:, C_STACK:C_STACK + T] = (p[:, None] % T == np.arange(T)[None])
    c[:, C_BLK:C_BLK + 64] = (p[:, None] // T == np.arange(64)[None] // HD)
    same = (p[:, None] // HD == np.arange(8)[None])
    c[:, C_HM1:C_HM1 + 8] = same
    c[:, C_HM4:C_HM4 + 8] = same * HD ** -0.5
    c[:, C_HM16:C_HM16 + 8] = same * D ** -0.5
    d = np.arange(D)
    turn = (np.outer(d, d) % D) * (2 * np.pi / D)
    cs = np.concatenate([np.cos(turn), np.sin(turn)], 1).reshape(KC, P, 2 * D)
    c[:, C_CS:C_CS + KC * 2 * D] = cs.transpose(1, 0, 2).reshape(P, -1)
    turn = (np.outer(p % T, p % T) % T) * (2 * np.pi / T)
    mine = (p[:, None] // T == p[None] // T)
    c[:, C_BD:C_BD + P] = np.cos(turn) * mine
    c[:, C_BD + P:C_BD + 2 * P] = -np.sin(turn) * mine
    q = (p % T)[:, None]
    j = np.arange(KW)[None]
    c[:, C_M0:C_M0 + KW] = np.where((j >= 1) & (j < NKEY) & (q < CF * (j - 1) + CF - 1), MASK_VALUE, 0.0)
    c[:, C_M1:C_M1 + KW] = np.where(j > q, MASK_VALUE, 0.0)

    def rope(pos, theta):
        freqs = np.float32(theta) ** (-np.arange(0, HD, 2, dtype=np.float32) / np.float32(HD))
        ang = pos.astype(np.float32)[:, None] * freqs[None]
        return np.concatenate([np.cos(ang), np.cos(ang), -np.sin(ang), np.sin(ang)], 1) * HD ** 0.5

    c[:, C_RQ:C_RQ + 32] = rope(p % T, 32.0)
    for m in range(VT):
        c[:, C_RK + 32 * m:C_RK + 32 * m + 32] = rope((P * m + p) % S, 1000.0)
    c[:, C_IOTA:C_IOTA + E_] = np.arange(E_)[None]
    c[:, C_TRI:C_TRI + P] = p[:, None] < p[None]
    c[:, C_ONES:C_ONES + P] = 1.0
    c[:, C_THR:C_THR + NT] = P * np.arange(NT)[None]
    c[:, C_TILE:C_TILE + NTILE] = np.arange(NTILE)[None]
    return c


class Tally:

    def __init__(self, sem):
        self.sem, self.n = sem, 0

    def inc(self, ins):
        ins.then_inc(self.sem, 1)
        self.n += 1
        return self.n


class Signals(dict):

    def __init__(self, make, stage):
        super().__init__()
        self.make, self.stage = make, stage

    def __missing__(self, name):
        self[name] = self.make(self.stage + name)
        return self[name]


def perceiver_block(nc, io, out):
    ctx = ExitStack()
    with ctx:
        def sb(name, shape, dt=F32):
            return ctx.enter_context(nc.sbuf_tensor(name, shape, dt))

        def sem(name):
            return ctx.enter_context(nc.semaphore(name))

        bank = [ctx.enter_context(nc.psum_tensor(f"bank{i}", [P, 512], F32)) for i in range(4)]
        upper = ctx.enter_context(nc.psum_tensor("upper", [P, 4, 512], F32))
        bank += [upper[:, i, :] for i in range(4)]

        const = sb("const", [P, NCONST])
        vec = sb("vec", [P, NVEC])
        ident = const[:, C_IDENT:C_IDENT + P]
        stack = const[:, C_STACK:C_STACK + T]
        blk = const[:, C_BLK:C_BLK + 64]
        x = sb("x", [P, NT, D])
        xn = sb("xn", [P, NT, D])
        xnT = sb("xnT", [P, KC, TOK])
        qT = sb("qT", [P, KC, TOK])
        outT = sb("outT", [P, KC, TOK])
        ln_stats = sb("ln_stats", [P, NT, 6])
        ln_mv = sb("ln_mv", [P, NT, 2])
        ln_ve = sb("ln_ve", [P, NT])
        ln_sd = sb("ln_sd", [P, NT])
        ln_rs = sb("ln_rs", [P, NT])

        wq = [sb(f"wq{l}", [P, KC, D]) for l in range(2)]
        wkv = [sb(f"wkv{l}", [P, KC, 2 * D]) for l in range(2)]
        wo = [sb(f"wo{l}", [P, KC, D]) for l in range(2)]
        bo_bc = sb("bo_bc", [P, D])
        negmask = sb("negmask", [P, S])
        wqkv = sb("wqkv", [P, KC, 3 * D])
        wout = sb("wout", [P, KC, D])
        cw = sb("cw", [P, KC * CF, HD])
        normw = sb("normw", [P, 2, HD])
        ropew = sb("ropew", [P, 2 * HD * (1 + VT)])

        arena = sb("arena", [P, 26000])

        class Arena:
            def __init__(self):
                self.at = 0

            def take(self, *shape):
                n = int(np.prod(shape))
                v = arena[:, self.at:self.at + n]
                self.at += n
                assert self.at <= 26000, self.at
                if len(shape) == 1:
                    return v
                names = "abcd"[:len(shape)]
                return v.rearrange(f"p ({' '.join(names)}) -> p {' '.join(names)}",
                                   **{m: s for m, s in zip(names, shape)})

        const_loaded = sem("const_loaded")
        x_loaded = sem("x_loaded")
        wx_loaded = [sem(f"wx{l}_loaded") for l in range(2)]
        mask_loaded = sem("mask_loaded")
        wa_loaded = sem("wa_loaded")
        normw_loaded = sem("normw_loaded")
        x_ready = sem("x_ready")
        ln_own = sem("ln_own")
        ln_var = sem("ln_var")
        ln_std = sem("ln_std")
        ln_norm = sem("ln_norm")
        ln_turned = sem("ln_turned")
        ln_copied = sem("ln_copied")
        out_stored = sem("out_stored")

        zeroed = sem("zeroed")
        blank = sem("blank")
        gathered = [sem(f"gathered{h}") for h in range(2)]
        blanked = sem("blanked")
        weights_in = sem("router_loaded")
        scattered = sem("scattered")
        gate_exp = sem("gate_exp")
        pool_own = sem("pool_own")
        routed = sem("routed")
        ranked = sem("ranked")
        ROUTED = [{m: i + 1 for i, m in enumerate(("less_max", "hot", "gate", "slots", "tiles"))},
                  {m: i + 6 for i, m in enumerate(("less_max", "hot", "slots", "tiles"))}]
        RANKED = [{"logits": 1, "ranks": 2, "gates": 3}, {"logits": 4, "ranks": 5}]
        xs = [Signals(sem, f"cross{l}_") for l in range(2)]
        selfs = [Signals(sem, f"self{l}_") for l in range(2)]
        ms = [Signals(sem, f"experts{l}_") for l in range(2)]

        ar = Arena()
        ctxb = [ar.take(KC, QS) for _ in range(2)]
        ktb = [ar.take(KC, QS) for _ in range(2)]
        vb = [ar.take(VT, D) for _ in range(2)]
        xqbd = [ar.take(KC, QB, 8, T) for _ in range(2)]
        smask = [ar.take(2, S) for _ in range(2)]
        pwin = [[ar.take(2, WIN) for _ in range(2)] for _ in range(QB)]
        pTb = [ar.take(2, WIN) for _ in range(2)]
        omb = [ar.take(P) for _ in range(2)]
        xsmall = ar.take(64)
        negmax = [xsmall[:, 2 * i:2 * i + 2] for i in range(2)]
        rowsum = [xsmall[:, 4 + 2 * i:6 + 2 * i] for i in range(2)]
        rcp = [xsmall[:, 8 + 2 * i:10 + 2 * i] for i in range(2)]
        kraw = sb("kraw", [P, KRAW, D])
        ksq = sb("ksq", [P, 3, D])
        kn = sb("kn", [P, 3, D])
        ka = sb("ka", [P, D])
        kb = sb("kb", [P, D])
        krope = sb("krope", [P, 3, D])
        kss = sb("kss", [P, VT, NH])
        root_v = sb("root_v", [P, NT * NH])
        root_t = sb("root_t", [P, NT * NH])
        root_y = sb("root_y", [P, NT * NH], I32)
        kr = sb("kr", [P, VT, NH])
        qss = root_t
        qr = sb("qr", [P, NT * NH])

        rope_q = ropew[:, 0:32]

        def rope_k(m):
            return ropew[:, 32 + 32 * m:64 + 32 * m]

        def parts(l):
            if l == 0:
                order = [("K", i) for i in range(8)] + [("V", i) for i in range(VT)]
                cut = [2, 2, 2, 2, 2, 2, 2, 3]
            else:
                order = [("A", 0), ("A", 1), ("A", 2), ("A", 3), ("A", 4), ("T", 0), ("A", 5), ("T", 1), ("A", 6),
                         ("T", 2), ("A", 7), ("A", 8), ("T", 3), ("T", 4), ("T", 5), ("T", 6), ("T", 7), ("T", 8)]
                cut = [3, 2, 3, 3, 3, 1, 3, 0]
            steps, at = [], 0
            for n in cut:
                steps.append([(at + i, *order[at + i]) for i in range(n)])
                at += n
            assert at == len(order)
            return steps, len(order), {o: i for i, o in enumerate(order)}

        def first_items(l, early):
            items = [item_ for st in parts(l)[0] for item_ in st]
            cut = items.index(next(item_ for item_ in items if item_[1] == "T")) if l == 1 else 0
            return items[:cut] if early else items[cut:]

        def item_bank(n, idx):
            return bank[7 - idx % 2] if isinstance(n, int) and n == 0 else bank[7]

        ar = Arena()
        kT = ar.take(KC, TOK)
        vT = ar.take(KC, TOK)
        kcT = ar.take(KC, B, KW)
        vcT = ar.take(KC, B, KW)
        bdw = ar.take(KC * CF, P)
        vall = ar.take(NT, D)
        sqbd = [ar.take(KC, QB, 8, T) for _ in range(2)]
        vq = [ar.take(QB, D) for _ in range(2)]
        sprob = [ar.take(NH, KW) for _ in range(2)]
        pn = [ar.take(GH, QB, KW) for _ in range(2)]
        spT = [ar.take(GH, P) for _ in range(2)]
        som = [ar.take(KC, P) for _ in range(2)]
        zT = kT
        af = [vT[:, i, 0:2 * D] for i in range(2)]
        rowmax = sb("rowmax", [P, 2])
        spare = sb("spare", [1, 1])
        mark = sb("mark", [1, 1])
        smx = sb("smx", [P, NH])
        ssum = sb("ssum", [P, NH])
        srcp = sb("srcp", [P, NH])

        ar = Arena()
        HC = (H0 // P, H1 // P)
        EW = (KC * H0 + H0 // P * D, 2 * KC * H1 + H1 // P * D)
        ew = [ar.take(max(EW)) for _ in range(EB)]
        eb1 = [ar.take(H0 // P) for _ in range(EB)]
        eh = [ar.take(H0 // P, P) for _ in range(2)]
        esilu = [ar.take(H1) for _ in range(2)]
        exs = [ar.take(D) for _ in range(EB)]
        exT = [ar.take(KC, P) for _ in range(2)]
        eys = [ar.take(D) for _ in range(2)]
        eyg = [[ar.take(D) for _ in range(TOPK)] for _ in range(NT)]
        zero = sb("zero", [P, D])
        onehot = [sb(f"onehot{i}", [P, NT, E_]) for i in range(TOPK)]
        chosen = sb("chosen", [P, NT * E_])
        seen = [sb(f"seen{i}", [P, 2 * NT, E_]) for i in range(4)]
        used = [sb(f"used{i}", [P, 2 * E_]) for i in range(4)]
        more_than = sb("more_than", [P, E_, NT])
        slot_base = sb("place", [P, NT, E_])
        picked = sb("picked", [P, NT, E_])
        slotf = sb("slotf", [P, TOPK, NT])
        slot = sb("slot", [P, TOPK, NT], U32)
        ends = sb("ends", [P, NTILE, E_])
        tilef = sb("tilef", [P, NTILE])
        tile_expert = sb("tile_expert", [P, NTILE], I32)
        xslot = [nc.dram_tensor(f"xslot{l}", [NTILE * P, D], F32, kind="Internal").ap() for l in range(2)]
        yslot = [nc.dram_tensor(f"yslot{l}", [NTILE * P, D], F32, kind="Internal").ap() for l in range(2)]
        rw0 = sb("rw0", [P, KC, E_])
        rw1 = sb("rw1", [P, KC, E_])
        b2sb = sb("b2sb", [E_, D])
        lg = sb("lg", [P, NT, E_])
        pr = sb("pr", [P, NT, E_])
        top = sb("top", [P, NT, 8])
        topi = sb("topi", [P, NT, 8], U32)
        topf = sb("topf", [P, NT, 8])
        gsm = sb("gsm", [P, 4, NT])
        gate = sb("gate", [P, NT, E_])
        gateT = qT[0:E_, 0, :]

        block = ctx.enter_context(nc.Block())

        def head_mask(a, h):
            return const[32 * a:32 * a + 32, C_HM1 + h:C_HM1 + h + 1]

        def head_picks(l, n, k, odd):
            weighted = upper.rearrange("p j (c h q) -> p (j c) h q", c=KC, h=8)
            for a in range(4):
                h = 2 * a + odd
                rows = slice(32 * a, 32 * a + 32)
                if l == 0:
                    v = outT.rearrange("p c n -> p (c n)")[:, bass.ds(n * D, D)]
                    yield v.rearrange("p (b q) -> p b q", q=T)[rows, :, :], weighted[rows, :, h, :], head_mask(a, h)
                else:
                    for c in range(KC):
                        yield (som[k][:, c, :].rearrange("p (j q) -> p j q", q=T)[rows, :, :],
                               weighted[rows, c::KC, h, :], head_mask(a, h))

        def slot_plan(items):
            return items[0:1], items[1:2], items[2:]

        @block.sync
        def _(sp):
            sp.dma_start(x[:, :, :], io["x"].rearrange("(t p) d -> p t d", p=P)).then_inc(x_loaded, 16)
            sp.dma_start(const[:, :], io["const"]).then_inc(const_loaded, 16)
            sp.dma_start(vec[:, :], io["vec"]).then_inc(const_loaded, 16)

            def cross_weights(l):
                for dst, src in ((wq[l], "q"), (wkv[l], "kv"), (wo[l], "o")):
                    sp.dma_start(dst[:, :, :], io[f"w{l}{src}"].rearrange("(c p) n -> p c n", p=P)).then_inc(wx_loaded[l], 16)

            cross_weights(0)

            def load_ctx(l, k, n):
                sp.dma_start(ctxb[k], io["ctxT"].rearrange("(c p) n -> p c n", p=P)[:, :, bass.ds(n * QS, QS)])\
                  .then_inc(xs[l][f"ctx{k}"], 16)

            def cross_loads(l):
                load_ctx(l, 0, 0)
                load_ctx(l, 1, 1)
                if l == 0:
                    for h in range(QB):
                        sp.dma_start(negmask[T * h:T * h + T, :], io["mask"]).then_inc(mask_loaded, 16)
                    sp.dma_start(bo_bc[:, :], io["bo"]).then_inc(mask_loaded, 16)
                    sp.dma_start(wqkv[:, :, :], io["wqkv"].rearrange("(c p) n -> p c n", p=P)).then_inc(wa_loaded, 16)
                    sp.dma_start(wout[:, :, :], io["wout"].rearrange("(c p) n -> p c n", p=P)).then_inc(wa_loaded, 16)
                    sp.dma_start(cw[:, :, :], io["conv"]).then_inc(wa_loaded, 16)
                    cross_weights(1)
                    sp.dma_start(normw[:, :, :], io["normw"]).then_inc(normw_loaded, 16)
                nit = parts(l)[1]
                with sp.Fori(1, NT // 2) as it:
                    for k in range(2):
                        sp.wait_ge(xs[l]["kvw"], (2 * it + k - 1) * nit)
                        load_ctx(l, k, 2 * it + k)

            def expert_traffic(l):
                q = ms[l]

                def weights(m, k):
                    e = sp.value_load(tile_expert[0:1, bass.ds(m, 1)], min_val=0, max_val=E_ - 1)
                    sp.dma_start(ew[k][:, 0:EW[l]], io[f"ew{l}"][:, bass.ds(e * EW[l], EW[l])]).then_inc(q[f"w{k}"], 16)
                    if l == 0:
                        sp.dma_start(eb1[k], io["b1"][:, bass.ds(e * (H0 // P), H0 // P)]).then_inc(q[f"w{k}"], 16)

                def tokens(m, k):
                    sp.dma_start(exs[k], xslot[l][bass.ds(m * P, P), :]).then_inc(q[f"xs{k}"], 16)

                def store(m, k):
                    sp.wait_ge(q["dnc"], m + 1)
                    sp.dma_start(yslot[l][bass.ds(m * P, P), :], eys[k % 2]).then_inc(q[f"ys{k % 2}"], 16)

                sp.wait_ge(routed, ROUTED[l]["tiles"])
                weights(0, 0)
                weights(1, 1)
                sp.wait_ge(scattered, 16 * TOPK * NT * (l + 1))
                for k in range(EB):
                    tokens(k, k)
                for k in range(2, EB):
                    weights(k, k)

                def turn_over(m, k, more):
                    if more:
                        sp.wait_ge(q["xst"], m + 1)
                        tokens(m + EB, k)
                        sp.wait_ge(q["dnw"], m + 1)
                        weights(m + EB, k)
                    store(m, k)

                with sp.Fori(0, ROUNDS - 2) as it:
                    for k in range(EB):
                        turn_over(EB * it + k, k, True)
                for m in range((ROUNDS - 2) * EB, NTILE):
                    turn_over(m, m % EB, m + EB < NTILE)

            cross_loads(0)
            sp.dma_start(rw0[:, :, :], io["rw0"].rearrange("(c p) n -> p c n", p=P)).then_inc(weights_in, 16)
            sp.dma_start(b2sb[:, :], io["b2"]).then_inc(weights_in, 16)
            sp.dma_start(rw1[:, :, :], io["rw1"].rearrange("(c p) n -> p c n", p=P)).then_inc(weights_in, 16)
            sp.wait_ge(blank, 1)
            for l in range(2):
                sp.dma_start(xslot[l].rearrange("(t p) d -> p t d", p=P),
                             zero[:, :].unsqueeze(1).to_broadcast([P, NTILE, D])).then_inc(zeroed, 16)
            expert_traffic(0)
            sp.wait_ge(ms[0]["dnw"], NTILE)
            cross_loads(1)
            expert_traffic(1)
            sp.wait_ge(x_ready, 6)
            sp.dma_start(out.rearrange("(t p) d -> p t d", p=P), x[:, :, :]).then_inc(out_stored, 16)
            sp.wait_ge(out_stored, 16)

        def after(eng, sem, value):
            if not isinstance(value, int) or value > 0:
                eng.wait_ge(sem, value)

        def before(n, k, u, back):
            u -= back
            if u < 0:
                n, k, u = n - 1, k ^ 1, u + 8
            return None if isinstance(n, int) and n < 0 else (n, k, u)

        def quads(eng, body):
            for k in range(2):
                body(k, k, True)
            with eng.Fori(1, NT // 2 - 1) as it:
                for k in range(2):
                    body(2 * it + k, k, True)
            for k in range(2):
                body(NT - 2 + k, k, k == 0)

        def tiles(eng, body):
            for k in range(EB):
                body(k, k, 0, 2)
            with eng.Fori(1, ROUNDS - 1) as it:
                for k in range(EB):
                    body(EB * it + k, k, it, 2)
            for k in range(LAST):
                body(NTILE - LAST + k, k, ROUNDS - 1, min(2, LAST - 1 - k))

        @block.tensor
        def _(pe):
            mm = nc.tensor.matmul

            def turn_xn(s):
                if s == 0:
                    pe.wait_ge(const_loaded, 32)
                for b in range(4):
                    pe.wait_ge(ln_norm, 8 * s + 2 * b + 2)
                    for t in range(2):
                        for c in range(KC):
                            ins = nc.tensor.transpose(bank[b][:, (2 * t + c) * P:(2 * t + c + 1) * P],
                                                      xn[:, 2 * b + t, c * P:c * P + P], ident)
                    ins.then_inc(ln_turned, 1)

            def cross(l, early=False):
                q = xs[l]
                steps, nit, place = parts(l)

                def item(n, k, idx, kind, i, pair):
                    bk = item_bank(n, idx)
                    first = isinstance(n, int) and n == 0
                    after(pe, q["kvc"], idx - 1 if first else n * nit + idx)
                    if idx == 0:
                        pe.wait_ge(q[f"ctx{k}"], 16 * (pair + 1))
                    r = min(P, QS - P * i) if kind != "K" else P
                    if kind == "T":
                        pe.wait_ge(q["krope"], VT * n + i + 1)
                        for c in range(KC):
                            ins = nc.tensor.transpose(bk[:, c * P:c * P + P], krope[:, i % 3, c * P:c * P + P], ident)
                    else:
                        for c in range(KC):
                            if kind == "K":
                                j, m = divmod(i, 2)
                                o, a, b = bk[:, 0:S], wkv[l][:, c, m * P:m * P + P], ctxb[k][:, c, j * S:j * S + S]
                            elif kind == "V":
                                o, a, b = bk[0:r, 0:D], ctxb[k][:, c, P * i:P * i + r], wkv[l][:, c, D:2 * D]
                            else:
                                o, a, b = bk[0:r, :], ctxb[k][:, c, P * i:P * i + r], wkv[l][:, c, :]
                            ins = mm(o, a, b, start=(c == 0), stop=(c == KC - 1))
                    ins.then_inc(q["kvw"], 1)

                def scores(n, k, u):
                    j, c = divmod(u, 2)
                    if u == 0:
                        pe.wait_ge(q["kvc"], n * nit + (8 if l == 0 else nit))
                    if u < 2:
                        pe.wait_ge(q["qbd"], 2 * n + u + 1)
                    after(pe, q["masked" if l == 0 else "probs"], 8 * n + u - 1)
                    for g in range(2):
                        ins = mm(bank[2 * (u % 2) + g][:, 0:S], xqbd[k][:, c, j, 4 * g:4 * g + 4, :],
                                 ktb[k][:, c, j * S:j * S + S], start=True, stop=True)
                    ins.then_inc(q["scores"], 1)

                def turns(n, k, u):
                    j, c = divmod(u, 2)
                    pe.wait_ge(q["probs"], 8 * n + u + 1)
                    after(pe, q["pta"], 8 * n + u)
                    after(pe, q["ptd"], 8 * n + u)
                    for g in range(2):
                        for w in range(3):
                            ins = nc.tensor.transpose(bank[4 + g][:, w * P:w * P + P],
                                                      pwin[j][c][:, g, w * P:w * P + P], ident)
                    ins.then_inc(q["ptw"], 1)

                def collapse(n, k, u):
                    pe.wait_ge(q["normed"], 8 * n + u + 1)
                    mm(bank[6][:, 256:256 + T], omb[u % 2], stack, start=True, stop=True).then_inc(q["colw"], 1)

                def weigh(n, k, u):
                    j, c = divmod(u, 2)
                    if u == 0:
                        pe.wait_ge(q["kvc"], (n + 1) * nit)
                    pe.wait_ge(q["pta"], 8 * n + u + 1)
                    pe.wait_ge(q["ptd"], 8 * n + u + 1)
                    after(pe, q["colc"], 8 * n + u)
                    for g in range(2):
                        for w in range(3):
                            r = P if w < 2 else j + 1
                            ins = mm(bank[6][:, 64 * g:64 * g + 64], pTb[u % 2][0:r, g, w * P:w * P + P],
                                     vb[k][0:r, 2 * j + w, 64 * (2 * c + g):64 * (2 * c + g) + 64],
                                     start=(w == 0), stop=(w == 2))
                    ins.then_inc(q["pvw"], 1)

                pe.wait_ge(wx_loaded[l], 48)
                if early:
                    for item_ in first_items(l, True):
                        item(0, 0, *item_, 0)
                    return
                if l == 0:
                    for i in range(4):
                        m, h = divmod(i, 2)
                        pe.wait_ge(ln_copied, 4 * 0 + 2 * h + 2)
                        after(pe, q["qc"], i - 1)
                        for c in range(KC):
                            ins = mm(bank[4 + i % 2][:, :], wq[0][:, c, m * P:m * P + P], xnT[:, c, h * 512:h * 512 + 512],
                                     start=(c == 0), stop=(c == KC - 1))
                        ins.then_inc(q["qw"], 1)
                else:
                    pe.wait_ge(q["kvc"], len(first_items(l, True)))
                    for t in range(NT):
                        pe.wait_ge(ln_copied, 4 * 3 + t // 2 + 1)
                        after(pe, q["qc"], t - 2)
                        for c in range(KC):
                            ins = mm(bank[4 + t % 3][:, 0:D], xnT[:, c, t * P:t * P + P], wq[1][:, c, :],
                                     start=(c == 0), stop=(c == KC - 1))
                        ins.then_inc(q["qw"], 1)
                if l == 1:
                    pe.wait_ge(q["qc"], NT)
                for item_ in first_items(l, False):
                    item(0, 0, *item_, 0)
                if l == 1:
                    pe.wait_ge(q["qrope"], 1)
                    for b in range(4):
                        for t in range(2):
                            for c in range(KC):
                                ins = nc.tensor.transpose(bank[b][:, (2 * t + c) * P:(2 * t + c + 1) * P],
                                                          xn[:, 2 * b + t, c * P:c * P + P], ident)
                        ins.then_inc(q["qtw"], 1)
                scores(0, 0, 0)

                def body(n, k, more):
                    for u in range(8):
                        if u < 7:
                            scores(n, k, u + 1)
                        elif more:
                            scores(n + 1, k ^ 1, 0)
                        a, b, c = slot_plan(steps[u] if more else [])
                        pair = (n - k) // 2 if isinstance(n, int) else body.it
                        nxt = [(n + 1, k ^ 1), pair + k]
                        for item_ in a:
                            item(*nxt[0], *item_, nxt[1])
                        turns(n, k, u)
                        past = before(n, k, u, 2)
                        if past:
                            collapse(*past)
                        for item_ in b:
                            item(*nxt[0], *item_, nxt[1])
                        past = before(n, k, u, 1)
                        if past:
                            weigh(*past)
                        for item_ in c:
                            item(*nxt[0], *item_, nxt[1])

                for k in range(2):
                    body(k, k, True)
                with pe.Fori(1, NT // 2 - 1) as it:
                    body.it = it
                    for k in range(2):
                        body(2 * it + k, k, True)
                for k in range(2):
                    body(NT - 2 + k, k, k == 0)
                collapse(NT - 1, 1, 6)
                weigh(NT - 1, 1, 7)
                collapse(NT - 1, 1, 7)
                pe.wait_ge(q["colc"], 8 * NT)
                for t in range(NT):
                    for c in range(KC):
                        ins = mm(bank[t][:, 0:D], outT[:, c, t * P:t * P + P], wo[l][:, c, :],
                                 start=(c == 0), stop=(c == KC - 1))
                    ins.then_inc(q["postw"], 1)

            def selfattn(l):
                q = selfs[l]
                w = NKEY if l == 0 else T
                src = kcT if l == 0 else None
                if l == 0:
                    pe.wait_ge(wa_loaded, 48)
                    for i in range(12):
                        m, h = divmod(i, 2)
                        pe.wait_ge(ln_copied, 4 + 2 * h + 2)
                        after(pe, q["prc"], i - 1)
                        for c in range(KC):
                            ins = mm(bank[4 + i % 2][:, :], wqkv[:, c, m * P:m * P + P], xnT[:, c, h * 512:h * 512 + 512],
                                     start=(c == 0), stop=(c == KC - 1))
                        ins.then_inc(q["prw"], 1)
                    pe.wait_ge(q["bdw"], 1)
                    pe.wait_ge(q["prc"], 12)
                    for i in range(4):
                        kind, c = divmod(i, 2)
                        zsrc = (kT, vT)[kind]
                        for f in range(CF):
                            ins = mm(bank[6 + i % 2][:, (i // 2) * 256:(i // 2) * 256 + 256], bdw[:, c * CF + f, :],
                                     zsrc[:, c, f:TOK:CF], start=(f == 0), stop=(f == CF - 1))
                        ins.then_inc(q["cvw"], 1)
                        if i == 1:
                            pe.wait_ge(q["cvc"], 2)
                    pe.wait_ge(q["cvc"], 4)
                    pe.wait_ge(q["null"], 4)
                    for b in range(4):
                        for t in range(2):
                            for c in range(KC):
                                ins = nc.tensor.transpose(bank[b][:, (2 * t + c) * P:(2 * t + c + 1) * P],
                                                          vcT[:, c, 4 * (2 * b + t):4 * (2 * b + t) + 4, :], ident)
                        ins.then_inc(q["vtw"], 1)
                    pe.wait_ge(q["vtc"], 4)
                else:
                    pe.wait_ge(ln_copied, 4 * 5)

                def scores(n, k):
                    pe.wait_ge(q["qbd"], n + 1)
                    pe.wait_ge(q["qbd1"], n + 1)
                    after(pe, q["sub"], n - 1)
                    for j in range(QB):
                        for g in range(GH):
                            if l == 0:
                                keys = kcT.rearrange("p c b w -> p c (b w)")[:, g // 2, bass.ds(n * P + KW * j, w)]
                            else:
                                keys = xnT[:, g // 2, bass.ds(n * P + T * j, w)]
                            at = (4 * j + g) * KW
                            ins = mm(bank[k][:, at:at + w], sqbd[k][:, g // 2, j, 4 * (g % 2):4 * (g % 2) + 4, :], keys,
                                     start=True, stop=True)
                    ins.then_inc(q["sw"], 1)

                def rest(n, k):
                    pe.wait_ge(q["pn"], n + 1)
                    if l == 1:
                        after(pe, q["colc"], n - 1)
                    for g in range(GH):
                        ins = nc.tensor.transpose(bank[2 + k][:, g * P:g * P + P], pn[k][:, g, :, :], ident)
                    ins.then_inc(q["ptw"], 1)
                    if l == 1 and not (isinstance(n, int) and n == 0):
                        turn_back(n - 1, k ^ 1)
                    pe.wait_ge(q["ptc"], n + 1)
                    pe.wait_ge(q["vq"], n + 1)
                    after(pe, q["own_heads"], n)
                    for j in range(QB):
                        for c in range(KC):
                            ins = mm(bank[4 + j][:, c * 8 * T:(c + 1) * 8 * T], vq[k][:, j, c * P:c * P + P],
                                     spT[k][:, 2 * c:2 * c + 2, :], start=True, stop=True)
                    ins.then_inc(q["pvw"], 1)

                def turn_back(n, k):
                    pe.wait_ge(q["own_heads"], n + 1)
                    for c in range(KC):
                        ins = nc.tensor.transpose(bank[2 + k][:, c * P:c * P + P], som[k][:, c, :], ident)
                    ins.then_inc(q["colw"], 1)

                def body(n, k, more):
                    if more:
                        scores(n + 1, k ^ 1)
                    rest(n, k)

                scores(0, 0)
                quads(pe, body)
                if l == 1:
                    turn_back(NT - 1, 1)
                if l == 0:
                    pe.wait_ge(q["own_heads"], NT)
                    for i in range(4):
                        m, h = divmod(i, 2)
                        for c in range(KC):
                            attended = outT.rearrange("p c n -> p (c n)").rearrange("p (b c q) -> p c b q", c=KC, q=T)
                            ins = mm(bank[i][:, :], wout[:, c, m * P:m * P + P], attended[:, c, 16 * h:16 * h + 16, :],
                                     start=(c == 0), stop=(c == KC - 1))
                        ins.then_inc(q["zw"], 1)
                    pe.wait_ge(q["zc"], 4)

                    def along_channels(t):
                        after(pe, q["ac"], t - 1)
                        for c in range(KC):
                            ins = mm(bank[4 + t % 2][:, :], zT[:, c, t * P:t * P + P],
                                     const[:, C_CS + c * 2 * D:C_CS + (c + 1) * 2 * D], start=(c == 0), stop=(c == KC - 1))
                        ins.then_inc(q["aw"], 1)

                    def along_tokens(t):
                        pe.wait_ge(q["ac"], t + 1)
                        after(pe, q["yc"], t - 1)
                        for c in range(2):
                            ins = mm(bank[6 + t % 2][:, 0:D], const[:, C_BD + c * P:C_BD + c * P + P],
                                     af[t % 2][:, c * D:c * D + D], start=(c == 0), stop=(c == 1))
                        ins.then_inc(q["yw"], 1)

                    along_channels(0)
                    for t in range(NT):
                        if t + 1 < NT:
                            along_channels(t + 1)
                        along_tokens(t)

            def experts(l, s):
                q = ms[l]
                nh = HC[l]
                rw = (rw0, rw1)[l]
                pe.wait_ge(ln_copied, 4 * (s + 1))
                pe.wait_ge(weights_in, 48)
                for t in range(NT):
                    for c in range(KC):
                        ins = mm(bank[7][:, t * E_:t * E_ + E_], xnT[:, c, t * P:t * P + P], rw[:, c, :],
                                 start=(c == 0), stop=(c == KC - 1))
                ins.then_inc(ranked, 1)
                pe.wait_ge(routed, ROUTED[l]["hot"])
                mm(bank[6][:, 0:NT * E_], const[:, C_TRI:C_TRI + P], chosen[:, :], start=True, stop=True)
                mm(bank[6][:, P:P + NT * E_], const[:, C_ONES:C_ONES + P], chosen[:, :], start=True, stop=True)\
                    .then_inc(ranked, 1)
                if l == 0:
                    pe.wait_ge(routed, ROUTED[l]["gate"])
                    for t in range(NT):
                        ins = nc.tensor.transpose(bank[4 + t // 4][0:E_, (t % 4) * P:(t % 4) * P + P], gate[:, t, :], ident)
                    ins.then_inc(ranked, 1)
                    pe.wait_ge(q["cwtc"], 2)
                    for t in range(NT):
                        after(pe, q["cwbc"], t - 1)
                        mm(bank[4 + t % 2][:, 0:D], gateT[:, t * P:t * P + P], b2sb[:, :], start=True, stop=True)\
                            .then_inc(q["cwb"], 1)
                    pe.wait_ge(q["cwbc"], NT)

                def turn(m, k, it):
                    pe.wait_ge(q[f"xs{k}"], 16 * (it + 1))
                    after(pe, q["xsc"], m)
                    for c in range(KC):
                        ins = nc.tensor.transpose(bank[0][:, c * P:c * P + P], exs[k][:, c * P:c * P + P], ident)
                    ins.then_inc(q["xst"], 1)

                def hidden(m, k, it):
                    pe.wait_ge(q["xsc"], m + 1)
                    pe.wait_ge(q[f"w{k}"], (32 if l == 0 else 16) * (it + 1))
                    for half in range(2):
                        if l == 0:
                            after(pe, q["upc"], 2 * m + half - 1)
                        else:
                            after(pe, q["silu" if half == 0 else "upc"], m)
                        for i in range(4):
                            for c in range(KC):
                                at = c * H0 + (4 * half + i) * P if l == 0 else half * KC * H1 + c * H1 + i * P
                                ins = mm(bank[1 + half][:, i * P:i * P + P], ew[k][:, at:at + P], exT[k % 2][:, c, :],
                                         start=(c == 0), stop=(c == KC - 1))
                        ins.then_inc(q["upw"], 1)

                def lower(m, k):
                    pe.wait_ge(q["upc"], (2 if l == 0 else 1) * (m + 1))
                    after(pe, q["dnc"], m - 1)
                    for i in range(nh):
                        at = EW[l] - nh * D + i * D
                        ins = mm(bank[4 + k % 2][:, 0:D], eh[k % 2][:, i, :], ew[k][:, at:at + D], start=(i == 0), stop=(i == nh - 1))
                    ins.then_inc(q["dnw"], 1)

                def ahead(by, m, k, it):
                    return m + by, (k + by) % EB, it + (k + by) // EB

                def body(m, k, it, more=2):
                    if more > 0:
                        hidden(*ahead(1, m, k, it))
                    if more > 1:
                        turn(*ahead(2, m, k, it))
                    lower(m, k)

                turn(0, 0, 0)
                hidden(0, 0, 0)
                turn(1, 1, 0)
                tiles(pe, body)

            turn_xn(0)
            cross(0)
            turn_xn(1)
            selfattn(0)
            turn_xn(2)
            experts(0, 2)
            cross(1, early=True)
            turn_xn(3)
            cross(1)
            turn_xn(4)
            selfattn(1)
            turn_xn(5)
            experts(1, 5)

        @block.scalar
        def _(act):
            copy = ACT.Copy
            A = nc.scalar.activation

            def ln_root(s):
                act.wait_ge(ln_var, s + 1)
                A(ln_sd[:, :], ln_ve[:, :], ACT.Sqrt).then_inc(ln_std, 1)

            def ln_copy(s):
                for b in range(4):
                    act.wait_ge(ln_turned, 4 * s + b + 1)
                    A(xnT[:, :, 256 * b:256 * b + 256].rearrange("p c (t q) -> p t c q", t=2),
                      bank[b][:, :].rearrange("p (t c q) -> p t c q", t=2, c=KC), copy).then_inc(ln_copied, 1)

            def cross(l, early=False):
                q = xs[l]
                steps, nit, place = parts(l)

                def item(n, k, idx, kind, i):
                    bk = item_bank(n, idx)
                    act.wait_ge(q["kvw"], n * nit + idx + 1)
                    r = min(P, QS - P * i)
                    if kind == "K":
                        j, m = divmod(i, 2)
                        ins = A(ktb[k][:, m, j * S:j * S + S], bk[:, 0:S], ACT.Identity, bias=vec[:, V_BK + m:V_BK + m + 1])
                    elif kind == "V":
                        ins = A(vb[k][0:r, i, :], bk[0:r, 0:D], copy)
                    elif kind == "A":
                        after(act, q["ss"], VT * n + i - 2)
                        after(act, q["kw"], VT * n + (i - KRAW + 1 if i else 0))
                        A(ksq[0:r, i % 3, :], bk[0:r, 0:D], ACT.Square).then_inc(q["sq"], 1)
                        A(kraw[0:r, i % KRAW, :], bk[0:r, 0:D], copy)
                        ins = A(vb[k][0:r, i, :], bk[0:r, D:2 * D], copy)
                    else:
                        ins = A(ktb[k][:, :, P * i:P * i + r],
                                bk[:, 0:2 * P].rearrange("p (c r) -> p c r", c=KC)[:, :, 0:r], copy)
                    ins.then_inc(q["kvc"], 1)

                def exps(n, k, u):
                    j, c = divmod(u, 2)
                    act.wait_ge(q["negmax"], 8 * n + u + 1)
                    after(act, q["recip"], 8 * n + u - 1)
                    for g in range(2):
                        src = smask[u % 2][:, g, :] if l == 0 else bank[2 * (u % 2) + g][:, 0:S]
                        ins = A(pwin[j][c][:, g, j:j + S], src, ACT.Exp, bias=negmax[u % 2][:, g:g + 1],
                                accum_out=rowsum[u % 2][:, g:g + 1])
                    ins.then_inc(q["probs"], 1)

                def turned(n, k, u):
                    act.wait_ge(q["ptw"], 8 * n + u + 1)
                    A(pTb[u % 2][:, 0, :], bank[4][:, 0:WIN], copy).then_inc(q["pta"], 1)

                if early:
                    for item_ in first_items(l, True):
                        item(0, 0, *item_)
                    return
                if l == 0:
                    for i in range(4):
                        m, h = divmod(i, 2)
                        act.wait_ge(q["qw"], i + 1)
                        A(qT[:, m, h * 512:h * 512 + 512], bank[4 + i % 2][:, :], ACT.Identity,
                          bias=vec[:, V_BQ + m:V_BQ + m + 1]).then_inc(q["qc"], 1)
                else:
                    qsq = outT.rearrange("p c n -> p (c n)").rearrange("p (t d) -> p t d", t=NT)
                    for t in range(NT):
                        act.wait_ge(q["qw"], t + 1)
                        A(qsq[:, t, :], bank[4 + t % 3][:, 0:D], ACT.Square)
                        A(xn[:, t, :], bank[4 + t % 3][:, 0:D], copy).then_inc(q["qc"], 1)
                for item_ in first_items(l, False):
                    item(0, 0, *item_)
                if l == 1:
                    for b in range(4):
                        act.wait_ge(q["qtw"], b + 1)
                        A(qT[:, :, 256 * b:256 * b + 256].rearrange("p c (t q) -> p t c q", t=2),
                          bank[b][:, :].rearrange("p (t c q) -> p t c q", t=2, c=KC), copy).then_inc(q["qtc"], 1)
                exps(0, 0, 0)

                def body(n, k, more):
                    for u in range(8):
                        a, b, c = slot_plan(steps[u] if more else [])
                        for item_ in a:
                            item(n + 1, k ^ 1, *item_)
                        if u < 7:
                            exps(n, k, u + 1)
                        elif more:
                            exps(n + 1, k ^ 1, 0)
                        turned(n, k, u)
                        for item_ in b + c:
                            item(n + 1, k ^ 1, *item_)

                quads(act, body)

            def selfattn(l):
                q = selfs[l]
                w = NKEY if l == 0 else T
                if l == 0:
                    for i in range(12):
                        m, h = divmod(i, 2)
                        act.wait_ge(q["prw"], i + 1)
                        dst = (qT, kT, vT)[m // 2][:, m % 2, h * 512:h * 512 + 512]
                        A(dst, bank[4 + i % 2][:, :], copy).then_inc(q["prc"], 1)
                    act.wait_ge(blanked, l + 1)
                    for i in range(4):
                        kind, c = divmod(i, 2)
                        act.wait_ge(q["cvw"], i + 1)
                        A((kcT, vcT)[kind][:, c, :, 1:NKEY],
                          bank[6 + i % 2][:, (i // 2) * 256:(i // 2) * 256 + 256].rearrange("p (b k) -> p b k", b=B),
                          ACT.Identity, bias=vec[:, V_CB + c:V_CB + c + 1]).then_inc(q["cvc"], 1)
                    for b in range(4):
                        act.wait_ge(q["vtw"], b + 1)
                        A(vall[:, 2 * b:2 * b + 2, :], bank[b][:, :].rearrange("p (t d) -> p t d", t=2), copy)\
                            .then_inc(q["vtc"], 1)

                src, vsrc, col = ((qT, vall, C_HM16), (xnT, xn, C_HM4))[l]

                def spread(n, k):
                    after(act, q["sw"], n - 1)
                    for h in range(8):
                        ins = A(sqbd[k][:, 1, :, h, :], src[:, 1, bass.ds(n * P, P)].rearrange("p (j q) -> p j q", j=QB),
                                copy, scale=const[:, col + h:col + h + 1])
                    ins.then_inc(q["qbd1"], 1)

                def values(n, k):
                    after(act, q["pvw"], n - 1)
                    v = vsrc.rearrange("p t d -> p (t d)")[:, bass.ds(n * D, D)]
                    for j in range(QB):
                        ins = A(vq[k][T * j:T * j + T, j, :], v[T * j:T * j + T, :], copy)
                    ins.then_inc(q["vq"], 1)

                def exps(n, k):
                    act.wait_ge(q["sub"], n + 1)
                    A(sprob[k][:, :, 0:w], sprob[k][:, :, 0:w], ACT.Exp).then_inc(q["exp"], 1)

                def body(n, k, more):
                    act.wait_ge(q["ptw"], n + 1)
                    A(spT[k].rearrange("p g q -> p (g q)"), bank[2 + k][:, :], copy).then_inc(q["ptc"], 1)
                    if more:
                        exps(n + 1, k ^ 1)
                    if not (isinstance(n, int) and n + 2 >= NT):
                        spread(n + 2, k)
                    act.wait_ge(q["pvw"], n + 1)
                    if l == 1:
                        after(act, q["colw"], n - 1)
                    for dst, weighted, mask in head_picks(l, n, k, 0):
                        ins = A(dst, weighted, copy, scale=mask)
                    ins.then_inc(q["even"], 1)
                    if not (isinstance(n, int) and n + 2 >= NT):
                        values(n + 2, k)

                if l == 0:
                    act.wait_ge(q["vtc"], 4)
                else:
                    act.wait_ge(ln_copied, 4 * 5)
                    act.wait_ge(blanked, l + 1)
                for k in range(2):
                    spread(k, k)
                    values(k, k)
                exps(0, 0)
                quads(act, body)
                if l == 0:
                    for i in range(4):
                        m, h = divmod(i, 2)
                        act.wait_ge(q["zw"], i + 1)
                        A(zT[:, m, h * 512:h * 512 + 512], bank[i][:, :], ACT.Identity,
                          bias=vec[:, V_BO + m:V_BO + m + 1]).then_inc(q["zc"], 1)
                    for t in range(NT):
                        act.wait_ge(q["aw"], t + 1)
                        after(act, q["yw"], t - 1)
                        A(af[t % 2], bank[4 + t % 2][:, :], copy).then_inc(q["ac"], 1)

            def experts(l):
                q = ms[l]
                if l == 0:
                    act.wait_ge(routed, ROUTED[l]["less_max"])
                    A(lg[:, :, :], lg[:, :, :], ACT.Exp).then_inc(gate_exp, 1)
                else:
                    act.wait_ge(routed, ROUTED[l]["less_max"])
                    A(gsm[:, 1, :], gsm[:, 0, :], ACT.Exp).then_inc(gate_exp, 1)

                def body(m, k, it, more=True):
                    if l == 0:
                        act.wait_ge(q[f"w{k}"], 32 * (it + 1))
                        for half in range(2):
                            act.wait_ge(q["upw"], 2 * m + half + 1)
                            for i in range(4):
                                c = 4 * half + i
                                ins = A(eh[k % 2][:, c, :], bank[1 + half][:, i * P:i * P + P], ACT.Gelu_apprx_tanh,
                                        bias=eb1[k][:, c:c + 1])
                            ins.then_inc(q["upc"], 1)
                    else:
                        after(act, q["upc"], m - 1)
                        act.wait_ge(q["upw"], 2 * m + 1)
                        A(esilu[k % 2], bank[1][:, :], ACT.Silu).then_inc(q["silu"], 1)

                tiles(act, body)
                if l == 0:
                    cross(1, early=True)

            for s in range(6):
                ln_root(s)
                ln_copy(s)
                (lambda: cross(0), lambda: selfattn(0), lambda: experts(0),
                 lambda: cross(1), lambda: selfattn(1), lambda: experts(1))[s]()

        @block.vector
        def _(dve):
            V = nc.vector
            own = Tally(ln_own)

            def mine(ins):
                dve.wait_ge(ln_own, own.inc(ins))

            def stats(t):
                return V.bn_stats(ln_stats[:, t, :], x[:, t, :])

            def ln(s):
                if s == 0:
                    dve.wait_ge(x_loaded, 16)
                else:
                    dve.wait_ge(x_ready, s)
                for t in range(NT) if s == 0 else (NT - 1,):
                    ins = stats(t)
                mine(ins)
                for t in range(NT):
                    ins = V.bn_aggr(ln_mv[:, t, :], ln_stats[:, t, :])
                mine(ins)
                V.tensor_scalar(ln_ve[:, :], ln_mv[:, :, 1], 1e-5, None, ALU.add).then_inc(ln_var, 1)
                dve.wait_ge(ln_std, s + 1)
                mine(V.reciprocal(ln_rs[:, :], ln_sd[:, :]))
                for t in range(NT):
                    V.tensor_scalar(xn[:, t, :], x[:, t, :], ln_mv[:, t, 0:1], ln_rs[:, t:t + 1],
                                    ALU.subtract, ALU.mult).then_inc(ln_norm, 1)

            def finish(ins, q, t):
                ins.then_inc(x_ready if t == NT - 1 else q, 1)

            def cross(l, early=False):
                q = xs[l]
                steps, nit, place = parts(l)

                def sums(n, idx, kind, i):
                    if kind == "A":
                        r = min(P, QS - P * i)
                        dve.wait_ge(q["sq"], VT * n + i + 1)
                        after(dve, q["root"], ROOT_STEPS * (VT // BATCH) * n)
                        V.tensor_reduce(kss[0:r, i, :], ksq[0:r, i % 3, :].rearrange("p (h d) -> p h d", d=HD),
                                        AX_X, ALU.add).then_inc(q["ss"], 1)

                def norms(n, idx, kind, i):
                    if kind == "A":
                        if i % BATCH == BATCH - 1:
                            dve.wait_ge(q["ss"], VT * n + i + 1)
                            first = i + 1 - BATCH
                            step = iter(range(1, ROOT_STEPS + 1))
                            base = ROOT_STEPS * ((VT // BATCH) * n + i // BATCH)

                            def rooted(ins):
                                ins.then_inc(q["root"], 1)
                                dve.wait_ge(q["root"], base + next(step))

                            flat = lambda v: v[:, first:i + 1, :].rearrange("p t h -> p (t h)")
                            inv_root(flat(kr), flat(kss), BATCH * NH, rooted)
                        if i >= BATCH - 1:
                            weigh_keys(n, i + 1 - BATCH)
                    elif kind == "T" and i in (VT - 6, VT - 5):
                        weigh_keys(n, i + 4)

                def weigh_keys(n, i):
                    r = min(P, QS - P * i)
                    t = VT * n + i
                    h3 = lambda v: v.rearrange("p (h d) -> p h d", d=HD)
                    after(dve, q["krope"], t - 2)
                    dve.wait_ge(q["kvc"], nit * n + place["A", i] + 1)
                    V.tensor_tensor(h3(kn[0:r, i % 3, :]), h3(kraw[0:r, i % KRAW, :]),
                                    kr[0:r, i, :].unsqueeze(2).to_broadcast([r, NH, HD]), ALU.mult).then_inc(q["kw"], 1)

                def maxima(n, u):
                    p = u % 2
                    after(dve, q["negmax"], 8 * n + u)
                    dve.wait_ge(q["scores"], 8 * n + u + 1)
                    if l == 0:
                        V.memset(spare[:, :], 0.0)
                        for g in range(2):
                            ins = V.tensor_tensor_reduce(smask[p][:, g, :], bank[2 * p + g][:, 0:S], negmask[:, :],
                                                         1.0, float(np.finfo(np.float32).min), ALU.add, ALU.max,
                                                         rowmax[:, g:g + 1])
                        ins.then_inc(q["masked"], 1)
                        dve.wait_ge(q["masked"], 8 * n + u + 1)
                        V.tensor_scalar(negmax[p], rowmax[:, :], -1.0, None, ALU.mult).then_inc(q["negmax"], 1)
                    else:
                        for g in range(2):
                            ins = V.tensor_reduce(negmax[p][:, g:g + 1], bank[2 * p + g][:, 0:S], AX_X, ALU.max, negate=True)
                        ins.then_inc(q["negmax"], 1)

                def invert(n, u):
                    after(dve, q["normed"], 8 * n + u - 1)
                    dve.wait_ge(q["probs"], 8 * n + u + 1)
                    V.reciprocal(rcp[u % 2], rowsum[u % 2]).then_inc(q["recip"], 1)

                def turned(n, u):
                    dve.wait_ge(q["ptw"], 8 * n + u + 1)
                    V.tensor_copy(pTb[u % 2][:, 1, :], bank[5][:, 0:WIN]).then_inc(q["ptd"], 1)

                def norm(n, u):
                    dve.wait_ge(q["pvw"], 8 * n + u + 1)
                    dve.wait_ge(q["recip"], 8 * n + u + 1)
                    for g in range(2):
                        ins = V.scalar_tensor_tensor(omb[u % 2][:, 64 * g:64 * g + 64], bank[6][:, 64 * g:64 * g + 64],
                                                     rcp[u % 2][:, g:g + 1], blk, ALU.mult, ALU.mult)
                    ins.then_inc(q["normed"], 1)

                def collapsed(n, u):
                    j, c = divmod(u, 2)
                    dve.wait_ge(q["colw"], 8 * n + u + 1)
                    dst = outT[:, c, bass.ds(n * P + T * j, T)]
                    if l == 0:
                        ins = V.tensor_scalar(dst, bank[6][:, 256:256 + T], vec[:, V_BV + c:V_BV + c + 1], None, ALU.add)
                    else:
                        ins = V.tensor_copy(dst, bank[6][:, 256:256 + T])
                    ins.then_inc(q["colc"], 1)

                def inv_root(dst, src, w, step):
                    v, t = root_v[:, 0:w], root_t[:, 0:w]
                    yi = root_y[:, 0:w]
                    y = yi.bitcast(F32)
                    step(V.tensor_scalar(v, src, 1e-6 * HD, None, ALU.add))
                    step(V.tensor_scalar(yi, v.bitcast(I32), 1, None, ALU.logical_shift_right))
                    step(V.tensor_scalar(yi, yi, -1.0, float(0x5f3759df - 2 ** 31), ALU.mult, ALU.add))
                    for i in range(3):
                        step(V.scalar_tensor_tensor(t, v, 0.5, y, ALU.mult, ALU.mult))
                        step(V.tensor_tensor(t, t, y, ALU.mult))
                        step(V.scalar_tensor_tensor(dst if i == 2 else y, t, 1.5, y, ALU.subtract, ALU.mult))

                if early:
                    mine(V.memset(kss[:, :, :], 1.0))
                    for item_ in first_items(l, True):
                        sums(0, *item_)
                        norms(0, *item_)
                    return
                if l == 0:
                    dve.wait_ge(mask_loaded, 16 * (QB + 1))
                    mine(V.tensor_scalar(negmask[:, :], negmask[:, :], -1e9, None, ALU.mult))
                    for t in range(NT):
                        ins = V.tensor_tensor(x[:, t, :], x[:, t, :], bo_bc[:, :], ALU.add)
                    mine(ins)
                else:
                    q1 = outT.rearrange("p c n -> p (c n)")
                    q2 = qT.rearrange("p c n -> p (c n)")
                    q0 = xn.rearrange("p t d -> p (t d)")
                    h3 = lambda v: v.rearrange("p (a d) -> p a d", d=HD)
                    bc = lambda v, n: v.unsqueeze(1).to_broadcast([P, NT * NH, n])
                    dve.wait_ge(q["qc"], NT)
                    mine(V.tensor_reduce(qss[:, :], h3(q1), AX_X, ALU.add))
                    inv_root(qr[:, :], qss[:, :], NT * NH, mine)
                    mine(V.tensor_tensor(h3(q0), h3(q0), qr[:, :].unsqueeze(2).to_broadcast([P, NT * NH, HD]), ALU.mult))
                    dve.wait_ge(q["rw"], 1)
                    V.tensor_tensor(h3(q1), h3(q0), bc(rope_q[:, 0:HD], HD), ALU.mult)
                    V.tensor_tensor(h3(q2)[:, :, 0:8], h3(q0)[:, :, 8:16], bc(rope_q[:, HD:HD + 8], 8), ALU.mult)
                    mine(V.tensor_tensor(h3(q2)[:, :, 8:16], h3(q0)[:, :, 0:8], bc(rope_q[:, HD + 8:2 * HD], 8), ALU.mult))
                    V.tensor_tensor(q0, q1, q2, ALU.add).then_inc(q["qrope"], 1)
                    for item_ in first_items(l, False):
                        sums(0, *item_)
                        norms(0, *item_)
                maxima(0, 0)

                def body(n, k, more):
                    for u in range(8):
                        a, b, c = slot_plan(steps[u] if more else [])
                        if u < 7:
                            maxima(n, u + 1)
                        elif more:
                            maxima(n + 1, 0)
                        invert(n, u)
                        turned(n, u)
                        for item_ in a:
                            sums(n + 1, *item_)
                        past = before(n, k, u, 2)
                        if past:
                            collapsed(past[0], past[2])
                        for item_ in b:
                            sums(n + 1, *item_)
                        past = before(n, k, u, 1)
                        if past:
                            norm(past[0], past[2])
                        for item_ in c:
                            sums(n + 1, *item_)
                        for item_ in a + b + c:
                            norms(n + 1, *item_)

                quads(dve, body)
                collapsed(NT - 1, 6)
                norm(NT - 1, 7)
                collapsed(NT - 1, 7)
                for t in range(NT):
                    dve.wait_ge(q["postw"], t + 1)
                    finish(V.tensor_tensor(x[:, t, :], x[:, t, :], bank[t][:, 0:D], ALU.add), q["xadd"], t)
                    if t:
                        dve.wait_ge(q["xadd"], t)
                        stats(t - 1)

            def selfattn(l):
                q = selfs[l]
                w = NKEY if l == 0 else T

                def scores(n, k):
                    after(dve, q["sub"], n)
                    after(dve, q["pn"], n)
                    dve.wait_ge(q["sw"], n + 1)
                    s3 = sprob[k][:, :, 0:w]
                    raw = bank[k][:, :].rearrange("p (a w) -> p a w", w=KW)[:, :, 0:w]
                    mcol = const[:, (C_M0, C_M1)[l]:(C_M0, C_M1)[l] + w]
                    V.tensor_tensor(s3, raw, mcol.unsqueeze(1).to_broadcast([P, NH, w]), ALU.add).then_inc(q["own"], 1)
                    dve.wait_ge(q["own"], 2 * n + 1)
                    V.tensor_reduce(smx[:, :], s3, AX_X, ALU.max).then_inc(q["own"], 1)
                    dve.wait_ge(q["own"], 2 * n + 2)
                    V.tensor_tensor(s3, s3, smx[:, :].unsqueeze(2).to_broadcast([P, NH, w]), ALU.subtract)\
                        .then_inc(q["sub"], 1)

                def norm(n, k):
                    dve.wait_ge(q["exp"], n + 1)
                    s3 = sprob[k][:, :, 0:w]
                    V.tensor_reduce(ssum[:, :], s3, AX_X, ALU.add).then_inc(q["sum"], 1)
                    dve.wait_ge(q["sum"], 2 * n + 1)
                    V.reciprocal(srcp[:, :], ssum[:, :]).then_inc(q["sum"], 1)
                    dve.wait_ge(q["sum"], 2 * n + 2)
                    V.tensor_tensor(pn[k].rearrange("p g j w -> p j g w")[:, :, :, 0:w],
                                    s3.rearrange("p (j g) w -> p j g w", j=QB),
                                    srcp[:, :].rearrange("p (j g) -> p j g", j=QB).unsqueeze(3).to_broadcast([P, QB, GH, w]),
                                    ALU.mult).then_inc(q["pn"], 1)

                def odd_heads(n, k):
                    dve.wait_ge(q["even"], n + 1)
                    for dst, weighted, mask in head_picks(l, n, k, 1):
                        ins = V.scalar_tensor_tensor(dst, weighted, mask, dst, ALU.mult, ALU.add)
                    ins.then_inc(q["own_heads"], 1)

                def added(n, k):
                    dve.wait_ge(q["colw"], n + 1)
                    xv = x.rearrange("p t d -> p (t d)")[:, bass.ds(n * D, D)]
                    V.tensor_tensor(xv, xv, bank[2 + k][:, 0:D], ALU.add).then_inc(q["colc"], 1)

                def body(n, k, more):
                    if more:
                        scores(n + 1, k ^ 1)
                    if l == 1 and not (isinstance(n, int) and n == 0):
                        added(n - 1, k ^ 1)
                    if more:
                        norm(n + 1, k ^ 1)
                    odd_heads(n, k)
                    if l == 1 and not (isinstance(n, int) and n == 0):
                        dve.wait_ge(q["colc"], n)
                        V.bn_stats(ln_stats.rearrange("p t s -> p (t s)")[:, bass.ds((n - 1) * 6, 6)],
                                   x.rearrange("p t d -> p (t d)")[:, bass.ds((n - 1) * D, D)])

                if l == 0:
                    for i in range(4):
                        kind, c = divmod(i, 2)
                        if i == 0:
                            dve.wait_ge(blanked, l + 1)
                        V.tensor_copy((kcT, vcT)[kind][:, c, :, 0:1],
                                      vec[:, (V_NK, V_NV)[kind] + c:(V_NK, V_NV)[kind] + c + 1].unsqueeze(1)
                                      .to_broadcast([P, B, 1])).then_inc(q["null"], 1)
                scores(0, 0)
                norm(0, 0)
                quads(dve, body)
                if l == 0:
                    for t in range(NT):
                        dve.wait_ge(q["yw"], t + 1)
                        finish(V.tensor_tensor(x[:, t, :], x[:, t, :], bank[6 + t % 2][:, 0:D], ALU.add), q["yc"], t)
                        if t:
                            dve.wait_ge(q["yc"], t)
                            stats(t - 1)
                else:
                    added(NT - 1, 1)
                    dve.wait_ge(q["colc"], NT)
                    V.memset(spare[:, :], 0.0).then_inc(x_ready, 1)

            def experts(l, s):
                q = ms[l]
                nh = HC[l]
                if l == 0:
                    for v in seen + used:
                        ins = V.memset(v[:, 0:8] if v in used else v[:, 0:NT, :], 0.0)
                    mine(ins)
                dve.wait_ge(ranked, RANKED[l]["logits"])
                raw = bank[7][:, 0:NT * E_].rearrange("p (t e) -> p t e", e=E_)
                mine(V.tensor_copy(pr[:, :, :], raw))
                b3 = lambda v: v.unsqueeze(2).to_broadcast([P, NT, E_])
                if l == 0:
                    mine(V.tensor_reduce(gsm[:, 0, :], pr[:, :, :], AX_X, ALU.max))
                    V.tensor_tensor(lg[:, :, :], pr[:, :, :], b3(gsm[:, 0, :]), ALU.subtract).then_inc(routed, 1)
                    dve.wait_ge(gate_exp, l + 1)
                    mine(V.tensor_reduce(gsm[:, 0, :], lg[:, :, :], AX_X, ALU.add))
                    mine(V.reciprocal(gsm[:, 1, :], gsm[:, 0, :]))
                    mine(V.tensor_tensor(pr[:, :, :], lg[:, :, :], b3(gsm[:, 1, :]), ALU.mult))
                for t in range(NT):
                    ins = V.max(top[:, t, :], pr[:, t, :])
                mine(ins)
                for t in range(NT):
                    ins = V.max_index(topi[:, t, :], top[:, t, :], pr[:, t, :])
                mine(ins)
                mine(V.tensor_copy(topf[:, :, 0:2], topi[:, :, 0:2]))
                if l == 0:
                    mine(V.tensor_tensor(gsm[:, 0, :], top[:, :, 0], top[:, :, 1], ALU.add))
                    mine(V.tensor_scalar(gsm[:, 0, :], gsm[:, 0, :], 1e-8, None, ALU.add))
                    mine(V.reciprocal(gsm[:, 1, :], gsm[:, 0, :]))
                    V.tensor_tensor(gsm[:, 2, :], top[:, :, 0], gsm[:, 1, :], ALU.mult)
                    mine(V.tensor_tensor(gsm[:, 3, :], top[:, :, 1], gsm[:, 1, :], ALU.mult))
                else:
                    V.tensor_tensor(gsm[:, 0, :], top[:, :, 1], top[:, :, 0], ALU.subtract).then_inc(routed, 1)
                    dve.wait_ge(gate_exp, l + 1)
                    mine(V.tensor_scalar(gsm[:, 0, :], gsm[:, 1, :], 1.0, None, ALU.add))
                    mine(V.reciprocal(gsm[:, 2, :], gsm[:, 0, :]))
                    mine(V.tensor_tensor(gsm[:, 3, :], gsm[:, 1, :], gsm[:, 2, :], ALU.mult))
                iota = const[:, C_IOTA:C_IOTA + E_].unsqueeze(1).to_broadcast([P, NT, E_])
                for i in range(TOPK):
                    ins = V.tensor_tensor(onehot[i][:, :, :], iota, b3(topf[:, :, i]), ALU.is_equal)
                mine(ins)
                flat = lambda v: v.rearrange("p t e -> p (t e)")
                V.tensor_tensor(chosen[:, :], flat(onehot[0]), flat(onehot[1]), ALU.add).then_inc(routed, 1)
                if l == 0:
                    V.tensor_tensor(gate[:, :, :], onehot[0][:, :, :], b3(gsm[:, 2, :]), ALU.mult)
                    mine(V.tensor_tensor(lg[:, :, :], onehot[1][:, :, :], b3(gsm[:, 3, :]), ALU.mult))
                    V.tensor_tensor(gate[:, :, :], gate[:, :, :], lg[:, :, :], ALU.add).then_inc(routed, 1)

                dve.wait_ge(ranked, RANKED[l]["ranks"])
                mine(V.tensor_copy(seen[0][:, NT:, :], bank[6][:, P:P + NT * E_].rearrange("p (t e) -> p t e", e=E_)))
                for i in range(3):
                    mine(V.tensor_tensor(seen[i + 1][:, NT:, :], seen[i][:, NT:, :],
                                         seen[i][:, NT - 2 ** i:2 * NT - 2 ** i, :], ALU.add))
                total = seen[3][:, 2 * NT - 1, :]
                mine(V.tensor_tensor(more_than[:, :, :], total.unsqueeze(2).to_broadcast([P, E_, NT]),
                                     const[:, C_THR:C_THR + NT].unsqueeze(1).to_broadcast([P, E_, NT]), ALU.is_gt))
                mine(V.tensor_reduce(used[0][:, E_:], more_than[:, :, :], AX_X, ALU.add))
                for i in range(3):
                    mine(V.tensor_tensor(used[i + 1][:, E_:], used[i][:, E_:], used[i][:, E_ - 2 ** i:2 * E_ - 2 ** i], ALU.add))
                mine(V.tensor_tensor(slot_base[:, :, :], bank[6][:, 0:NT * E_].rearrange("p (t e) -> p t e", e=E_),
                                     seen[3][:, NT - 1:2 * NT - 1, :], ALU.add))
                mine(V.scalar_tensor_tensor(slot_base[:, :, :], used[3][:, E_ - 1:2 * E_ - 1].unsqueeze(1)
                                            .to_broadcast([P, NT, E_]), float(P), slot_base[:, :, :], ALU.mult, ALU.add))
                for i in range(TOPK):
                    mine(V.tensor_tensor(picked[:, :, :], onehot[i][:, :, :], slot_base[:, :, :], ALU.mult))
                    mine(V.tensor_reduce(slotf[:, i, :], picked[:, :, :], AX_X, ALU.add))
                V.tensor_copy(slot[:, :, :], slotf[:, :, :]).then_inc(routed, 1)
                mine(V.tensor_tensor(ends[:, :, :], const[:, C_TILE:C_TILE + NTILE].unsqueeze(2).to_broadcast([P, NTILE, E_]),
                                     used[3][:, E_:].unsqueeze(1).to_broadcast([P, NTILE, E_]), ALU.is_ge))
                mine(V.tensor_reduce(tilef[:, :], ends[:, :, :], AX_X, ALU.add))
                V.tensor_scalar(tile_expert[:, :], tilef[:, :], float(E_ - 1), None, ALU.min).then_inc(routed, 1)
                if l == 0:
                    dve.wait_ge(ranked, RANKED[l]["gates"])
                    for b in range(2):
                        V.tensor_copy(gateT[:, 512 * b:512 * b + 512], bank[4 + b][0:E_, :]).then_inc(q["cwtc"], 1)
                    for t in range(NT):
                        dve.wait_ge(q["cwb"], t + 1)
                        V.tensor_tensor(x[:, t, :], x[:, t, :], bank[4 + t % 2][:, 0:D], ALU.add).then_inc(q["cwbc"], 1)

                def turned(m, k):
                    dve.wait_ge(q["xst"], m + 1)
                    V.tensor_copy(exT[k % 2].rearrange("p c q -> p (c q)"), bank[0][:, 0:D]).then_inc(q["xsc"], 1)

                def prod(m, k):
                    if l == 1:
                        dve.wait_ge(q["silu"], m + 1)
                        dve.wait_ge(q["upw"], 2 * m + 2)
                        V.tensor_tensor(eh[k % 2][:, 0:nh, :].rearrange("p c q -> p (c q)"), bank[2][:, :], esilu[k % 2],
                                        ALU.mult).then_inc(q["upc"], 1)

                def outputs(m, k, it):
                    after(dve, q[f"ys{k % 2}"], 16 * (EB // 2 * it + k // 2))
                    dve.wait_ge(q["dnw"], m + 1)
                    V.tensor_copy(eys[k % 2], bank[4 + k % 2][:, 0:D]).then_inc(q["dnc"], 1)

                def body(m, k, it, more=2):
                    if more > 0:
                        prod(m + 1, (k + 1) % EB)
                    if more > 1:
                        turned(m + 2, (k + 2) % EB)
                    outputs(m, k, it)

                turned(0, 0)
                prod(0, 0)
                turned(1, 1)
                tiles(dve, body)
                if l == 0:
                    cross(1, early=True)
                for t in range(NT):
                    dve.wait_ge(gathered[t // (NT // 2)], 16 * TOPK * (NT // 2) * (l + 1))
                    for i in range(TOPK):
                        if t == 0 and i == 0 and l == 0:
                            dve.wait_ge(q["cwbc"], NT)
                        ins = V.scalar_tensor_tensor(x[:, t, :], eyg[t][i], gsm[:, 2 + i, t:t + 1], x[:, t, :],
                                                     ALU.mult, ALU.add)
                        if t < NT - 1 or i == 0:
                            mine(ins)
                    if t < NT - 1 and l == 0:
                        stats(t)
                if t == NT - 1:
                    ins.then_inc(x_ready, 1)

            V.memset(zero[:, :], 0.0).then_inc(blank, 1)
            for s in range(6):
                ln(s)
                (lambda: cross(0), lambda: selfattn(0), lambda: experts(0, 2),
                 lambda: cross(1), lambda: selfattn(1), lambda: experts(1, 5))[s]()

        @block.gpsimd
        def _(pool):
            G = nc.gpsimd
            own = Tally(pool_own)

            def spread(dst, src, n, c, col, q):
                G.tensor_tensor(dst[:, c, :, :, :],
                                src[:, c, bass.ds(n * P, P)].rearrange("p (j q) -> p j q", j=QB).unsqueeze(2)
                                .to_broadcast([P, QB, 8, T]),
                                const[:, col:col + 8].unsqueeze(1).unsqueeze(3).to_broadcast([P, QB, 8, T]),
                                ALU.mult).then_inc(q["qbd"], 1)

            def cross(l, s):
                q = xs[l]
                steps, nit, place = parts(l)
                if s:
                    pool.wait_ge(x_ready, s)
                for j in range(QB):
                    for c in range(KC):
                        own.inc(G.memset(pwin[j][c], 0.0))
                if l == 1:
                    pool.wait_ge(normw_loaded, 16)
                    pool.wait_ge(const_loaded, 32)
                    for base, m_, dst in ((C_RQ, 1, 0), (C_RK, VT, 32)):
                        which = 0 if base == C_RQ else 1
                        tab = const[:, base:base + 32 * m_].rearrange("p (m k) -> p m k", k=32)
                        o = ropew[:, dst:dst + 32 * m_].rearrange("p (m k) -> p m k", k=32)
                        for a, b, wa in ((0, 16, 0), (16, 24, 8), (24, 32, 0)):
                            wv = normw[:, which, wa:wa + b - a].unsqueeze(1).to_broadcast([P, m_, b - a])
                            ins = G.tensor_tensor(o[:, :, a:b], tab[:, :, a:b], wv, ALU.mult)
                            own.inc(ins)
                    pool.wait_ge(pool_own, own.n)
                    G.memset(mark[:, :], 0.0).then_inc(q["rw"], 1)
                pool.wait_ge(pool_own, own.n)

                def rotate(n, i):
                    r = min(P, QS - P * i)
                    t = VT * n + i
                    rt = rope_k(i)
                    h3 = lambda v: v.rearrange("p (h d) -> p h d", d=HD)
                    bc = lambda v: v[0:r, :].unsqueeze(1).to_broadcast([r, NH, v.shape[-1]])
                    after(pool, q["krope"], t)
                    pool.wait_ge(q["kw"], t + 1)
                    kn3, kb3 = h3(kn[0:r, i % 3, :]), h3(kb[0:r, :])
                    G.tensor_tensor(kb3[:, :, 0:8], kn3[:, :, 8:16], bc(rt[:, HD:HD + 8]), ALU.mult).then_inc(q["kn"], 1)
                    G.tensor_tensor(kb3[:, :, 8:16], kn3[:, :, 0:8], bc(rt[:, HD + 8:2 * HD]), ALU.mult).then_inc(q["kn"], 1)
                    G.tensor_tensor(h3(ka[0:r, :]), kn3, bc(rt[:, 0:HD]), ALU.mult).then_inc(q["kn"], 1)
                    pool.wait_ge(q["kn"], 3 * t + 3)
                    if i >= 3:
                        pool.wait_ge(q["kvw"], nit * n + place["T", i - 3] + 1)
                    elif not (isinstance(n, int) and n == 0):
                        pool.wait_ge(q["kvw"], nit * (n - 1) + place["T", i + VT - 3] + 1)
                    G.tensor_tensor(krope[0:r, i % 3, :], ka[0:r, :], kb[0:r, :], ALU.add).then_inc(q["krope"], 1)

                def rotated_keys(n):
                    for i in range(VT):
                        rotate(n, i)

                if l == 1:
                    rotated_keys(0)
                pool.wait_ge(q["qc"] if l == 0 else q["qtc"], 4)
                pool.wait_ge(const_loaded, 32)
                for c in range(KC):
                    spread(xqbd[0], qT, 0, c, C_HM4, q)

                def body(n, k, more):
                    if more:
                        after(pool, q["scores"], 8 * n)
                        spread(xqbd[k ^ 1], qT, n + 1, 0, C_HM4, q)
                        if l == 1:
                            rotated_keys(n + 1)
                        spread(xqbd[k ^ 1], qT, n + 1, 1, C_HM4, q)

                quads(pool, body)

            def selfattn(l, s):
                q = selfs[l]
                src, col = ((qT, C_HM16), (xnT, C_HM4))[l]
                pool.wait_ge(x_ready, s)
                for v in vq:
                    own.inc(G.memset(v.rearrange("p j d -> p (j d)"), 0.0))
                if l == 0:
                    for v in (vcT.rearrange("p c b w -> p (c b w)"), kcT.rearrange("p c b w -> p (c b w)")):
                        own.inc(G.memset(v, 0.0))
                    for v in pn:
                        own.inc(G.memset(v.rearrange("p g j w -> p (g j w)"), 0.0))
                pool.wait_ge(pool_own, own.n)
                G.memset(mark[:, :], 0.0).then_inc(blanked, 1)
                if l == 0:
                    pool.wait_ge(wa_loaded, 48)
                    G.tensor_tensor(bdw.rearrange("p a (h o) -> p a h o", o=HD),
                                    cw[:, :, :].unsqueeze(2).to_broadcast([P, KC * CF, 8, HD]),
                                    const[:, C_HM1:C_HM1 + 8].unsqueeze(1).unsqueeze(3).to_broadcast([P, KC * CF, 8, HD]),
                                    ALU.mult).then_inc(q["bdw"], 1)
                    pool.wait_ge(q["prc"], 4)
                else:
                    pool.wait_ge(ln_copied, 4 * 5)

                def body(n, k):
                    after(pool, q["sw"], n - 1)
                    spread(sqbd[k], src, n, 0, col, q)

                for k in range(2):
                    body(k, k)
                with pool.Fori(1, NT // 2) as it:
                    for k in range(2):
                        body(2 * it + k, k)

            def experts(l, s):
                q = ms[l]
                pool.wait_ge(zeroed, 32)
                pool.wait_ge(routed, ROUTED[l]["slots"])
                pool.wait_ge(ln_norm, NT * (s + 1))
                at = lambda i, t: bass.IndirectOffsetOnAxis(ap=slot[:, i, t:t + 1], axis=0)
                for t in range(NT):
                    for i in range(TOPK):
                        G.indirect_dma_start(out=xslot[l], out_offset=at(i, t), in_=xn[:, t, :], in_offset=None)\
                            .then_inc(scattered, 16)
                for k in range(2):
                    pool.wait_ge(q[f"ys{k}"], 16 * ((NTILE + 1 - k) // 2))
                for t in range(NT):
                    for i in range(TOPK):
                        G.indirect_dma_start(out=eyg[t][i], out_offset=None, in_=yslot[l], in_offset=at(i, t))\
                            .then_inc(gathered[t // (NT // 2)], 16)

            cross(0, 0)
            selfattn(0, 1)
            experts(0, 2)
            cross(1, 3)
            selfattn(1, 4)
            experts(1, 5)


def kernel(**inputs):
    import concourse.bacc as _bacc
    from concourse.bass_utils import run_bass_kernel_spmd as _run

    a = {k: np.asarray(v) for k, v in inputs.items()}
    cols = lambda v: v.reshape(-1, KC, P).transpose(2, 0, 1).reshape(P, -1)
    rows = lambda v: np.broadcast_to(v.reshape(1, -1), (P, v.size))
    chunks = lambda w: w.reshape(E_, -1, P, w.shape[2]).transpose(2, 0, 1, 3).reshape(P, E_, -1)
    expert_rows = lambda *w: np.concatenate([chunks(m) for m in w], 2).reshape(P, -1)
    kv = lambda k, v: np.concatenate([k, v], 1)
    arrays = {
        "x": a["x"].reshape(TOK, D),
        "ctxT": a["ctx_1024"].reshape(B * S, D).T,
        "mask": a["mask_1x1xSxS2_fk1"].reshape(T, S),
        "const": shape_constants(),
        "vec": np.concatenate([cols(a[n]) for n in ("L0_xattn_bq", "L0_xattn_bk", "L0_xattn_bv", "L0_attn_conv_b",
                                                    "L0_attn_b_out", "L0_attn_null_k", "L0_attn_null_v")], 1),
        "bo": rows(a["L0_xattn_bo"]),
        "w0q": a["L0_xattn_Wq"], "w0kv": kv(a["L0_xattn_Wk"], a["L0_xattn_Wv"]), "w0o": a["L0_xattn_Wo"],
        "w1q": a["L1_xattn_Wq"].T, "w1kv": kv(a["L1_xattn_Wk"].T, a["L1_xattn_Wv"].T), "w1o": a["L1_xattn_Wo"].T,
        "wqkv": a["L0_attn_Wqkv"], "wout": a["L0_attn_W_out"],
        "conv": a["L0_attn_conv_w"].reshape(KC, 8, HD, HD, CF).transpose(1, 3, 0, 4, 2).reshape(P, KC * CF, HD),
        "normw": np.stack([rows(a["L1_xattn_q_norm_w"]), rows(a["L1_xattn_k_norm_w"])], 1),
        "rw0": a["L0_ffn_router_w"].T, "rw1": a["L1_ffn_w_gate"],
        "b1": a["L0_ffn_b1"].reshape(E_, H0 // P, P).transpose(2, 0, 1).reshape(P, -1), "b2": a["L0_ffn_b2"],
        "ew0": expert_rows(a["L0_ffn_w1"].transpose(0, 2, 1), a["L0_ffn_w2"].transpose(0, 2, 1)),
        "ew1": expert_rows(a["L1_ffn_w1"], a["L1_ffn_w3"], a["L1_ffn_w2"]),
    }
    nc = _bacc.Bacc("TRN2", target_bir_lowering=False, num_devices=1)
    named, io = {}, {}
    for name, v in arrays.items():
        v = np.ascontiguousarray(v)
        named[f"in_{name}_dram"] = v
        io[name] = nc.dram_tensor(f"in_{name}_dram", v.shape, mybir.dt.from_np(v.dtype), kind="ExternalInput").ap()
    out = nc.dram_tensor("out_0_dram", (TOK, D), F32, kind="ExternalOutput").ap()
    perceiver_block(nc, io, out)
    r = _run(nc, [named], core_ids=[0])
    return r.results[0]["out_0_dram"].reshape(B, T, D)
```
